# Optimizing a Trainium2 kernel written in Bass

```python
import numpy as np
import jax
import jax.numpy as jnp

def _softmax(x, axis=-1):
    return jax.nn.softmax(x, axis=axis)

def _gelu(x):
    return jax.nn.gelu(x, approximate=True)

def _silu(x):
    return jax.nn.silu(x)

def _sigmoid(x):
    return jax.nn.sigmoid(x)

def _layernorm(x, axis=-1, eps=1e-05):
    m = jnp.mean(x, axis=axis, keepdims=True)
    v = jnp.var(x, axis=axis, keepdims=True)
    return (x - m) / jnp.sqrt(v + eps)

def _scatter_add(tgt, idx, src, axis=0):
    return tgt.at[idx].add(src)

def _segment_sum(src, seg, n):
    return jax.ops.segment_sum(src, seg, n)
kernel_name = 'mk_decoder_preln_d4_seqx_r8_8ab293'

def setup_inputs(seed: int=0):
    np.random.seed(seed)
    _w = jnp.asarray

    def _rec_inputs():
        import jax
        import jax.numpy as jnp
        _rk = jax.random.key(seed)
        x = 7.22e-05 + 1 * jax.random.normal(jax.random.fold_in(_rk, 1), (2, 512, 128), jnp.float32)
        _lenS = 512 - jax.random.randint(jax.random.fold_in(_rk, 7), (2,), 0, max(1, 512 // 4) + 1, jnp.int32)
        _lenS2 = 32 - jax.random.randint(jax.random.fold_in(_rk, 8), (2,), 0, max(1, 32 // 4) + 1, jnp.int32)
        _ctx_768P = jax.random.normal(jax.random.fold_in(_rk, 11), (2, 16, 96), jnp.float32)
        _ctx_768c = jax.random.dirichlet(jax.random.fold_in(_rk, 511), 0.3 * jnp.ones((16,), jnp.float32), (2, 32))
        _ctx_768t = jnp.einsum('bsk,bkd->bsd', _ctx_768c, _ctx_768P)
        _ctx_768t = _ctx_768t * jax.lax.rsqrt(jnp.mean(jnp.square(_ctx_768t)) + 1e-12) * 0.953939
        ctx_768 = -0.000191848 + 0.999787 * (_ctx_768t + 0.3 * jax.random.normal(jax.random.fold_in(_rk, 611), (2, 32, 96), jnp.float32))
        return (x, ctx_768)
    x, ctx_768 = _rec_inputs()

    def _L0_attn_setup():
        import jax, jax.numpy as jnp
        import numpy as np
        N_HEADS = 16
        EPS = 1e-06
        key = jax.random.key(seed)
        ks = jax.random.split(key, 5)
        B, N, D, H = (4, 256, 128, N_HEADS)
        x = jax.random.normal(ks[0], (B, N, D), dtype=jnp.float32)
        Wq = jax.random.normal(ks[1], (D, D), dtype=jnp.float32) * D ** (-0.5)
        Wk = jax.random.normal(ks[2], (D, D), dtype=jnp.float32) * D ** (-0.5)
        Wv = jax.random.normal(ks[3], (D, D), dtype=jnp.float32) * D ** (-0.5)
        Wo = jax.random.normal(ks[4], (D, D), dtype=jnp.float32) * D ** (-0.5)
        q_scale = jnp.ones((H,), dtype=jnp.float32)
        k_scale = jnp.ones((H,), dtype=jnp.float32)
        return {'x': x, 'Wq': Wq, 'Wk': Wk, 'Wv': Wv, 'Wo': Wo, 'q_scale': q_scale, 'k_scale': k_scale}
    _L0_attn_all = _L0_attn_setup()
    _L0_attn_in = {k: v for k, v in _L0_attn_all.items() if k in ('Wq', 'Wk', 'Wv', 'Wo', 'q_scale', 'k_scale')}
    del _L0_attn_all

    def _L0_xattn_setup():
        import jax, jax.numpy as jnp
        import numpy as np
        NUM_HEADS = 16
        CLAMP = 10000.0
        key = jax.random.key(seed)
        ks = jax.random.split(key, 8)
        B, Nq, Nkv, Cq, Ckv = (4, 256, 256, 128, 96)
        s_q = 1.0 / np.sqrt(Cq)
        s_kv = 1.0 / np.sqrt(Ckv)
        return {'query': jax.random.normal(ks[0], (B, Nq, Cq), jnp.float32), 'key_value': jax.random.normal(ks[1], (B, Nkv, Ckv), jnp.float32), 'Wq': jax.random.normal(ks[2], (Cq, Cq), jnp.float32) * s_q, 'bq': jnp.zeros((Cq,), jnp.float32), 'Wk': jax.random.normal(ks[3], (Ckv, Cq), jnp.float32) * s_kv, 'bk': jnp.zeros((Cq,), jnp.float32), 'Wv': jax.random.normal(ks[4], (Ckv, Cq), jnp.float32) * s_kv, 'bv': jnp.zeros((Cq,), jnp.float32), 'Wo': jax.random.normal(ks[5], (Cq, Cq), jnp.float32) * s_q, 'bo': jnp.zeros((Cq,), jnp.float32)}
    _L0_xattn_all = _L0_xattn_setup()
    _L0_xattn_in = {k: v for k, v in _L0_xattn_all.items() if k in ('Wq', 'bq', 'Wk', 'bk', 'Wv', 'bv', 'Wo', 'bo')}
    del _L0_xattn_all

    def _L0_ffn_setup():
        import jax, jax.numpy as jnp
        import numpy as np
        H = 128
        I = 512
        E = 4
        LN_EPS = 1e-12

        def _layer_norm(x, gamma, beta, eps=LN_EPS):
            mu = jnp.mean(x, axis=-1, keepdims=True)
            var = jnp.mean(jnp.square(x - mu), axis=-1, keepdims=True)
            return (x - mu) * jax.lax.rsqrt(var + eps) * gamma + beta
        key = jax.random.key(seed)
        ks = jax.random.split(key, 8)
        B, S = (4, 64)
        scale = 0.02
        return {'hidden_states': jax.random.normal(ks[0], (B, S, H), jnp.float32), 'W_router': jax.random.normal(ks[1], (H, E), jnp.float32) * scale, 'W1': jax.random.normal(ks[2], (E, H, I), jnp.float32) * scale, 'b1': jax.random.normal(ks[3], (E, I), jnp.float32) * scale, 'Wo': jax.random.normal(ks[4], (I, H), jnp.float32) * scale, 'bo': jax.random.normal(ks[5], (H,), jnp.float32) * scale, 'ln_gamma': jnp.ones((H,), jnp.float32), 'ln_beta': jnp.zeros((H,), jnp.float32)}
    _L0_ffn_all = _L0_ffn_setup()
    _L0_ffn_in = {k: v for k, v in _L0_ffn_all.items() if k in ('W_router', 'W1', 'b1', 'Wo', 'bo', 'ln_gamma', 'ln_beta')}
    del _L0_ffn_all

    def _L1_attn_setup():
        import jax, jax.numpy as jnp
        import numpy as np
        D_MODEL = 128
        N_HEAD = 16
        D_HEAD = D_MODEL // N_HEAD
        N_CTX = 256
        ROPE_BASE = 10000.0
        SCALE = 1

        def _rope_cache(seq_len, d_head, dtype=jnp.float32):
            inv_freq = 1.0 / ROPE_BASE ** (jnp.arange(0, d_head, 2, dtype=jnp.float32) / d_head)
            t = jnp.arange(seq_len, dtype=jnp.float32)
            freqs = jnp.outer(t, inv_freq)
            emb = jnp.concatenate([freqs, freqs], -1)
            cos = jnp.cos(emb)[None, :, None, :].astype(dtype)
            sin = jnp.sin(emb)[None, :, None, :].astype(dtype)
            return (cos, sin)

        def _apply_rope(x, cos, sin):
            x_even = x[..., 0::2]
            x_odd = x[..., 1::2]
            x_rot = jnp.stack([-x_odd, x_even], axis=-1).reshape(x.shape)
            return x * cos + x_rot * sin

        def _rmsnorm(x, w):
            eps = jnp.finfo(x.dtype).eps
            var = jnp.mean(jnp.square(x), axis=-1, keepdims=True)
            return x * jax.lax.rsqrt(var + eps) * w
        key = jax.random.key(seed)
        ks = jax.random.split(key, 9)
        B, S = (2, N_CTX)
        x = jax.random.normal(ks[0], (B, S, D_MODEL), jnp.float32)
        s = 0.02
        Wq = jax.random.normal(ks[1], (D_MODEL, D_MODEL), jnp.float32) * s
        bq = jax.random.normal(ks[2], (D_MODEL,), jnp.float32) * s
        Wk = jax.random.normal(ks[3], (D_MODEL, D_MODEL), jnp.float32) * s
        bk = jax.random.normal(ks[4], (D_MODEL,), jnp.float32) * s
        Wv = jax.random.normal(ks[5], (D_MODEL, D_MODEL), jnp.float32) * s
        bv = jax.random.normal(ks[6], (D_MODEL,), jnp.float32) * s
        Wo = jax.random.normal(ks[7], (D_MODEL, D_MODEL), jnp.float32) * s
        norm_w = jnp.ones((D_HEAD,), jnp.float32)
        return {'x': x, 'Wq': Wq, 'bq': bq, 'Wk': Wk, 'bk': bk, 'Wv': Wv, 'bv': bv, 'Wo': Wo, 'norm_w': norm_w}
    _L1_attn_all = _L1_attn_setup()
    _L1_attn_in = {k: v for k, v in _L1_attn_all.items() if k in ('Wq', 'bq', 'Wk', 'bk', 'Wv', 'bv', 'Wo', 'norm_w')}
    del _L1_attn_all

    def _L1_xattn_setup():
        import jax, jax.numpy as jnp
        import numpy as np
        QUERY_DIM = 128
        CONTEXT_DIM = 96
        HEADS = 8
        DIM_HEAD = 64
        INNER = HEADS * DIM_HEAD
        key = jax.random.key(seed)
        ks = jax.random.split(key, 7)
        B, S, L = (8, 512, 77)
        x = jax.random.normal(ks[0], (B, S, QUERY_DIM), dtype=jnp.float32)
        context = jax.random.normal(ks[1], (B, L, CONTEXT_DIM), dtype=jnp.float32)
        Wq = jax.random.normal(ks[2], (QUERY_DIM, INNER), dtype=jnp.float32) * QUERY_DIM ** (-0.5)
        Wk = jax.random.normal(ks[3], (CONTEXT_DIM, INNER), dtype=jnp.float32) * CONTEXT_DIM ** (-0.5)
        Wv = jax.random.normal(ks[4], (CONTEXT_DIM, INNER), dtype=jnp.float32) * CONTEXT_DIM ** (-0.5)
        Wo = jax.random.normal(ks[5], (INNER, QUERY_DIM), dtype=jnp.float32) * INNER ** (-0.5)
        bo = jax.random.normal(ks[6], (QUERY_DIM,), dtype=jnp.float32) * 0.01
        return {'x': x, 'context': context, 'Wq': Wq, 'Wk': Wk, 'Wv': Wv, 'Wo': Wo, 'bo': bo}
    _L1_xattn_all = _L1_xattn_setup()
    _L1_xattn_in = {k: v for k, v in _L1_xattn_all.items() if k in ('Wq', 'Wk', 'Wv', 'Wo', 'bo')}
    del _L1_xattn_all

    def _L1_ffn_setup():
        import jax, jax.numpy as jnp
        import numpy as np
        TOP_K = 2
        key = jax.random.key(seed)
        ks = jax.random.split(key, 5)
        B, T, D, F, E = (2, 256, 128, 512, 8)
        x = jax.random.normal(ks[0], (B, T, D), dtype=jnp.float32)
        router_w = jax.random.normal(ks[1], (D, E + 1), dtype=jnp.float32) * 0.02
        router_b = jax.random.normal(ks[2], (E + 1,), dtype=jnp.float32) * 0.02
        w1 = jax.random.normal(ks[3], (E, D, F), dtype=jnp.float32) * 0.02
        w2 = jax.random.normal(ks[4], (E, F, D), dtype=jnp.float32) * 0.02
        return {'x': x, 'router_w': router_w, 'router_b': router_b, 'w1': w1, 'w2': w2}
    _L1_ffn_all = _L1_ffn_setup()
    _L1_ffn_in = {k: v for k, v in _L1_ffn_all.items() if k in ('router_w', 'router_b', 'w1', 'w2')}
    del _L1_ffn_all

    def _L2_attn_setup():
        import jax, jax.numpy as jnp
        import numpy as np
        B, S, D, H = (4, 256, 128, 16)
        DH = D // H
        key = jax.random.key(seed)
        ks = jax.random.split(key, 5)
        std = 1.0 / np.sqrt(D)
        return {'x': jax.random.normal(ks[0], (B, S, D), dtype=jnp.float32), 'mask': jnp.ones((S, S), dtype=bool), 'Wq': jax.random.normal(ks[1], (D, D), dtype=jnp.float32) * std, 'Wk': jax.random.normal(ks[2], (D, D), dtype=jnp.float32) * std, 'Wv': jax.random.normal(ks[3], (D, D), dtype=jnp.float32) * std, 'Wout': jax.random.normal(ks[4], (D, D), dtype=jnp.float32) * std}
    _L2_attn_all = _L2_attn_setup()
    _L2_attn_in = {k: v for k, v in _L2_attn_all.items() if k in ('mask', 'Wq', 'Wk', 'Wv', 'Wout')}
    del _L2_attn_all

    def _L2_xattn_setup():
        import jax, jax.numpy as jnp
        import numpy as np
        DIM_Q = 128
        DIM_KV = 96
        N_HEADS = 4

        def _split_heads(x):
            b, l, d = x.shape
            return x.reshape(b, l, N_HEADS, d // N_HEADS).transpose(0, 2, 1, 3)
        key = jax.random.key(seed)
        ks = jax.random.split(key, 7)
        b, lq, lkv = (4, 256, 256)
        q = jax.random.normal(ks[0], (b, lq, DIM_Q), dtype=jnp.float32)
        kv = jax.random.normal(ks[1], (b, lkv, DIM_KV), dtype=jnp.float32)
        s_q = 1.0 / np.sqrt(DIM_Q)
        s_kv = 1.0 / np.sqrt(DIM_KV)
        Wq = jax.random.normal(ks[2], (DIM_Q, DIM_Q), dtype=jnp.float32) * s_q
        Wk = jax.random.normal(ks[3], (DIM_Q, DIM_KV), dtype=jnp.float32) * s_kv
        Wv = jax.random.normal(ks[4], (DIM_Q, DIM_KV), dtype=jnp.float32) * s_kv
        Wo = jax.random.normal(ks[5], (DIM_Q, DIM_Q), dtype=jnp.float32) * s_q
        bo = jax.random.normal(ks[6], (DIM_Q,), dtype=jnp.float32) * 0.01
        return {'q': q, 'kv': kv, 'Wq': Wq, 'Wk': Wk, 'Wv': Wv, 'Wo': Wo, 'bo': bo}
    _L2_xattn_all = _L2_xattn_setup()
    _L2_xattn_in = {k: v for k, v in _L2_xattn_all.items() if k in ('Wq', 'Wk', 'Wv', 'Wo', 'bo')}
    del _L2_xattn_all

    def _L2_ffn_setup():
        import jax, jax.numpy as jnp
        import numpy as np
        HIDDEN = 128
        INNER = 512

        def _weight_quant(w):
            scale = 1.0 / jnp.clip(jnp.mean(jnp.abs(w)), 1e-05)
            wq = jnp.clip(jnp.round(w * scale), -1.0, 1.0) / scale
            return w + jax.lax.stop_gradient(wq - w)

        def _act_quant(x):
            scale = 127.0 / jnp.clip(jnp.max(jnp.abs(x), axis=-1, keepdims=True), 1e-05)
            xq = jnp.clip(jnp.round(x * scale), -128.0, 127.0) / scale
            return x + jax.lax.stop_gradient(xq - x)

        def _bitlinear(x, w):
            return jnp.einsum('bsi,oi->bso', _act_quant(x), _weight_quant(w))
        key = jax.random.key(seed)
        k0, k1, k2, k3 = jax.random.split(key, 4)
        x = jax.random.normal(k0, (4, 256, HIDDEN), dtype=jnp.float32)
        w_gate = jax.random.normal(k1, (INNER, HIDDEN), dtype=jnp.float32) / np.sqrt(HIDDEN)
        w_up = jax.random.normal(k2, (INNER, HIDDEN), dtype=jnp.float32) / np.sqrt(HIDDEN)
        w_down = jax.random.normal(k3, (HIDDEN, INNER), dtype=jnp.float32) / np.sqrt(INNER)
        return {'x': x, 'w_gate': w_gate, 'w_up': w_up, 'w_down': w_down}
    _L2_ffn_all = _L2_ffn_setup()
    _L2_ffn_in = {k: v for k, v in _L2_ffn_all.items() if k in ('w_gate', 'w_up', 'w_down')}
    del _L2_ffn_all

    def _L3_attn_setup():
        import jax, jax.numpy as jnp
        import numpy as np
        D_MODEL, N_HEADS, BATCH, SEQ = (128, 16, 2, 256)

        def get_freqs(seq, n_dim):
            inv_freq = 1.0 / 10000.0 ** (jnp.arange(0, n_dim, 2, dtype=jnp.float32) / n_dim)
            pos = jnp.arange(seq, dtype=jnp.float32)
            return pos[:, None] * inv_freq[None, :]

        def rope(x, freq):
            cos = jnp.cos(freq)[None, :, None, :]
            sin = jnp.sin(freq)[None, :, None, :]
            x1, x2 = (x[..., ::2], x[..., 1::2])
            r1 = x1 * cos - x2 * sin
            r2 = x1 * sin + x2 * cos
            return jnp.stack([r1, r2], axis=-1).reshape(x.shape)
        key = jax.random.key(seed)
        ks = jax.random.split(key, 5)
        w_scale = 0.01
        return {'x': jax.random.normal(ks[0], (BATCH, SEQ, D_MODEL), dtype=jnp.float32), 'qw': jax.random.normal(ks[1], (D_MODEL, D_MODEL), dtype=jnp.float32) * w_scale, 'kw': jax.random.normal(ks[2], (D_MODEL, D_MODEL), dtype=jnp.float32) * w_scale, 'vw': jax.random.normal(ks[3], (D_MODEL, D_MODEL), dtype=jnp.float32) * w_scale, 'ow': jax.random.normal(ks[4], (D_MODEL, D_MODEL), dtype=jnp.float32) * w_scale}
    _L3_attn_all = _L3_attn_setup()
    _L3_attn_in = {k: v for k, v in _L3_attn_all.items() if k in ('qw', 'kw', 'vw', 'ow')}
    del _L3_attn_all

    def _L3_xattn_setup():
        import math
        import jax, jax.numpy as jnp
        import numpy as np
        B, SQ, SKV = (4, 256, 256)
        D_EMBED, D_CROSS, D_ATT, N_HEADS = (128, 96, 128, 16)
        D_HEAD = D_ATT // N_HEADS

        def _split_heads(t):
            b, s, _ = t.shape
            return t.reshape(b, s, N_HEADS, D_HEAD).transpose(0, 2, 1, 3)
        key = jax.random.key(seed)
        ks = jax.random.split(key, 10)
        s_e = 1.0 / math.sqrt(D_EMBED)
        s_c = 1.0 / math.sqrt(D_CROSS)
        s_a = 1.0 / math.sqrt(D_ATT)
        return {'x': jax.random.normal(ks[0], (B, SQ, D_EMBED), jnp.float32), 'y': jax.random.normal(ks[1], (B, SKV, D_CROSS), jnp.float32), 'Wq': jax.random.normal(ks[2], (D_EMBED, D_ATT), jnp.float32) * s_e, 'bq': jax.random.normal(ks[3], (D_ATT,), jnp.float32) * 0.01, 'Wk': jax.random.normal(ks[4], (D_CROSS, D_ATT), jnp.float32) * s_c, 'bk': jax.random.normal(ks[5], (D_ATT,), jnp.float32) * 0.01, 'Wv': jax.random.normal(ks[6], (D_CROSS, D_ATT), jnp.float32) * s_c, 'bv': jax.random.normal(ks[7], (D_ATT,), jnp.float32) * 0.01, 'Wo': jax.random.normal(ks[8], (D_ATT, D_EMBED), jnp.float32) * s_a, 'bo': jax.random.normal(ks[9], (D_EMBED,), jnp.float32) * 0.01}
    _L3_xattn_all = _L3_xattn_setup()
    _L3_xattn_in = {k: v for k, v in _L3_xattn_all.items() if k in ('Wq', 'bq', 'Wk', 'bk', 'Wv', 'bv', 'Wo', 'bo')}
    del _L3_xattn_all

    def _L3_ffn_setup():
        import jax, jax.numpy as jnp
        import numpy as np
        TOPK = 2
        EPS = 1e-06
        key = jax.random.key(seed)
        ks = jax.random.split(key, 8)
        b, t, d, h, n = (2, 128, 128, 256, 16)
        x = jax.random.normal(ks[0], (b, t, d), dtype=jnp.float32)
        router_w = jax.random.normal(ks[1], (n, d), dtype=jnp.float32) * (1.0 / np.sqrt(d))
        router_bias = jnp.zeros((n,), dtype=jnp.float32)
        bank_mag = jax.random.normal(ks[2], (n, d, h), dtype=jnp.float32) * (1.0 / np.sqrt(d))
        bank_freq = jax.random.uniform(ks[3], (n, d, h), dtype=jnp.float32, minval=0.5, maxval=2.0) * (1.0 / np.sqrt(d))
        bank_phase = jax.random.uniform(ks[4], (n, h), dtype=jnp.float32, minval=-0.3, maxval=0.3)
        bank_down = jax.random.normal(ks[5], (n, h, d), dtype=jnp.float32) * (1.0 / np.sqrt(h))
        norm_w = jnp.ones((d,), dtype=jnp.float32)
        return {'x': x, 'router_w': router_w, 'router_bias': router_bias, 'bank_mag': bank_mag, 'bank_freq': bank_freq, 'bank_phase': bank_phase, 'bank_down': bank_down, 'norm_w': norm_w}
    _L3_ffn_all = _L3_ffn_setup()
    _L3_ffn_in = {k: v for k, v in _L3_ffn_all.items() if k in ('router_w', 'router_bias', 'bank_mag', 'bank_freq', 'bank_phase', 'bank_down', 'norm_w')}
    del _L3_ffn_all
    return {'x': x, 'ctx_768': ctx_768, 'L0_attn_Wq': _L0_attn_in['Wq'], 'L0_attn_Wk': _L0_attn_in['Wk'], 'L0_attn_Wv': _L0_attn_in['Wv'], 'L0_attn_Wo': _L0_attn_in['Wo'], 'L0_attn_q_scale': _L0_attn_in['q_scale'], 'L0_attn_k_scale': _L0_attn_in['k_scale'], 'L0_xattn_Wq': _L0_xattn_in['Wq'], 'L0_xattn_bq': _L0_xattn_in['bq'], 'L0_xattn_Wk': _L0_xattn_in['Wk'], 'L0_xattn_bk': _L0_xattn_in['bk'], 'L0_xattn_Wv': _L0_xattn_in['Wv'], 'L0_xattn_bv': _L0_xattn_in['bv'], 'L0_xattn_Wo': _L0_xattn_in['Wo'], 'L0_xattn_bo': _L0_xattn_in['bo'], 'L0_ffn_W_router': _L0_ffn_in['W_router'], 'L0_ffn_W1': _L0_ffn_in['W1'], 'L0_ffn_b1': _L0_ffn_in['b1'], 'L0_ffn_Wo': _L0_ffn_in['Wo'], 'L0_ffn_bo': _L0_ffn_in['bo'], 'L0_ffn_ln_gamma': _L0_ffn_in['ln_gamma'], 'L0_ffn_ln_beta': _L0_ffn_in['ln_beta'], 'L1_attn_Wq': _L1_attn_in['Wq'], 'L1_attn_bq': _L1_attn_in['bq'], 'L1_attn_Wk': _L1_attn_in['Wk'], 'L1_attn_bk': _L1_attn_in['bk'], 'L1_attn_Wv': _L1_attn_in['Wv'], 'L1_attn_bv': _L1_attn_in['bv'], 'L1_attn_Wo': _L1_attn_in['Wo'], 'L1_attn_norm_w': _L1_attn_in['norm_w'], 'L1_xattn_Wq': _L1_xattn_in['Wq'], 'L1_xattn_Wk': _L1_xattn_in['Wk'], 'L1_xattn_Wv': _L1_xattn_in['Wv'], 'L1_xattn_Wo': _L1_xattn_in['Wo'], 'L1_xattn_bo': _L1_xattn_in['bo'], 'L1_ffn_router_w': _L1_ffn_in['router_w'], 'L1_ffn_router_b': _L1_ffn_in['router_b'], 'L1_ffn_w1': _L1_ffn_in['w1'], 'L1_ffn_w2': _L1_ffn_in['w2'], 'L2_attn_mask': _L2_attn_in['mask'], 'L2_attn_Wq': _L2_attn_in['Wq'], 'L2_attn_Wk': _L2_attn_in['Wk'], 'L2_attn_Wv': _L2_attn_in['Wv'], 'L2_attn_Wout': _L2_attn_in['Wout'], 'L2_xattn_Wq': _L2_xattn_in['Wq'], 'L2_xattn_Wk': _L2_xattn_in['Wk'], 'L2_xattn_Wv': _L2_xattn_in['Wv'], 'L2_xattn_Wo': _L2_xattn_in['Wo'], 'L2_xattn_bo': _L2_xattn_in['bo'], 'L2_ffn_w_gate': _L2_ffn_in['w_gate'], 'L2_ffn_w_up': _L2_ffn_in['w_up'], 'L2_ffn_w_down': _L2_ffn_in['w_down'], 'L3_attn_qw': _L3_attn_in['qw'], 'L3_attn_kw': _L3_attn_in['kw'], 'L3_attn_vw': _L3_attn_in['vw'], 'L3_attn_ow': _L3_attn_in['ow'], 'L3_xattn_Wq': _L3_xattn_in['Wq'], 'L3_xattn_bq': _L3_xattn_in['bq'], 'L3_xattn_Wk': _L3_xattn_in['Wk'], 'L3_xattn_bk': _L3_xattn_in['bk'], 'L3_xattn_Wv': _L3_xattn_in['Wv'], 'L3_xattn_bv': _L3_xattn_in['bv'], 'L3_xattn_Wo': _L3_xattn_in['Wo'], 'L3_xattn_bo': _L3_xattn_in['bo'], 'L3_ffn_router_w': _L3_ffn_in['router_w'], 'L3_ffn_router_bias': _L3_ffn_in['router_bias'], 'L3_ffn_bank_mag': _L3_ffn_in['bank_mag'], 'L3_ffn_bank_freq': _L3_ffn_in['bank_freq'], 'L3_ffn_bank_phase': _L3_ffn_in['bank_phase'], 'L3_ffn_bank_down': _L3_ffn_in['bank_down'], 'L3_ffn_norm_w': _L3_ffn_in['norm_w']}

def reference(x, ctx_768, L0_attn_Wq, L0_attn_Wk, L0_attn_Wv, L0_attn_Wo, L0_attn_q_scale, L0_attn_k_scale, L0_xattn_Wq, L0_xattn_bq, L0_xattn_Wk, L0_xattn_bk, L0_xattn_Wv, L0_xattn_bv, L0_xattn_Wo, L0_xattn_bo, L0_ffn_W_router, L0_ffn_W1, L0_ffn_b1, L0_ffn_Wo, L0_ffn_bo, L0_ffn_ln_gamma, L0_ffn_ln_beta, L1_attn_Wq, L1_attn_bq, L1_attn_Wk, L1_attn_bk, L1_attn_Wv, L1_attn_bv, L1_attn_Wo, L1_attn_norm_w, L1_xattn_Wq, L1_xattn_Wk, L1_xattn_Wv, L1_xattn_Wo, L1_xattn_bo, L1_ffn_router_w, L1_ffn_router_b, L1_ffn_w1, L1_ffn_w2, L2_attn_mask, L2_attn_Wq, L2_attn_Wk, L2_attn_Wv, L2_attn_Wout, L2_xattn_Wq, L2_xattn_Wk, L2_xattn_Wv, L2_xattn_Wo, L2_xattn_bo, L2_ffn_w_gate, L2_ffn_w_up, L2_ffn_w_down, L3_attn_qw, L3_attn_kw, L3_attn_vw, L3_attn_ow, L3_xattn_Wq, L3_xattn_bq, L3_xattn_Wk, L3_xattn_bk, L3_xattn_Wv, L3_xattn_bv, L3_xattn_Wo, L3_xattn_bo, L3_ffn_router_w, L3_ffn_router_bias, L3_ffn_bank_mag, L3_ffn_bank_freq, L3_ffn_bank_phase, L3_ffn_bank_down, L3_ffn_norm_w):
    import jax
    import jax.numpy as jnp

    def _L0_attn_ref(x, Wq, Wk, Wv, Wo, q_scale, k_scale):
        import jax, jax.numpy as jnp
        import numpy as np
        N_HEADS = 16
        EPS = 1e-06
        B, N, D = x.shape
        H = N_HEADS
        hd = D // H
        q = jax.nn.silu(x @ Wq.T)
        k = jax.nn.silu(x @ Wk.T)
        v = jax.nn.silu(x @ Wv.T)
        q = q.reshape(B, N, H, hd).transpose(0, 2, 1, 3)
        k = k.reshape(B, N, H, hd).transpose(0, 2, 1, 3)
        v = v.reshape(B, N, H, hd).transpose(0, 2, 1, 3)
        r_q = jnp.linalg.norm(q, axis=-1, keepdims=True)
        r_k = jnp.linalg.norm(k, axis=-1, keepdims=True)
        q_dir = q / (r_q + EPS)
        k_dir = k / (r_k + EPS)
        scores = jnp.einsum('bhnd,bhmd->bhnm', q_dir, k_dir)
        sq = q_scale[None, :, None, None]
        sk = k_scale[None, :, None, None]
        scores = scores * (r_q * sq) * (jnp.swapaxes(r_k, -2, -1) * sk)
        mask = jnp.tril(jnp.ones((N, N), dtype=bool))
        scores = jnp.where(mask, scores, -jnp.inf)
        probs = jax.nn.softmax(scores, axis=-1)
        out = jnp.einsum('bhnm,bhmd->bhnd', probs, v)
        out = out.transpose(0, 2, 1, 3).reshape(B, N, D)
        return out @ Wo.T

    def _L0_xattn_ref(query, key_value, Wq, bq, Wk, bk, Wv, bv, Wo, bo):
        import jax, jax.numpy as jnp
        import numpy as np
        NUM_HEADS = 16
        CLAMP = 10000.0
        B, Nq, Cq = query.shape
        Nkv = key_value.shape[1]
        H = NUM_HEADS
        D = Cq // H
        scale = D ** (-0.5)
        q = (query @ Wq + bq).reshape(B, Nq, H, D).transpose(0, 2, 1, 3)
        k = (key_value @ Wk + bk).reshape(B, Nkv, H, D).transpose(0, 2, 1, 3)
        v = (key_value @ Wv + bv).reshape(B, Nkv, H, D).transpose(0, 2, 1, 3)
        attn = jnp.einsum('bhqd,bhkd->bhqk', q, k) * scale
        attn = jnp.clip(attn, -CLAMP, CLAMP)
        attn = jax.nn.softmax(attn, axis=-1)
        attn = jnp.where(jnp.any(jnp.isnan(attn)), jnp.asarray(1.0 / Nkv, attn.dtype), attn)
        x = jnp.einsum('bhqk,bhkd->bqhd', attn, v).reshape(B, Nq, Cq)
        return x @ Wo + bo

    def _L0_ffn_ref(hidden_states, W_router, W1, b1, Wo, bo, ln_gamma, ln_beta):
        import jax, jax.numpy as jnp
        import numpy as np
        H = 128
        I = 512
        E = 4
        LN_EPS = 1e-12

        def _layer_norm(x, gamma, beta, eps=LN_EPS):
            mu = jnp.mean(x, axis=-1, keepdims=True)
            var = jnp.mean(jnp.square(x - mu), axis=-1, keepdims=True)
            return (x - mu) * jax.lax.rsqrt(var + eps) * gamma + beta
        B, S, _ = hidden_states.shape
        x = hidden_states.reshape(-1, H)
        logits = x @ W_router
        expert_idx = jnp.argmax(logits, axis=-1)
        h = jnp.einsum('th,ehi->tei', x, W1) + b1
        h = jax.nn.gelu(h, approximate=False)
        onehot = jax.nn.one_hot(expert_idx, E, dtype=x.dtype)
        intermediate = jnp.einsum('te,tei->ti', onehot, h)
        y = intermediate @ Wo + bo + x
        y = _layer_norm(y, ln_gamma, ln_beta)
        return y.reshape(B, S, H)

    def _L1_attn_ref(x, Wq, bq, Wk, bk, Wv, bv, Wo, norm_w):
        import jax, jax.numpy as jnp
        import numpy as np
        D_MODEL = 128
        N_HEAD = 16
        D_HEAD = D_MODEL // N_HEAD
        N_CTX = 256
        ROPE_BASE = 10000.0
        SCALE = 1

        def _rope_cache(seq_len, d_head, dtype=jnp.float32):
            inv_freq = 1.0 / ROPE_BASE ** (jnp.arange(0, d_head, 2, dtype=jnp.float32) / d_head)
            t = jnp.arange(seq_len, dtype=jnp.float32)
            freqs = jnp.outer(t, inv_freq)
            emb = jnp.concatenate([freqs, freqs], -1)
            cos = jnp.cos(emb)[None, :, None, :].astype(dtype)
            sin = jnp.sin(emb)[None, :, None, :].astype(dtype)
            return (cos, sin)

        def _apply_rope(x, cos, sin):
            x_even = x[..., 0::2]
            x_odd = x[..., 1::2]
            x_rot = jnp.stack([-x_odd, x_even], axis=-1).reshape(x.shape)
            return x * cos + x_rot * sin

        def _rmsnorm(x, w):
            eps = jnp.finfo(x.dtype).eps
            var = jnp.mean(jnp.square(x), axis=-1, keepdims=True)
            return x * jax.lax.rsqrt(var + eps) * w
        B, S, _ = x.shape
        split = lambda t: t.reshape(B, S, N_HEAD, D_HEAD)
        q = split(x @ Wq.T + bq)
        k = split(x @ Wk.T + bk)
        v = split(x @ Wv.T + bv)
        cos, sin = _rope_cache(S, D_HEAD, x.dtype)
        q = _apply_rope(_rmsnorm(q, norm_w), cos, sin)
        k = _apply_rope(_rmsnorm(k, norm_w), cos, sin)
        scores = jnp.einsum('bqhd,bkhd->bhqk', q, k)
        causal = jnp.tril(jnp.ones((S, S), x.dtype))
        pattern = jnp.square(scores / D_HEAD) * causal
        z = jnp.einsum('bhqk,bkhd->bqhd', pattern, v).reshape(B, S, D_MODEL)
        return x + z @ Wo.T * SCALE

    def _L1_xattn_ref(x, context, Wq, Wk, Wv, Wo, bo):
        import jax, jax.numpy as jnp
        import numpy as np
        QUERY_DIM = 128
        CONTEXT_DIM = 96
        HEADS = 8
        DIM_HEAD = 64
        INNER = HEADS * DIM_HEAD
        B, S, _ = x.shape
        L = context.shape[1]
        scale = DIM_HEAD ** (-0.5)
        q = (x @ Wq).reshape(B, S, HEADS, DIM_HEAD).transpose(0, 2, 1, 3)
        k = (context @ Wk).reshape(B, L, HEADS, DIM_HEAD).transpose(0, 2, 1, 3)
        v = (context @ Wv).reshape(B, L, HEADS, DIM_HEAD).transpose(0, 2, 1, 3)
        attn = jnp.einsum('bhsd,bhld->bhsl', q, k) * scale
        attn = jax.nn.softmax(attn, axis=-1)
        out = jnp.einsum('bhsl,bhld->bhsd', attn, v)
        out = out.transpose(0, 2, 1, 3).reshape(B, S, INNER)
        return out @ Wo + bo

    def _L1_ffn_ref(x, router_w, router_b, w1, w2):
        import jax, jax.numpy as jnp
        import numpy as np
        TOP_K = 2
        E = w1.shape[0]
        logits = x @ router_w + router_b
        probs = jax.nn.softmax(logits, axis=-1)
        top_v, top_i = jax.lax.top_k(probs, TOP_K)
        gates = jnp.sum(jax.nn.one_hot(top_i, E + 1, dtype=x.dtype) * top_v[..., None], axis=-2)
        h = jax.nn.gelu(jnp.einsum('btd,edf->ebtf', x, w1), approximate=False)
        y = jnp.einsum('ebtf,efd->ebtd', h, w2)
        out = jnp.einsum('bte,ebtd->btd', gates[..., :E], y) + gates[..., E:] * x
        return out

    def _L2_attn_ref(x, mask, Wq, Wk, Wv, Wout):
        import jax, jax.numpy as jnp
        import numpy as np
        B, S, D, H = (4, 256, 128, 16)
        DH = D // H
        n, s, d = x.shape
        scale = 1.0 / np.sqrt(DH).astype(np.float32)
        q = (x @ Wq).reshape(n, s, H, DH)
        k = (x @ Wk).reshape(n, s, H, DH)
        v = (x @ Wv).reshape(n, s, H, DH)
        attn = jnp.einsum('nqhd,nkhd->nqkh', q, k) * scale
        attn = jax.nn.softmax(attn, axis=-2)
        z = jnp.einsum('nqkh,nkhd->nqhd', attn, v).reshape(n, s, d)
        z = jnp.einsum('nqd,de->nqe', z, Wout)
        return x + z

    def _L2_xattn_ref(q, kv, Wq, Wk, Wv, Wo, bo):
        import jax, jax.numpy as jnp
        import numpy as np
        DIM_Q = 128
        DIM_KV = 96
        N_HEADS = 4

        def _split_heads(x):
            b, l, d = x.shape
            return x.reshape(b, l, N_HEADS, d // N_HEADS).transpose(0, 2, 1, 3)
        qp = q @ Wq.T
        kp = kv @ Wk.T
        vp = kv @ Wv.T
        qh, kh, vh = (_split_heads(qp), _split_heads(kp), _split_heads(vp))
        scale = (DIM_Q // N_HEADS) ** (-0.5)
        scores = jnp.einsum('bhqd,bhkd->bhqk', qh, kh) * scale
        attn = jax.nn.softmax(scores, axis=-1)
        ctx = jnp.einsum('bhqk,bhkd->bhqd', attn, vh)
        b, h, lq, hd = ctx.shape
        ctx = ctx.transpose(0, 2, 1, 3).reshape(b, lq, h * hd)
        return ctx @ Wo.T + bo

    def _L2_ffn_ref(x, w_gate, w_up, w_down):
        import jax, jax.numpy as jnp
        import numpy as np
        HIDDEN = 128
        INNER = 512

        def _weight_quant(w):
            scale = 1.0 / jnp.clip(jnp.mean(jnp.abs(w)), 1e-05)
            wq = jnp.clip(jnp.round(w * scale), -1.0, 1.0) / scale
            return w + jax.lax.stop_gradient(wq - w)

        def _act_quant(x):
            scale = 127.0 / jnp.clip(jnp.max(jnp.abs(x), axis=-1, keepdims=True), 1e-05)
            xq = jnp.clip(jnp.round(x * scale), -128.0, 127.0) / scale
            return x + jax.lax.stop_gradient(xq - x)

        def _bitlinear(x, w):
            return jnp.einsum('bsi,oi->bso', _act_quant(x), _weight_quant(w))
        gate = jax.nn.silu(_bitlinear(x, w_gate))
        up = _bitlinear(x, w_up)
        return _bitlinear(gate * up, w_down)

    def _L3_attn_ref(x, qw, kw, vw, ow):
        import jax, jax.numpy as jnp
        import numpy as np
        D_MODEL, N_HEADS, BATCH, SEQ = (128, 16, 2, 256)

        def get_freqs(seq, n_dim):
            inv_freq = 1.0 / 10000.0 ** (jnp.arange(0, n_dim, 2, dtype=jnp.float32) / n_dim)
            pos = jnp.arange(seq, dtype=jnp.float32)
            return pos[:, None] * inv_freq[None, :]

        def rope(x, freq):
            cos = jnp.cos(freq)[None, :, None, :]
            sin = jnp.sin(freq)[None, :, None, :]
            x1, x2 = (x[..., ::2], x[..., 1::2])
            r1 = x1 * cos - x2 * sin
            r2 = x1 * sin + x2 * cos
            return jnp.stack([r1, r2], axis=-1).reshape(x.shape)
        batch, seq, dim = x.shape
        n_heads = N_HEADS
        n_dim = dim // n_heads
        Q = (x @ qw).astype(jnp.float32).reshape(batch, seq, n_heads, n_dim)
        K = (x @ kw).astype(jnp.float32).reshape(batch, seq, n_heads, n_dim)
        V = (x @ vw).astype(jnp.float32).reshape(batch, seq, n_heads, n_dim)
        freq = get_freqs(seq, n_dim)
        Q = rope(Q, freq)
        K = rope(K, freq)
        Q = jnp.transpose(Q, (0, 2, 1, 3))
        K = jnp.transpose(K, (0, 2, 1, 3))
        V = jnp.transpose(V, (0, 2, 1, 3))
        scale = jnp.sqrt(jnp.float32(n_dim))
        score = jnp.einsum('bhqd,bhkd->bhqk', Q, K) / scale
        causal = jnp.tril(jnp.ones((1, 1, seq, seq), dtype=jnp.float32))
        score = score - 10000000000.0 * (1.0 - causal)
        score = score - jnp.max(score, axis=-1, keepdims=True)
        weights = jax.nn.softmax(score, axis=-1)
        attn = jnp.einsum('bhqk,bhkd->bhqd', weights, V)
        merged = jnp.transpose(attn, (0, 2, 1, 3)).reshape(batch, seq, dim)
        return (merged @ ow).astype(x.dtype)

    def _L3_xattn_ref(x, y, Wq, bq, Wk, bk, Wv, bv, Wo, bo):
        import math
        import jax, jax.numpy as jnp
        import numpy as np
        B, SQ, SKV = (4, 256, 256)
        D_EMBED, D_CROSS, D_ATT, N_HEADS = (128, 96, 128, 16)
        D_HEAD = D_ATT // N_HEADS

        def _split_heads(t):
            b, s, _ = t.shape
            return t.reshape(b, s, N_HEADS, D_HEAD).transpose(0, 2, 1, 3)
        q = _split_heads(x @ Wq + bq)
        k = _split_heads(y @ Wk + bk)
        v = _split_heads(y @ Wv + bv)
        scale = 1.0 / math.sqrt(D_HEAD)
        scores = jnp.einsum('bhqd,bhkd->bhqk', q, k) * scale
        weights = jax.nn.softmax(scores, axis=-1)
        out = jnp.einsum('bhqk,bhkd->bhqd', weights, v)
        out = out.transpose(0, 2, 1, 3).reshape(x.shape[0], x.shape[1], D_ATT)
        return out @ Wo + bo

    def _L3_ffn_ref(x, router_w, router_bias, bank_mag, bank_freq, bank_phase, bank_down, norm_w):
        import jax, jax.numpy as jnp
        import numpy as np
        TOPK = 2
        EPS = 1e-06
        b, t, d = x.shape
        scores = jnp.einsum('btd,nd->btn', x, router_w) + router_bias
        topv, topi = jax.lax.top_k(scores, TOPK)
        weights = jax.nn.softmax(topv, axis=-1)
        fx = x.reshape(b * t, d)
        mag = jnp.einsum('td,ndh->tnh', fx, bank_mag)
        freq = jnp.einsum('td,ndh->tnh', fx, bank_freq)
        hidden = jnp.tanh(mag) * jnp.cos(jax.nn.softplus(freq) + 0.1 + bank_phase[None, :, :])
        out_all = jnp.einsum('tnh,nhd->tnd', hidden, bank_down)
        ti = topi.reshape(b * t, TOPK)
        sel = jnp.take_along_axis(out_all, ti[:, :, None], axis=1)
        out = jnp.einsum('tkd,tk->td', sel, weights.reshape(b * t, TOPK)).reshape(b, t, d)
        out = out * jax.lax.rsqrt(jnp.mean(out * out, axis=-1, keepdims=True) + EPS) * norm_w
        return out
    x = x + _L0_attn_ref(_layernorm(x, axis=-1), L0_attn_Wq, L0_attn_Wk, L0_attn_Wv, L0_attn_Wo, L0_attn_q_scale, L0_attn_k_scale)
    x = x + _L0_xattn_ref(_layernorm(x, axis=-1), ctx_768, L0_xattn_Wq, L0_xattn_bq, L0_xattn_Wk, L0_xattn_bk, L0_xattn_Wv, L0_xattn_bv, L0_xattn_Wo, L0_xattn_bo)
    x = x + _L0_ffn_ref(_layernorm(x, axis=-1), L0_ffn_W_router, L0_ffn_W1, L0_ffn_b1, L0_ffn_Wo, L0_ffn_bo, L0_ffn_ln_gamma, L0_ffn_ln_beta)
    x = x + _L1_attn_ref(_layernorm(x, axis=-1), L1_attn_Wq, L1_attn_bq, L1_attn_Wk, L1_attn_bk, L1_attn_Wv, L1_attn_bv, L1_attn_Wo, L1_attn_norm_w)
    x = x + _L1_xattn_ref(_layernorm(x, axis=-1), ctx_768, L1_xattn_Wq, L1_xattn_Wk, L1_xattn_Wv, L1_xattn_Wo, L1_xattn_bo)
    x = x + _L1_ffn_ref(_layernorm(x, axis=-1), L1_ffn_router_w, L1_ffn_router_b, L1_ffn_w1, L1_ffn_w2)
    x = x + _L2_attn_ref(_layernorm(x, axis=-1), L2_attn_mask, L2_attn_Wq, L2_attn_Wk, L2_attn_Wv, L2_attn_Wout)
    x = x + _L2_xattn_ref(_layernorm(x, axis=-1), ctx_768, L2_xattn_Wq, L2_xattn_Wk, L2_xattn_Wv, L2_xattn_Wo, L2_xattn_bo)
    x = x + _L2_ffn_ref(_layernorm(x, axis=-1), L2_ffn_w_gate, L2_ffn_w_up, L2_ffn_w_down)
    x = x + _L3_attn_ref(_layernorm(x, axis=-1), L3_attn_qw, L3_attn_kw, L3_attn_vw, L3_attn_ow)
    x = x + _L3_xattn_ref(_layernorm(x, axis=-1), ctx_768, L3_xattn_Wq, L3_xattn_bq, L3_xattn_Wk, L3_xattn_bk, L3_xattn_Wv, L3_xattn_bv, L3_xattn_Wo, L3_xattn_bo)
    x = x + _L3_ffn_ref(_layernorm(x, axis=-1), L3_ffn_router_w, L3_ffn_router_bias, L3_ffn_bank_mag, L3_ffn_bank_freq, L3_ffn_bank_phase, L3_ffn_bank_down, L3_ffn_norm_w)
    return x

_drawn_inputs = setup_inputs


def setup_inputs(seed=0):
    import zlib

    import numpy as np

    out = dict(_drawn_inputs(seed))
    spreads = {'L0_attn_q_scale': (1.0, 0.2),
     'L0_attn_k_scale': (1.0, 0.2),
     'L0_xattn_bq': (0.0, 0.1),
     'L0_xattn_bk': (0.0, 2.0),
     'L0_xattn_bv': (0.0, 0.1),
     'L0_xattn_bo': (0.0, 0.1),
     'L0_ffn_ln_gamma': (1.0, 0.2),
     'L0_ffn_ln_beta': (0.0, 0.1),
     'L1_attn_norm_w': (1.0, 0.2),
     'L3_ffn_router_bias': (0.0, 0.1),
     'L3_ffn_norm_w': (1.0, 0.2)}
    factors = {'L0_ffn_b1': 8.0,
     'L1_xattn_bo': 4.767,
     'L1_ffn_router_w': 3.545,
     'L1_ffn_router_b': 8.0,
     'L1_ffn_w1': 5.237,
     'L1_ffn_w2': 5.381,
     'L2_xattn_bo': 5.081,
     'L3_attn_qw': 27.92,
     'L3_attn_kw': 25.664,
     'L3_attn_vw': 8.0,
     'L3_attn_ow': 5.597,
     'L3_xattn_bq': 38.07,
     'L3_xattn_bk': 64.0,
     'L3_xattn_bv': 6.762,
     'L3_xattn_bo': 7.082}
    for name, (base, spread) in spreads.items():
        noise = np.random.default_rng([zlib.crc32(name.encode()), seed]).standard_normal(out[name].shape)
        drawn = base * np.exp(spread * noise) if base else spread * noise
        out[name] = jnp.asarray(drawn.astype(out[name].dtype))
    for name, factor in factors.items():
        out[name] = (out[name] * factor).astype(out[name].dtype)
    return out
```

```python
import concourse.bass as bass
from concourse import mybir
from contextlib import ExitStack

F32 = mybir.dt.float32
BF16 = mybir.dt.bfloat16
ACT = mybir.ActivationFunctionType
ALU = mybir.AluOpType
AXIS = mybir.AxisListType

P = 128
BATCH, SEQ, D = 2, 512, 128
TILES = BATCH * SEQ // P
TPB = SEQ // P
BANK = 512
LN_EPS = 1e-5
HEADS, DH = 16, 8
GH = 4
HG = HEADS // GH
GROUPS = BATCH * HG
SLOTS = 2 * GH
PARTS = 6
SHIFT = PARTS * DH
STACK = 64
NEG = -1e30
KEYS, CTX_D = 32, 96
MAGIC = 12582912.0
BIG_INDEX = 1000.0


def spread(ap, axis, n):
    ap = ap.unsqueeze(axis)
    shape = list(ap.shape)
    shape[axis] = n
    return ap.to_broadcast(shape)


class Signal:

    def __init__(self, handle):
        self.handle, self.base = handle, 0

    def at(self, n):
        return n + self.base

    def close(self, total):
        self.base += total


class Chain:

    def __init__(self, engine, signal):
        self.engine, self.paced, self.count = engine, signal, 0

    def __call__(self, instruction):
        instruction.then_inc(self.paced.handle, 1)
        self.count += 1
        self.engine.wait_ge(self.paced.handle, self.paced.at(self.count))


class Core:

    def __init__(self, nc, ctx):
        self.nc, self.ctx = nc, ctx
        self.signals = {}
        self.x = self.sbuf("x_resid", [P, TILES, D], F32)
        self.xn = self.sbuf("x_normed", [P, TILES, D], F32)
        self.xnT = self.sbuf("x_normed_T", [P, TILES * P], F32)
        self.stats = self.sbuf("bn_stats", [P, TILES, 6], F32)
        self.mean_var = self.sbuf("mean_var", [P, TILES, 2], F32)
        self.var_eps = self.sbuf("var_eps", [P, TILES], F32)
        self.rstd = self.sbuf("rstd", [P, TILES], F32)
        self.minus_half = self.sbuf("minus_half", [P, 1], F32)
        self.ones = self.sbuf("ones", [P, P], F32)
        self.psum = ctx.enter_context(nc.psum_tensor("psum", [P, 8, BANK], F32))
        self.bank = [self.psum[:, i, :] for i in range(8)]

    def sbuf(self, name, shape, dt):
        return self.ctx.enter_context(self.nc.sbuf_tensor(name, shape, dt))

    def sig(self, name):
        if name not in self.signals:
            self.signals[name] = Signal(self.ctx.enter_context(self.nc.semaphore(name)))
        return self.signals[name]



def norm_vector(core, dve):
    x, mv = core.x, core.mean_var
    stats, aggr = core.sig("ln_stats"), core.sig("ln_aggr")
    var_eps, rstd, xn = core.sig("ln_var_eps"), core.sig("ln_rstd"), core.sig("ln_xn")
    for half in range(BATCH):
        tiles = range(half * TPB, (half + 1) * TPB)
        part = slice(half * TPB, (half + 1) * TPB)
        for t in tiles:
            dve.bn_stats(core.stats[:, t, :], x[:, t, :]).then_inc(stats.handle, 1)
        for t in tiles:
            dve.wait_ge(stats.handle, stats.at(t + 1))
            dve.bn_aggr(mv[:, t, :], core.stats[:, t, :]).then_inc(aggr.handle, 1)
        dve.wait_ge(aggr.handle, aggr.at((half + 1) * TPB))
        dve.tensor_scalar(core.var_eps[:, part], mv[:, part, 1], LN_EPS, None, ALU.add)\
           .then_inc(var_eps.handle, 1)
    for half in range(BATCH):
        dve.wait_ge(rstd.handle, rstd.at(half + 1))
        for t in range(half * TPB, (half + 1) * TPB):
            dve.tensor_scalar(core.xn[:, t, :], x[:, t, :], mv[:, t, 0:1], core.rstd[:, t:t + 1],
                              ALU.subtract, ALU.mult).then_inc(xn.handle, 1)


def norm_gpsimd(core, pool):
    var_eps, rstd = core.sig("ln_var_eps"), core.sig("ln_rstd")
    for half in range(BATCH):
        part = slice(half * TPB, (half + 1) * TPB)
        pool.wait_ge(var_eps.handle, var_eps.at(half + 1))
        pool.tensor_tensor(core.rstd[:, part], core.var_eps[:, part],
                           core.minus_half[:, 0:1].to_broadcast([P, TPB]), ALU.pow).then_inc(rstd.handle, 1)


def norm_tensor(core, pe):
    xn, xnT_ps = core.sig("ln_xn"), core.sig("ln_xnT_ps")
    for t in range(TILES):
        pe.wait_ge(xn.handle, xn.at(t + 1))
        last = pe.transpose(core.bank[t // TPB][:, (t % TPB) * P:(t % TPB + 1) * P],
                            core.xn[:, t, :], core.ident)
        if t % TPB == TPB - 1:
            last.then_inc(xnT_ps.handle, 1)


def norm_scalar(core, act):
    xnT_ps, xnT = core.sig("ln_xnT_ps"), core.sig("ln_xnT")
    for half in range(BATCH):
        act.wait_ge(xnT_ps.handle, xnT_ps.at(half + 1))
        act.copy(core.xnT[:, half * SEQ:(half + 1) * SEQ], core.bank[half][:, :]).then_inc(xnT.handle, 1)


def norm_close(core):
    for name, total in (("ln_stats", TILES), ("ln_aggr", TILES), ("ln_var_eps", BATCH), ("ln_rstd", BATCH),
                        ("ln_xn", TILES), ("ln_xnT_ps", BATCH), ("ln_xnT", BATCH)):
        core.sig(name).close(total)


class SelfAttention:

    def __init__(self, name, kind, causal, scale, residual_normed):
        self.name, self.kind, self.causal, self.scale = name, kind, causal, scale
        self.residual_normed = residual_normed


W_QKV, W_OUT = slice(0, 384), slice(384, 512)


def self_attention_project(core, cfg, w, w_sem, qk, v):
    nc = core.nc
    sig = core.sig
    proj, evac, norm_in, norm_out = sig("sa_proj"), sig("sa_evac"), sig("sa_norm_in"), sig("sa_norm_out")
    chain = sig("dve_chain")
    xnT = sig("ln_xnT")
    with ExitStack() as ctx:
        def sbuf(name, shape, dt=F32):
            return ctx.enter_context(nc.sbuf_tensor(f"{cfg.name}_{name}", shape, dt))
        scratch = sbuf("scratch", [P, TILES, SLOTS * HG * DH])
        norm2 = sbuf("norm2", [P, GROUPS * TPB, SLOTS])
        norm1 = sbuf("norm1", [P, GROUPS * TPB, SLOTS])
        factor = sbuf("factor", [P, GROUPS * TPB, SLOTS])
        rows = qk[:, :, :, :].rearrange("p g t (s d) -> p (g t) s d", d=DH)
        scratch_rows = scratch[:, :, :].rearrange("p t (a s d) -> p (t a) s d", s=SLOTS, d=DH)
        counts = {}

        def evacuated(t):
            b, tb = divmod(t, TPB)
            groups = slice(b * HG, (b + 1) * HG)
            return qk[:, groups, tb, :], v[:, groups, tb, :]

        def from_bank(t):
            ps = core.bank[2 + t % 4]
            return (ps[:, 0:256].rearrange("p (g c) -> p g c", g=HG),
                    ps[:, 256:384].rearrange("p (g c) -> p g c", g=HG))

        def head_norms(act):
            act.wait_ge(norm_in.handle, norm_in.at(1))
            act.activation(norm1[:, :, :], norm2[:, :, :], ACT.Sqrt).then_inc(norm_out.handle, 1)

        with nc.Block() as block:
            @block.tensor
            def _(pe):
                norm_tensor(core, pe)
                pe.wait_ge(w_sem, 16)
                for t in range(TILES):
                    if t % TPB == 0:
                        pe.wait_ge(xnT.handle, xnT.at(t // TPB + 1))
                    if t >= 4:
                        pe.wait_ge(evac.handle, evac.at(2 * (t - 3)))
                    pe.matmul(core.bank[2 + t % 4][:, 0:384], core.xnT[:, t * P:(t + 1) * P], w[:, W_QKV],
                              start=True, stop=True).then_inc(proj.handle, 1)

            @block.scalar
            def _(act):
                norm_scalar(core, act)
                if cfg.kind == "square":
                    head_norms(act)
                    return
                func = ACT.Silu if cfg.kind == "silu" else ACT.Copy
                for t in range(TILES):
                    act.wait_ge(proj.handle, proj.at(t + 1))
                    for dst, src in zip(evacuated(t), from_bank(t)):
                        act.activation(dst, src, func).then_inc(evac.handle, 1)
                if cfg.kind == "silu":
                    head_norms(act)

            @block.gpsimd
            def _(pool):
                norm_gpsimd(core, pool)
            @block.vector
            def _(dve):
                norm_vector(core, dve)
                link = Chain(dve, chain)
                if cfg.kind == "square":
                    bias = w[:, 512:896]
                    dve.wait_ge(w_sem, 16)
                    for t in range(TILES):
                        dve.wait_ge(proj.handle, proj.at(t + 1))
                        both = (bias[:, 0:256].rearrange("p (g c) -> p g c", g=HG),
                                bias[:, 256:384].rearrange("p (g c) -> p g c", g=HG))
                        for dst, src, add in zip(evacuated(t), from_bank(t), both):
                            dve.tensor_tensor(dst, src, add, ALU.add).then_inc(evac.handle, 1)
                dve.wait_ge(evac.handle, evac.at(2 * TILES))
                if cfg.kind in ("silu", "square"):
                    link(dve.tensor_tensor(scratch_rows, rows, rows, ALU.mult))
                    link(dve.tensor_reduce(factor[:, :, :], scratch_rows, AXIS.X, ALU.add))
                    if cfg.kind == "silu":
                        dve.tensor_scalar(norm2[:, :, :], factor[:, :, :], 1e-34, None, ALU.max)\
                           .then_inc(norm_in.handle, 1)
                        dve.wait_ge(norm_out.handle, norm_out.at(1))
                        link(dve.tensor_scalar(norm2[:, :, :], norm1[:, :, :], 1e-6, None, ALU.add))
                        link(dve.reciprocal(factor[:, :, :], norm2[:, :, :]))
                        link(dve.tensor_tensor(factor[:, :, :], factor[:, :, :], norm1[:, :, :], ALU.mult))
                        scales = w[:, 512:512 + HG * SLOTS].rearrange("p (g s) -> p g s", g=HG)
                        for b in range(BATCH):
                            at = factor[:, b * HG * TPB:(b + 1) * HG * TPB, :]\
                                .rearrange("p (g t) s -> p g t s", t=TPB)
                            link(dve.tensor_tensor(at, at, spread(scales, 2, TPB), ALU.mult))
                    else:
                        dve.tensor_scalar(norm2[:, :, :], factor[:, :, :], 1.0 / DH, 2.0 ** -23,
                                          ALU.mult, ALU.add).then_inc(norm_in.handle, 1)
                        dve.wait_ge(norm_out.handle, norm_out.at(1))
                        link(dve.reciprocal(factor[:, :, :], norm1[:, :, :]))
                        link(dve.tensor_tensor(norm1[:, :, :], factor[:, :, :], factor[:, :, :], ALU.mult))
                        link(dve.tensor_tensor(norm1[:, :, :], norm1[:, :, :], norm2[:, :, :], ALU.mult))
                        link(dve.tensor_scalar(norm1[:, :, :], norm1[:, :, :], -0.5, 1.5, ALU.mult, ALU.add))
                        link(dve.tensor_tensor(factor[:, :, :], factor[:, :, :], norm1[:, :, :], ALU.mult))
                    link(dve.tensor_tensor(rows, rows, spread(factor[:, :, :], 3, DH), ALU.mult))
                if cfg.kind == "square":
                    per_token = qk[:, :, :, :].rearrange("p g t c -> p (g t) c")
                    link(dve.tensor_tensor(per_token, per_token,
                                           spread(w[:, 896:960], 1, GROUPS * TPB), ALU.mult))
                if cfg.kind in ("square", "rope"):
                    cos, sin = (core.rope_cos, core.rope_sin) if cfg.kind == "rope" \
                        else (core.rope_half_cos, core.rope_half_sin)
                    wide = qk[:, :, :, :].rearrange("p g t c -> p g (t c)")
                    turned = scratch[:, :, :]
                    link(dve.tensor_tensor(turned[:, :, 0::2], wide[:, :, 1::2],
                                           spread(sin[:, 0::2], 1, GROUPS), ALU.mult))
                    link(dve.tensor_tensor(turned[:, :, 1::2], wide[:, :, 0::2],
                                           spread(sin[:, 1::2], 1, GROUPS), ALU.mult))
                    link(dve.tensor_tensor(wide, wide, spread(cos, 1, GROUPS), ALU.mult))
                    link(dve.tensor_tensor(wide, wide, turned, ALU.add))
                counts["chain"] = link.count
    norm_close(core)
    proj.close(TILES)
    evac.close(2 * TILES)
    if cfg.kind in ("silu", "square"):
        norm_in.close(1)
        norm_out.close(1)
    chain.close(counts["chain"])


def self_attention_heads(core, cfg, qk, v, attn):
    nc, sig = core.nc, core.sig
    softmax = cfg.kind != "square"
    stack_ready, kq_ps, kq_ready = sig("sa_stack"), sig("sa_kq_ps"), sig("sa_kq")
    s_done, max_done, shift = sig("sa_scores"), sig("sa_max"), sig("sa_shift")
    q2_ps, q2_ready, st_done = sig("sa_q2_ps"), sig("sa_q2"), sig("sa_scores_T")
    exp_done, masked, pv_done = sig("sa_exp"), sig("sa_masked"), sig("sa_pv")
    o_copied, o_ps, o_done = sig("sa_o_copied"), sig("sa_o_ps"), sig("sa_o_done")
    pool_chain, dve_chain, filled = sig("pool_chain"), sig("dve_chain"), sig("sa_filled")
    inv_done, v_ready = sig("sa_inv"), sig("sa_v")
    POOL_STEPS, DVE_STEPS = 4, 4

    with ExitStack() as ctx:
        def sbuf(name, shape, dt=F32):
            return ctx.enter_context(nc.sbuf_tensor(f"{cfg.name}_{name}", shape, dt))
        stack = [sbuf(f"stack{i}", [P, TPB, SLOTS, STACK], BF16) for i in range(2)]
        parts = sbuf("parts", [P, 3, TPB, SLOTS, DH], BF16)
        rest = sbuf("rest", [P, TPB, SLOTS, DH])
        v_now = [sbuf(f"v_now{i}", [P, TPB, GH, 32]) for i in range(2)]
        kT = [sbuf(f"kT{i}", [P, 2, SEQ], BF16) for i in range(2)]
        qT = [sbuf(f"qT{i}", [P, 2, SEQ], BF16) for i in range(2)]
        q2T = [sbuf(f"q2T{i}", [P, 2, SEQ], BF16) for i in range(2)]
        maxes = sbuf("maxes", [P, TPB, GH])
        shift_parts = sbuf("shift_parts", [P, 2, TPB, GH], BF16)
        shift_rest = sbuf("shift_rest", [P, TPB, GH])
        probs = [sbuf(f"probs{i}", [P, GH, SEQ]) for i in range(2)]
        oT = sbuf("oT", [P, SEQ])
        inv = sbuf("inv", [P, TPB, GH])

        def score_steps():
            return [(h, qt, (qt + 1) * P if cfg.causal else SEQ) for h in range(GH) for qt in range(TPB)]

        def first_query(kt):
            return kt * P if cfg.causal else 0

        U = 2 * TPB
        S = GH * TPB

        READY = 2 * PARTS + (1 if softmax else 0)

        def wait_alone(pool, signal, n):
            pool.wait_ge(signal.handle, signal.at(n))
            pool.sem_inc(core.sig("pool_paced").handle, 1)

        def make_stack(pool, g, p):
            steps = [g * POOL_STEPS + 1]

            def link(instruction):
                instruction.then_inc(pool_chain.handle, 1)
                steps[0] += 1
                wait_alone(pool, pool_chain, steps[0])
            if not (isinstance(g, int) and g == 0):
                wait_alone(pool, stack_ready, g * READY)
            src = qk[:, bass.ds(g, 1), :, :].rearrange("p o t (s d) -> p (o t) s d", d=DH)
            h, m, lo = parts[:, 0], parts[:, 1], parts[:, 2]
            link(pool.tensor_copy(h, src))
            link(pool.tensor_tensor(rest[:, :, :, :], src, h, ALU.subtract))
            link(pool.tensor_copy(m, rest[:, :, :, :]))
            link(pool.tensor_tensor(lo, rest[:, :, :, :], m, ALU.subtract))
            if softmax:
                pool.memset(stack[p][:, :, 0:GH, SHIFT:SHIFT + 3], 0.0).then_inc(stack_ready.handle, 1)
            q = [stack[p][:, :, 0:GH, i * DH:(i + 1) * DH] for i in range(PARTS)]
            k = [stack[p][:, :, GH:SLOTS, i * DH:(i + 1) * DH] for i in range(PARTS)]
            for dst, part in zip(q, (h, m, lo, h, m, h)):
                pool.tensor_copy(dst, part[:, :, 0:GH, :]).then_inc(stack_ready.handle, 1)
            for dst, part in zip(k, (h, h, h, m, m, lo)):
                pool.tensor_copy(dst, part[:, :, GH:SLOTS, :]).then_inc(stack_ready.handle, 1)

        def take_v(pool, g, p):
            pool.tensor_copy(v_now[p][:, :, :, 0:DH],
                             v[:, bass.ds(g, 1), :, :].rearrange("p o t (h d) -> p (o t) h d", d=DH))\
                .then_inc(v_ready.handle, 1)

        def transpose_stack(pe, g, p, which):
            dst = core.bank[0 if which else 7][:, :].bitcast(BF16)
            base = 0 if which else GH
            for pair in range(2):
                for t in range(TPB):
                    last = pe.transpose(dst[:, pair * SEQ + t * P:pair * SEQ + (t + 1) * P],
                                        stack[p][:, t, base + 2 * pair:base + 2 * pair + 2, :], core.ident_bf)
            return last

        def prepare(pe, g, p):
            pe.wait_ge(stack_ready.handle, stack_ready.at((g + 1) * READY))
            early = isinstance(g, int) and g <= 2
            if not (isinstance(g, int) and g == 0):
                pe.wait_ge(kq_ready.handle, kq_ready.at(2 * g))
                if softmax:
                    pe.wait_ge(max_done.handle, max_done.at(g * S - 1))
            if not early:
                pe.wait_ge(o_done.handle, o_done.at(g - 2))
            transpose_stack(pe, g, p, 0).then_inc(kq_ps.handle, 1)
            transpose_stack(pe, g, p, 1).then_inc(kq_ps.handle, 1)

        def scores(pe, g, p, i, first):
            h, qt, width = score_steps()[i]
            if i == 0:
                pe.wait_ge(kq_ready.handle, kq_ready.at(2 * (g + 1)))
            if not (first and i < 2):
                pe.wait_ge(max_done.handle, max_done.at(g * S + i - 1))
            pair, at = h // 2, (h % 2) * STACK
            out = core.bank[i % 2][:, 0:width]
            rows = slice(at, at + STACK)
            last = pe.matmul(out, qT[p][rows, pair, qt * P:(qt + 1) * P], kT[p][rows, pair, 0:width],
                             start=True, stop=not cfg.causal)
            if cfg.causal:
                last = pe.matmul(out[:, width - P:width], core.ident_bf, core.mask_q, start=False, stop=True)
            last.then_inc(s_done.handle, 1)

        def scores_T(pe, g, p, u, first):
            kt, pair = divmod(u, 2)
            if u == 0:
                if softmax:
                    pe.wait_ge(q2_ready.handle, q2_ready.at(g + 1))
                else:
                    pe.wait_ge(kq_ready.handle, kq_ready.at(2 * (g + 1)))
            if not (first and u < 2):
                pe.wait_ge(exp_done.handle, exp_done.at(g * U + u - 1))
            q_from = first_query(kt)
            for half in range(2):
                rows = slice(half * STACK, (half + 1) * STACK)
                src = q2T[p] if softmax else qT[p]
                out = core.bank[2 + 2 * (u % 2) + half]
                masked_here = cfg.causal and softmax
                last = pe.matmul(out[:, 0:SEQ - q_from], kT[p][rows, pair, kt * P:(kt + 1) * P],
                                 src[rows, pair, q_from:SEQ], start=True, stop=not masked_here)
                if masked_here:
                    last = pe.matmul(out[:, 0:P], core.ident_bf, core.mask_k, start=False, stop=True)
            last.then_inc(st_done.handle, 1)

        def values(pe, g, p, kt, first):
            if softmax:
                pe.wait_ge(exp_done.handle, exp_done.at(g * U + 2 * kt + 2))
            else:
                pe.wait_ge(masked.handle, masked.at(g * U + 2 * kt + 2))
            if kt == 0:
                pe.wait_ge(v_ready.handle, v_ready.at(g + 1))
            if kt == 0 and not first:
                pe.wait_ge(o_copied.handle, o_copied.at(g))
            q_from = first_query(kt)
            for h in range(GH):
                last = pe.matmul(core.bank[6][32 * h:32 * h + 32, q_from:SEQ], v_now[p][:, kt, h, :],
                                 probs[kt % 2][:, h, q_from:SEQ], start=kt == 0, stop=kt == TPB - 1,
                                 tile_position=(0, 32 * h))
            last.then_inc(pv_done.handle, 1)

        def shifted(pe, g, p, prev):
            pe.wait_ge(shift.handle, shift.at(g + 1))
            if prev == "kq":
                pe.wait_ge(kq_ready.handle, kq_ready.at(2 * g + 3))
            else:
                pe.wait_ge(o_done.handle, o_done.at(g - 1))
            dst = core.bank[7][:, :].bitcast(BF16)
            for pair in range(2):
                for t in range(TPB):
                    last = pe.transpose(dst[:, pair * SEQ + t * P:pair * SEQ + (t + 1) * P],
                                        stack[p][:, t, 2 * pair:2 * pair + 2, :], core.ident_bf)
            last.then_inc(q2_ps.handle, 1)

        def output_T(pe, g, last_but):
            pe.wait_ge(o_copied.handle, o_copied.at(g + 1))
            if softmax and last_but >= 1:
                pe.wait_ge(q2_ready.handle, q2_ready.at(g + 2))
            elif not softmax and last_but >= 2:
                pe.wait_ge(kq_ready.handle, kq_ready.at(2 * g + 5))
            else:
                pe.wait_ge(o_done.handle, o_done.at(g))
            for t in range(TPB):
                last = pe.transpose(core.bank[7][:, t * P:(t + 1) * P], oT[:, t * P:(t + 1) * P], core.ident)
            last.then_inc(o_ps.handle, 1)

        def tensor_group(pe, g, p, last_but=9, first=False):
            for u in range(U):
                if softmax and last_but >= 1:
                    scores(pe, g + 1, 1 - p, 2 * u, False)
                    scores(pe, g + 1, 1 - p, 2 * u + 1, False)
                scores_T(pe, g, p, u, first)
                if u % 2 == 1 and u > 1:
                    values(pe, g, p, u // 2 - 1, first)
            if last_but >= 2:
                prepare(pe, g + 2, p)
            values(pe, g, p, TPB - 1, first)
            if softmax and last_but >= 1:
                shifted(pe, g + 1, 1 - p, "kq" if last_but >= 2 else "o")
            output_T(pe, g, last_but)

        def weights(act, g, u):
            kt, pair = divmod(u, 2)
            act.wait_ge(st_done.handle, st_done.at(g * U + u + 1))
            if not (isinstance(g, int) and g == 0 and kt < 2):
                act.wait_ge(pv_done.handle, pv_done.at(g * TPB + kt - 1))
            q_from = first_query(kt)
            width = SEQ - q_from
            b0 = 2 + 2 * (u % 2)
            src = core.psum[:, b0:b0 + 2, 0:width]
            act.activation(probs[kt % 2][:, 2 * pair:2 * pair + 2, q_from:SEQ], src,
                           ACT.Exp if softmax else ACT.Square, scale=cfg.scale).then_inc(exp_done.handle, 1)

        def copy_kq(act, g, p):
            for which, (bank, dst) in enumerate(((7, kT[p]), (0, qT[p]))):
                act.wait_ge(kq_ps.handle, kq_ps.at(2 * g + which + 1))
                act.copy(dst[:, :, :], core.bank[bank][:, :].bitcast(BF16)
                         .rearrange("p (a s) -> p a s", a=2)).then_inc(kq_ready.handle, 1)

        def copy_q2(act, g, p):
            act.wait_ge(q2_ps.handle, q2_ps.at(g + 1))
            act.copy(q2T[p][:, :, :], core.bank[7][:, :].bitcast(BF16)
                     .rearrange("p (a s) -> p a s", a=2)).then_inc(q2_ready.handle, 1)

        def scalar_group(act, g, p, last_but=9):
            for u in range(U):
                weights(act, g, u)
            if last_but >= 2:
                copy_kq(act, g + 2, p)
            act.wait_ge(pv_done.handle, pv_done.at((g + 1) * TPB))
            act.copy(oT[:, :], core.bank[6][:, :]).then_inc(o_copied.handle, 1)
            if softmax and last_but >= 1:
                copy_q2(act, g + 1, 1 - p)

        def maxima(dve, g, i):
            h, qt, width = score_steps()[i]
            dve.wait_ge(s_done.handle, s_done.at(g * S + i + 1))
            dve.tensor_reduce(maxes[:, qt, h:h + 1], core.bank[i % 2][:, 0:width], AXIS.X, ALU.max)\
               .then_inc(max_done.handle, 1)

        def make_shift(dve, g, p):
            link = Chain(dve, dve_chain)
            link.count = g * DVE_STEPS
            dve.wait_ge(max_done.handle, max_done.at((g + 1) * S))
            high, mid = shift_parts[:, 0], shift_parts[:, 1]
            link(dve.tensor_scalar(high, maxes[:, :, :], -1.0, None, ALU.mult))
            link(dve.scalar_tensor_tensor(shift_rest[:, :, :], maxes[:, :, :], -1.0, high, ALU.mult, ALU.subtract))
            link(dve.tensor_copy(mid, shift_rest[:, :, :]))
            q = stack[p][:, :, 0:GH, :]
            link(dve.tensor_copy(q[:, :, :, SHIFT:SHIFT + 2],
                                 shift_parts[:, :, :, :].rearrange("p w t h -> p t h w")))
            dve.tensor_tensor(q[:, :, :, SHIFT + 2], shift_rest[:, :, :], mid, ALU.subtract)\
               .then_inc(shift.handle, 1)

        def finish(dve, g):
            dve.wait_ge(o_ps.handle, o_ps.at(g + 1))
            out = core.bank[7][:, :].rearrange("p (t h c) -> p t h c", t=TPB, h=GH)
            start = g % HG + (g // HG) * (HG * TPB)
            dst = attn[:, bass.ds(start, TPB, HG), :].rearrange("p t (h d) -> p t h d", d=DH)
            if softmax:
                dve.reciprocal(inv[:, :, :], out[:, :, :, DH]).then_inc(inv_done.handle, 1)
                dve.wait_ge(inv_done.handle, inv_done.at(g + 1))
                dve.tensor_tensor(dst, out[:, :, :, 0:DH], spread(inv[:, :, :], 3, DH), ALU.mult)\
                   .then_inc(o_done.handle, 1)
            else:
                dve.tensor_copy(dst, out[:, :, :, 0:DH]).then_inc(o_done.handle, 1)

        def mask_squares(dve, g, u):
            kt, pair = divmod(u, 2)
            dve.wait_ge(exp_done.handle, exp_done.at(g * U + u + 1))
            at = probs[kt % 2][:, 2 * pair:2 * pair + 2, kt * P:(kt + 1) * P]
            dve.tensor_tensor(at, at, spread(core.keep_k, 1, 2), ALU.mult).then_inc(masked.handle, 1)

        def vector_group(dve, g, p, last_but=9):
            if softmax:
                if last_but >= 1:
                    for i in range(S):
                        maxima(dve, g + 1, i)
                    make_shift(dve, g + 1, 1 - p)
            else:
                for u in range(U):
                    mask_squares(dve, g, u)
            finish(dve, g)

        with nc.Block() as block:
            @block.gpsimd
            def _(pool):
                for p in range(2):
                    pool.memset(stack[p][:, :, :, SHIFT:STACK], 0.0).then_inc(filled.handle, 1)
                    pool.memset(v_now[p][:, :, :, DH:32], 0.0).then_inc(filled.handle, 1)
                pool.wait_ge(filled.handle, filled.at(4))
                for p in range(2):
                    pool.memset(stack[p][:, :, GH:SLOTS, SHIFT:SHIFT + 3], 1.0).then_inc(filled.handle, 1)
                    pool.memset(v_now[p][:, :, :, DH:DH + 1], 1.0).then_inc(filled.handle, 1)
                pool.wait_ge(filled.handle, filled.at(8))
                pool.memset(parts[:, 0:1, 0:1, 0:1, 0:1], 0.0).then_inc(pool_chain.handle, 1)
                pool.wait_ge(pool_chain.handle, pool_chain.at(1))
                for g in range(2):
                    make_stack(pool, g, g)
                    take_v(pool, g, g)
                with pool.Fori(1, GROUPS // 2) as i:
                    for p in range(2):
                        g = i * 2 + p
                        if softmax:
                            wait_alone(pool, q2_ps, g - 1)
                        wait_alone(pool, kq_ps, (g - 1) * 2)
                        make_stack(pool, g, p)
                        wait_alone(pool, pv_done, (g - 1) * TPB)
                        take_v(pool, g, p)

            @block.tensor
            def _(pe):
                pe.wait_ge(filled.handle, filled.at(8))
                prepare(pe, 0, 0)
                if softmax:
                    for i in range(S):
                        scores(pe, 0, 0, i, True)
                prepare(pe, 1, 1)
                if softmax:
                    shifted(pe, 0, 0, "kq")
                tensor_group(pe, 0, 0, first=True)
                tensor_group(pe, 1, 1)
                with pe.Fori(1, GROUPS // 2 - 1) as i:
                    for p in range(2):
                        tensor_group(pe, i * 2 + p, p)
                tensor_group(pe, GROUPS - 2, 0, 1)
                tensor_group(pe, GROUPS - 1, 1, 0)

            @block.scalar
            def _(act):
                copy_kq(act, 0, 0)
                copy_kq(act, 1, 1)
                if softmax:
                    copy_q2(act, 0, 0)
                scalar_group(act, 0, 0)
                scalar_group(act, 1, 1)
                with act.Fori(1, GROUPS // 2 - 1) as i:
                    for p in range(2):
                        scalar_group(act, i * 2 + p, p)
                scalar_group(act, GROUPS - 2, 0, 1)
                scalar_group(act, GROUPS - 1, 1, 0)

            @block.vector
            def _(dve):
                if softmax:
                    for i in range(S):
                        maxima(dve, 0, i)
                    make_shift(dve, 0, 0)
                with dve.Fori(0, GROUPS // 2 - 1) as i:
                    for p in range(2):
                        vector_group(dve, i * 2 + p, p)
                vector_group(dve, GROUPS - 2, 0, 1)
                vector_group(dve, GROUPS - 1, 1, 0)

    for s, total in ((stack_ready, GROUPS * READY), (v_ready, GROUPS), (kq_ps, 2 * GROUPS), (kq_ready, 2 * GROUPS),
                     (st_done, GROUPS * U), (exp_done, GROUPS * U), (pv_done, GROUPS * TPB),
                     (o_copied, GROUPS), (o_ps, GROUPS), (o_done, GROUPS), (filled, 8),
                     (pool_chain, GROUPS * POOL_STEPS + 1)):
        s.close(total)
    if softmax:
        for s, total in ((s_done, GROUPS * S), (max_done, GROUPS * S), (shift, GROUPS), (q2_ps, GROUPS),
                         (q2_ready, GROUPS), (inv_done, GROUPS), (dve_chain, GROUPS * DVE_STEPS)):
            s.close(total)
    else:
        masked.close(GROUPS * U)


def self_attention_out(core, cfg, w, attn):
    nc, sig = core.nc, core.sig
    ps, attnT_ready, done, added = sig("so_ps"), sig("so_attnT"), sig("so_done"), sig("so_added")
    with nc.sbuf_tensor(f"{cfg.name}_attnT", [P, TILES * P], F32) as attnT, nc.Block() as block:
        @block.tensor
        def _(pe):
            for b in range(BATCH):
                for t in range(TPB):
                    last = pe.transpose(core.bank[b][:, t * P:(t + 1) * P],
                                        attn[:, (b * TPB + t) * HG:(b * TPB + t + 1) * HG, :],
                                        core.ident)
                last.then_inc(ps.handle, 1)
            for b in range(BATCH):
                pe.wait_ge(attnT_ready.handle, attnT_ready.at(b + 1))
                for t in range(TPB):
                    at = (b * TPB + t) * P
                    last = pe.matmul(core.bank[2 + b][:, t * P:(t + 1) * P], attnT[:, at:at + P], w[:, W_OUT],
                                     start=True, stop=True)
                last.then_inc(done.handle, 1)

        @block.scalar
        def _(act):
            for b in range(BATCH):
                act.wait_ge(ps.handle, ps.at(b + 1))
                act.copy(attnT[:, b * SEQ:(b + 1) * SEQ], core.bank[b][:, :]).then_inc(attnT_ready.handle, 1)

        @block.vector
        def _(dve):
            if cfg.residual_normed:
                dve.tensor_tensor(core.x[:, :, :], core.x[:, :, :], core.xn[:, :, :], ALU.add)\
                   .then_inc(added.handle, 1)
                dve.wait_ge(added.handle, added.at(1))
            for b in range(BATCH):
                dve.wait_ge(done.handle, done.at(b + 1))
                xb = core.x[:, b * TPB:(b + 1) * TPB, :]
                dve.tensor_tensor(xb, xb, core.bank[2 + b][:, :].rearrange("p (t d) -> p t d", t=TPB),
                                  ALU.add).then_inc(added.handle, 1)
    ps.close(BATCH)
    attnT_ready.close(BATCH)
    done.close(BATCH)
    added.close(BATCH + (1 if cfg.residual_normed else 0))


def self_attention(core, cfg, w, w_sem):
    with core.nc.sbuf_tensor(f"{cfg.name}_qk", [P, GROUPS, TPB, SLOTS * DH], F32) as qk, \
            core.nc.sbuf_tensor(f"{cfg.name}_v", [P, GROUPS, TPB, GH * DH], F32) as v, \
            core.nc.sbuf_tensor(f"{cfg.name}_attn", [P, TILES * HG, GH * DH], F32) as attn:
        self_attention_project(core, cfg, w, w_sem, qk, v)
        self_attention_heads(core, cfg, qk, v, attn)
        self_attention_out(core, cfg, w, attn)


class CrossAttention:

    def __init__(self, name, heads, dh, biased, guarded):
        self.name, self.heads, self.dh, self.biased, self.guarded = name, heads, dh, biased, guarded
        self.inner = heads * dh
        self.chunks = self.inner // P
        self.heads_per_chunk = P // dh
        self.prob_chunks = heads * KEYS // P
        self.scale = dh ** -0.5
        at, self.cols = 0, {}
        for part, width in (("wq", self.inner), ("wo", self.inner), ("bo", D), ("bq", self.chunks),
                            ("bk", self.chunks), ("bv", self.inner)):
            if part in ("bq", "bk", "bv") and not biased:
                continue
            self.cols[part] = slice(at, at + width)
            at += width

    def prob_chunks_of(self, c):
        if self.chunks == 1:
            return range(self.prob_chunks)
        return [c * self.heads_per_chunk // (P // KEYS)]

    def v_block(self, c, pk):
        return pk if self.chunks == 1 else c


def prepare_context(core, cfgs, w, w_sem, ctx_w, ctx_sem):
    nc, sig = core.nc, core.sig
    k_done, v_done, chain = sig("cx_k"), sig("cx_v"), sig("dve_chain")
    ctxT, ctx4 = ctx_w[:, 0:BATCH * KEYS], ctx_w[:, BATCH * KEYS:BATCH * KEYS + BATCH * P]
    at = BATCH * KEYS + BATCH * P
    wk, wv = {}, {}
    for cfg in cfgs:
        wk[cfg.name] = ctx_w[:, at:at + cfg.inner]
        wv[cfg.name] = ctx_w[:, at + cfg.inner:at + 2 * cfg.inner]
        at += 2 * cfg.inner
    k_ps, v_ps, k_at, v_at = {}, {}, 0, 0
    for cfg in cfgs:
        k_ps[cfg.name] = core.bank[0][:, k_at:k_at + cfg.chunks * BATCH * KEYS]
        k_at += cfg.chunks * BATCH * KEYS
        for b in range(BATCH):
            v_ps[cfg.name, b] = core.bank[3 + b][:, :] if cfg.inner == BANK \
                else core.bank[1 + b][:, v_at:v_at + cfg.inner]
        v_at += 0 if cfg.inner == BANK else cfg.inner
    with nc.sbuf_tensor("cx_k_rows", [P, 4, BATCH * KEYS], F32) as k_rows, \
            nc.sbuf_tensor("cx_v_rows", [P, BANK], F32) as v_rows, nc.Block() as block:
        count = [0]

        @block.tensor
        def _(pe):
            pe.wait_ge(ctx_sem, 16)
            for cfg in cfgs:
                for c in range(cfg.chunks):
                    last = pe.matmul(k_ps[cfg.name][:, c * BATCH * KEYS:(c + 1) * BATCH * KEYS],
                                     wk[cfg.name][:, c * P:(c + 1) * P], ctxT, start=True, stop=True)
                last.then_inc(k_done.handle, 1)
                for b in range(BATCH):
                    last = pe.matmul(v_ps[cfg.name, b], ctx4[:, b * P:(b + 1) * P], wv[cfg.name],
                                     start=True, stop=True)
                last.then_inc(v_done.handle, 1)

        @block.vector
        def _(dve):
            link = Chain(dve, chain)
            for n, cfg in enumerate(cfgs):
                hc, dh = cfg.heads_per_chunk, cfg.dh
                kbd, vbd = core.kbd[cfg.name], core.vbd[cfg.name]
                pack, cols = w[cfg.name], cfg.cols
                dve.wait_ge(k_done.handle, k_done.at(len(cfgs)))
                dve.wait_ge(w_sem[cfg.name], 16)
                for c in range(cfg.chunks):
                    src = k_ps[cfg.name][:, c * BATCH * KEYS:(c + 1) * BATCH * KEYS]
                    if cfg.biased:
                        bk = pack[:, cols["bk"].start + c:cols["bk"].start + c + 1]
                        link(dve.tensor_scalar(k_rows[:, c, :], src, bk, cfg.scale, ALU.add, ALU.mult))
                    else:
                        link(dve.tensor_scalar(k_rows[:, c, :], src, cfg.scale, None, ALU.mult))
                    for b in range(BATCH):
                        link(dve.tensor_tensor(kbd[:, b, c, :].rearrange("p (h k) -> p h k", h=hc),
                                               spread(k_rows[:, c, b * KEYS:(b + 1) * KEYS], 1, hc),
                                               spread(core.const[f"head_mask{dh}"][:, 0:hc], 2, KEYS), ALU.mult))
                dve.wait_ge(v_done.handle, v_done.at(len(cfgs)))
                for b in range(BATCH):
                    src = v_ps[cfg.name, b]
                    if cfg.biased:
                        link(dve.tensor_tensor(v_rows[:, 0:cfg.inner], src, pack[:, cols["bv"]], ALU.add))
                    else:
                        link(dve.tensor_copy(v_rows[:, 0:cfg.inner], src))
                    mask = core.const[f"row_mask{dh}"].rearrange("p (a c) -> p a c", c=P)
                    rows = spread(v_rows[:, 0:P], 1, cfg.prob_chunks) if cfg.chunks == 1 \
                        else v_rows[:, :].rearrange("p (a c) -> p a c", c=P)
                    link(dve.tensor_tensor(vbd[:, b, :, :], rows, mask, ALU.mult))
            count[0] = link.count
    k_done.close(len(cfgs))
    v_done.close(len(cfgs))
    chain.close(count[0])


def cross_attention(core, cfg, w, w_sem):
    nc, sig = core.nc, core.sig
    H, C, PK = cfg.heads, cfg.chunks, cfg.prob_chunks
    q_ps, q_ready, s_ps, minus_max = sig("xa_q_ps"), sig("xa_q"), sig("xa_scores"), sig("xa_minus_max")
    exp_done, prob, pT_ps, pT_ready = sig("xa_exp"), sig("xa_prob"), sig("xa_pT_ps"), sig("xa_pT")
    o_ps, o_ready, out_ps, chain = sig("xa_o_ps"), sig("xa_o"), sig("xa_out_ps"), sig("dve_chain")
    nan_in, nan_ps, xnT = sig("xa_nan_in"), sig("xa_nan_ps"), sig("ln_xnT")
    kbd, vbd, cols = core.kbd[cfg.name], core.vbd[cfg.name], cfg.cols
    WIDTH = H * KEYS
    count = [0]
    with ExitStack() as ctx:
        def sbuf(name, shape, dt=F32):
            return ctx.enter_context(nc.sbuf_tensor(f"{cfg.name}_{name}", shape, dt))
        qT = sbuf("qT", [P, C, TILES * P])
        clipped = sbuf("clipped", [P, 2, WIDTH])
        top = sbuf("top", [P, TILES, H])
        probs = sbuf("probs", [P, TILES, H, KEYS])
        sums = sbuf("sums", [P, TILES, H])
        inv = sbuf("inv", [P, TILES, H])
        pT = sbuf("pT", [P, PK, TILES * P])
        oT = sbuf("oT", [P, C, TILES * P])
        odd = sbuf("odd", [P, TILES * H])
        odd_rows = sbuf("odd_rows", [P, 1])
        flag = sbuf("flag", [P, 1])
        share = sbuf("share", [P, 1])

        with nc.Block() as block:
            @block.tensor
            def _(pe):
                norm_tensor(core, pe)
                pe.wait_ge(w_sem, 16)
                for half in range(BATCH):
                    pe.wait_ge(xnT.handle, xnT.at(half + 1))
                    for c in range(C):
                        n = half * C + c
                        if n >= 4:
                            pe.wait_ge(q_ready.handle, q_ready.at(n - 3))
                        pe.matmul(core.bank[2 + n % 4], w[:, cols["wq"]][:, c * P:(c + 1) * P],
                                  core.xnT[:, half * SEQ:(half + 1) * SEQ], start=True, stop=True)\
                          .then_inc(q_ps.handle, 1)
                for t in range(TILES):
                    b = t // TPB
                    pe.wait_ge(q_ready.handle, q_ready.at((b + 1) * C))
                    if t >= 2:
                        pe.wait_ge(minus_max.handle, minus_max.at(t - 1))
                    for c in range(C):
                        width = WIDTH // C
                        last = pe.matmul(core.bank[6 + t % 2][:, c * width:(c + 1) * width],
                                         qT[:, c, t * P:(t + 1) * P], kbd[:, b, c, :], start=True, stop=True)
                    last.then_inc(s_ps.handle, 1)
                if cfg.guarded:
                    pe.wait_ge(nan_in.handle, nan_in.at(1))
                    pe.matmul(core.bank[6][:, 0:1], core.ones[:, :], odd_rows[:, :], start=True, stop=True)\
                      .then_inc(nan_ps.handle, 1)
                for t in range(TILES):
                    pe.wait_ge(prob.handle, prob.at(t + 1))
                    if t >= 2:
                        pe.wait_ge(pT_ready.handle, pT_ready.at(t - 1))
                    for k in range(PK):
                        last = pe.transpose(core.bank[t % 2][:, k * P:(k + 1) * P],
                                            probs[:, t, k * 4:(k + 1) * 4, :].rearrange("p h k -> p (h k)"),
                                            core.ident)
                    last.then_inc(pT_ps.handle, 1)
                    if t % TPB == TPB - 1:
                        b = t // TPB
                        pe.wait_ge(pT_ready.handle, pT_ready.at(t + 1))
                        for c in range(C):
                            n = b * C + c
                            if n >= 2:
                                pe.wait_ge(o_ready.handle, o_ready.at(n - 1))
                            chunks = list(cfg.prob_chunks_of(c))
                            for k in chunks:
                                last = pe.matmul(core.bank[2 + n % 2], vbd[:, b, cfg.v_block(c, k), :],
                                                 pT[:, k, b * SEQ:(b + 1) * SEQ],
                                                 start=k == chunks[0], stop=k == chunks[-1])
                            last.then_inc(o_ps.handle, 1)
                for b in range(BATCH):
                    pe.wait_ge(o_ready.handle, o_ready.at((b + 1) * C))
                    for t in range(TPB):
                        at = (b * TPB + t) * P
                        for c in range(C):
                            last = pe.matmul(core.bank[4 + b][:, t * P:(t + 1) * P], oT[:, c, at:at + P],
                                             w[:, cols["wo"]][:, c * D:(c + 1) * D],
                                             start=c == 0, stop=c == C - 1)
                    last.then_inc(out_ps.handle, 1)

            @block.gpsimd
            def _(pool):
                norm_gpsimd(core, pool)

            @block.scalar
            def _(act):
                norm_scalar(core, act)
                for n in range(BATCH * C):
                    half, c = divmod(n, C)
                    act.wait_ge(q_ps.handle, q_ps.at(n + 1))
                    dst, src = qT[:, c, half * SEQ:(half + 1) * SEQ], core.bank[2 + n % 4]
                    if cfg.biased:
                        at = cols["bq"].start + c
                        act.activation(dst, src, ACT.Identity, bias=w[:, at:at + 1]).then_inc(q_ready.handle, 1)
                    else:
                        act.copy(dst, src).then_inc(q_ready.handle, 1)
                for t in range(TILES):
                    act.wait_ge(minus_max.handle, minus_max.at(t + 1))
                    act.activation(probs[:, t, :, :], probs[:, t, :, :], ACT.Exp).then_inc(exp_done.handle, 1)
                for t in range(TILES):
                    act.wait_ge(pT_ps.handle, pT_ps.at(t + 1))
                    act.copy(pT[:, :, t * P:(t + 1) * P],
                             core.bank[t % 2][:, 0:PK * P].rearrange("p (k c) -> p k c", k=PK))\
                       .then_inc(pT_ready.handle, 1)
                    if t % TPB == TPB - 1:
                        b = t // TPB
                        for c in range(C):
                            n = b * C + c
                            act.wait_ge(o_ps.handle, o_ps.at(n + 1))
                            act.copy(oT[:, c, b * SEQ:(b + 1) * SEQ], core.bank[2 + n % 2])\
                               .then_inc(o_ready.handle, 1)

            @block.vector
            def _(dve):
                norm_vector(core, dve)
                link = Chain(dve, chain)

                def normalise(t):
                    dve.wait_ge(exp_done.handle, exp_done.at(t + 1))
                    link(dve.tensor_reduce(sums[:, t, :], probs[:, t, :, :], AXIS.X, ALU.add))
                    link(dve.reciprocal(inv[:, t, :], sums[:, t, :]))
                    done = dve.tensor_tensor(probs[:, t, :, :], probs[:, t, :, :], spread(inv[:, t, :], 2, KEYS),
                                             ALU.mult)
                    if cfg.guarded:
                        link(done)
                    else:
                        done.then_inc(prob.handle, 1)

                for t in range(TILES):
                    dve.wait_ge(s_ps.handle, s_ps.at(t + 1))
                    src = core.bank[6 + t % 2][:, 0:WIDTH]
                    if cfg.guarded:
                        link(dve.tensor_scalar(clipped[:, t % 2, :], src, -1e4, 1e4, ALU.max, ALU.min))
                        src = clipped[:, t % 2, :]
                    src = src.rearrange("p (h k) -> p h k", h=H)
                    link(dve.tensor_reduce(top[:, t, :], src, AXIS.X, ALU.max))
                    dve.tensor_tensor(probs[:, t, :, :], src, spread(top[:, t, :], 2, KEYS), ALU.subtract)\
                       .then_inc(minus_max.handle, 1)
                    if t >= 1:
                        normalise(t - 1)
                normalise(TILES - 1)
                if cfg.guarded:
                    all_sums = sums[:, :, :].rearrange("p t h -> p (t h)")
                    link(dve.memset(share[:, :], 1.0 / KEYS))
                    link(dve.tensor_tensor(odd[:, :], all_sums, all_sums, ALU.not_equal))
                    dve.tensor_reduce(odd_rows[:, :], odd[:, :], AXIS.X, ALU.max).then_inc(nan_in.handle, 1)
                    dve.wait_ge(nan_ps.handle, nan_ps.at(1))
                    link(dve.tensor_copy(flag[:, :], core.bank[6][:, 0:1]))
                    flat = probs[:, :, :, :].rearrange("p t h k -> p (t h k)")
                    n = TILES * WIDTH
                    dve.copy_predicated(flat, flag[:, :].bitcast(mybir.dt.uint32).to_broadcast([P, n]),
                                        share[:, :].to_broadcast([P, n])).then_inc(prob.handle, TILES)
                link(dve.tensor_tensor(core.x[:, :, :], core.x[:, :, :], spread(w[:, cols["bo"]], 1, TILES),
                                       ALU.add))
                for b in range(BATCH):
                    dve.wait_ge(out_ps.handle, out_ps.at(b + 1))
                    xb = core.x[:, b * TPB:(b + 1) * TPB, :]
                    link(dve.tensor_tensor(xb, xb, core.bank[4 + b].rearrange("p (t d) -> p t d", t=TPB),
                                           ALU.add))
                count[0] = link.count
    norm_close(core)
    for s, total in ((q_ps, BATCH * C), (q_ready, BATCH * C), (s_ps, TILES), (minus_max, TILES),
                     (exp_done, TILES), (prob, TILES), (pT_ps, TILES), (pT_ready, TILES),
                     (o_ps, BATCH * C), (o_ready, BATCH * C), (out_ps, BATCH)):
        s.close(total)
    if cfg.guarded:
        nan_in.close(1)
        nan_ps.close(1)
    chain.close(count[0])


def first_of_largest(dve, link, onehot, scores, iota, tmp, top):
    n = scores.shape[2]
    indices = spread(iota[:, 0:n], 1, TILES)
    link(dve.tensor_reduce(top, scores, AXIS.X, ALU.max))
    link(dve.tensor_tensor(tmp, scores, spread(top, 2, n), ALU.is_lt))
    link(dve.scalar_tensor_tensor(tmp, tmp, BIG_INDEX, indices, ALU.mult, ALU.add))
    link(dve.tensor_reduce(top, tmp, AXIS.X, ALU.min))
    link(dve.tensor_tensor(onehot, tmp, spread(top, 2, n), ALU.is_equal))


def router_tensor(core, pe, router, n, done):
    xnT = core.sig("ln_xnT")
    for t in range(TILES):
        if t % TPB == 0:
            pe.wait_ge(xnT.handle, xnT.at(t // TPB + 1))
        last = pe.matmul(core.bank[2][:, t * n:(t + 1) * n], core.xnT[:, t * P:(t + 1) * P], router,
                         start=True, stop=True)
    last.then_inc(done.handle, 1)


L0_EXPERTS, L0_INNER = 4, 512
L0F = {"router": slice(0, 4), "w1": slice(4, 2052), "wo": slice(2052, 2564), "bo": slice(2564, 2692),
       "gamma": slice(2692, 2820), "beta": slice(2820, 2948)}


def expert_feed_forward(core, w, w_sem, b1, b1_sem):
    nc, sig = core.nc, core.sig
    E, C = L0_EXPERTS, L0_INNER // P
    logits_ps, picked, masked = sig("f0_logits"), sig("f0_picked"), sig("f0_masked")
    mT_ps, mT_ready, oT_ps, oT_ready = sig("f0_mT_ps"), sig("f0_mT"), sig("f0_oT_ps"), sig("f0_oT")
    h_ps, h_ready, y_ps = sig("f0_h_ps"), sig("f0_h"), sig("f0_y_ps")
    var_eps, rstd, chain = sig("f0_var_eps"), sig("f0_rstd"), sig("dve_chain")
    count = [0]
    with ExitStack() as ctx:
        def sbuf(name, shape, dt=F32):
            return ctx.enter_context(nc.sbuf_tensor(f"l0_ffn_{name}", shape, dt))
        onehot = sbuf("onehot", [P, TILES, E])
        tmp = sbuf("tmp", [P, TILES, E])
        top = sbuf("top", [P, TILES])
        masked_x = sbuf("masked_x", [P, E, TILES, D])
        masked_xT = sbuf("masked_xT", [P, E, TILES * P])
        onehotT = sbuf("onehotT", [E, TILES * P])
        hT = sbuf("hT", [P, C, TILES * P])
        y = sbuf("y", [P, TILES, D])
        y_stats = sbuf("y_stats", [P, TILES, 6])
        y_mv = sbuf("y_mv", [P, TILES, 2])
        y_var = sbuf("y_var", [P, TILES])
        y_rstd = sbuf("y_rstd", [P, TILES])

        with nc.Block() as block:
            @block.tensor
            def _(pe):
                norm_tensor(core, pe)
                pe.wait_ge(w_sem, 16)
                router_tensor(core, pe, w[:, L0F["router"]], E, logits_ps)
                pe.wait_ge(picked.handle, picked.at(1))
                for b in range(BATCH):
                    for t in range(TPB):
                        last = pe.transpose(core.bank[2 + b][0:E, t * P:(t + 1) * P],
                                            onehot[:, b * TPB + t, :], core.ident)
                    last.then_inc(oT_ps.handle, 1)
                for e in range(E):
                    pe.wait_ge(masked.handle, masked.at(e + 1))
                    for b in range(BATCH):
                        n = e * BATCH + b
                        if n >= 2:
                            pe.wait_ge(mT_ready.handle, mT_ready.at(n - 1))
                        for t in range(TPB):
                            last = pe.transpose(core.bank[b][:, t * P:(t + 1) * P],
                                                masked_x[:, e, b * TPB + t, :], core.ident)
                        last.then_inc(mT_ps.handle, 1)
                pe.wait_ge(mT_ready.handle, mT_ready.at(E * BATCH))
                pe.wait_ge(oT_ready.handle, oT_ready.at(BATCH))
                pe.wait_ge(b1_sem, 16)
                for c in range(C):
                    for b in range(BATCH):
                        n = c * BATCH + b
                        if n >= 4:
                            pe.wait_ge(h_ready.handle, h_ready.at(n - 3))
                        out = core.bank[4 + n % 4]
                        cols = slice(b * SEQ, (b + 1) * SEQ)
                        for e in range(E):
                            at = e * L0_INNER + c * P
                            pe.matmul(out, w[:, L0F["w1"]][:, at:at + P], masked_xT[:, e, cols],
                                      start=e == 0, stop=False)
                        pe.matmul(out, b1[:, c * P:(c + 1) * P], onehotT[:, cols], start=False, stop=True)\
                          .then_inc(h_ps.handle, 1)
                pe.wait_ge(h_ready.handle, h_ready.at(C * BATCH))
                for b in range(BATCH):
                    for t in range(TPB):
                        at = (b * TPB + t) * P
                        for c in range(C):
                            last = pe.matmul(core.bank[2 + b][:, t * P:(t + 1) * P], hT[:, c, at:at + P],
                                             w[:, L0F["wo"]][:, c * D:(c + 1) * D], start=c == 0, stop=c == C - 1)
                    last.then_inc(y_ps.handle, 1)

            @block.gpsimd
            def _(pool):
                norm_gpsimd(core, pool)
                pool.wait_ge(var_eps.handle, var_eps.at(1))
                pool.tensor_tensor(y_rstd[:, :], y_var[:, :], core.minus_half[:, 0:1].to_broadcast([P, TILES]),
                                   ALU.pow).then_inc(rstd.handle, 1)

            @block.scalar
            def _(act):
                norm_scalar(core, act)
                for b in range(BATCH):
                    act.wait_ge(oT_ps.handle, oT_ps.at(b + 1))
                    act.copy(onehotT[:, b * SEQ:(b + 1) * SEQ], core.bank[2 + b][0:E, :])\
                       .then_inc(oT_ready.handle, 1)
                for n in range(L0_EXPERTS * BATCH):
                    e, b = divmod(n, BATCH)
                    act.wait_ge(mT_ps.handle, mT_ps.at(n + 1))
                    act.copy(masked_xT[:, e, b * SEQ:(b + 1) * SEQ], core.bank[b]).then_inc(mT_ready.handle, 1)
                for n in range(C * BATCH):
                    c, b = divmod(n, BATCH)
                    act.wait_ge(h_ps.handle, h_ps.at(n + 1))
                    act.activation(hT[:, c, b * SEQ:(b + 1) * SEQ], core.bank[4 + n % 4], ACT.Gelu)\
                       .then_inc(h_ready.handle, 1)

            @block.vector
            def _(dve):
                norm_vector(core, dve)
                link = Chain(dve, chain)
                dve.wait_ge(logits_ps.handle, logits_ps.at(1))
                first_of_largest(dve, link, onehot[:, :, :],
                                 core.bank[2][:, 0:TILES * E].rearrange("p (t e) -> p t e", t=TILES),
                                 core.const["iota"], tmp[:, :, :], top[:, :])
                dve.memset(y_var[:, :], 0.0).then_inc(picked.handle, 1)
                for e in range(E):
                    dve.tensor_tensor(masked_x[:, e, :, :], core.xn[:, :, :], spread(onehot[:, :, e], 2, D),
                                      ALU.mult).then_inc(masked.handle, 1)
                link(dve.tensor_tensor(y[:, :, :], core.xn[:, :, :], spread(w[:, L0F["bo"]], 1, TILES), ALU.add))
                for b in range(BATCH):
                    dve.wait_ge(y_ps.handle, y_ps.at(b + 1))
                    yb = y[:, b * TPB:(b + 1) * TPB, :]
                    link(dve.tensor_tensor(yb, yb, core.bank[2 + b].rearrange("p (t d) -> p t d", t=TPB), ALU.add))
                for t in range(TILES):
                    link(dve.bn_stats(y_stats[:, t, :], y[:, t, :]))
                    link(dve.bn_aggr(y_mv[:, t, :], y_stats[:, t, :]))
                dve.wait_ge(picked.handle, picked.at(1))
                dve.tensor_scalar(y_var[:, :], y_mv[:, :, 1], 1e-12, None, ALU.add).then_inc(var_eps.handle, 1)
                dve.wait_ge(rstd.handle, rstd.at(1))
                for t in range(TILES):
                    link(dve.tensor_scalar(y[:, t, :], y[:, t, :], y_mv[:, t, 0:1], y_rstd[:, t:t + 1],
                                           ALU.subtract, ALU.mult))
                link(dve.tensor_tensor(y[:, :, :], y[:, :, :], spread(w[:, L0F["gamma"]], 1, TILES), ALU.mult))
                link(dve.tensor_tensor(y[:, :, :], y[:, :, :], spread(w[:, L0F["beta"]], 1, TILES), ALU.add))
                link(dve.tensor_tensor(core.x[:, :, :], core.x[:, :, :], y[:, :, :], ALU.add))
                count[0] = link.count
    norm_close(core)
    for s, total in ((logits_ps, 1), (picked, 1), (masked, E), (mT_ps, E * BATCH), (mT_ready, E * BATCH),
                     (oT_ps, BATCH), (oT_ready, BATCH), (h_ps, C * BATCH), (h_ready, C * BATCH), (y_ps, BATCH),
                     (var_eps, 1), (rstd, 1), (chain, count[0])):
        s.close(total)


L1_EXPERTS, L1_INNER = 8, 512
L1F = {"router": slice(0, 9), "bias": slice(9, 18)}


def gated_experts(core, w, w_sem, w1_dram, w2_dram):
    nc, sig = core.nc, core.sig
    E, N, C = L1_EXPERTS, L1_EXPERTS + 1, L1_INNER // P
    logits_ps, exp_in, exp_out, gates_ready = sig("f1_logits"), sig("f1_exp_in"), sig("f1_exp_out"), sig("f1_gates")
    w1_in, w2_in = [sig("f1_w1_even"), sig("f1_w1_odd")], [sig("f1_w2_even"), sig("f1_w2_odd")]
    up_ps, h_ready, y_ps, y_read, chain = sig("f1_up_ps"), sig("f1_h"), sig("f1_y_ps"), sig("f1_y_read"), sig("dve_chain")
    count = [0]
    with ExitStack() as ctx:
        def sbuf(name, shape, dt=F32):
            return ctx.enter_context(nc.sbuf_tensor(f"l1_ffn_{name}", shape, dt))
        w1 = [sbuf(f"w1_{i}", [P, L1_INNER]) for i in range(2)]
        w2 = [sbuf(f"w2_{i}", [P, C * D]) for i in range(2)]
        hT = [sbuf(f"hT{i}", [P, C, TILES * P]) for i in range(2)]
        probs = sbuf("probs", [P, TILES, N])
        rest = sbuf("rest", [P, TILES, N])
        tmp = sbuf("tmp", [P, TILES, N])
        choice = sbuf("choice", [P, 2, TILES, N])
        top = sbuf("top", [P, TILES])
        gates = sbuf("gates", [P, TILES, N])
        acc = sbuf("acc", [P, TILES, D])

        def load(sp, e, p):
            sp.dma_start(w1[p][:, :], w1_dram[bass.ds(e, 1), :, :].rearrange("o p c -> (o p) c"))\
              .then_inc(w1_in[p].handle, 16)
            sp.dma_start(w2[p][:, :], w2_dram[bass.ds(e, 1), :, :].rearrange("o p c -> (o p) c"))\
              .then_inc(w2_in[p].handle, 16)

        def up(pe, e, p, half_e, first=False):
            pe.wait_ge(w1_in[p].handle, w1_in[p].at(16 * (half_e + 1)))
            for c in range(C):
                if not (first and c < 2):
                    pe.wait_ge(h_ready.handle, h_ready.at(e * C + c - 1))
                for b in range(BATCH):
                    last = pe.matmul(core.bank[3 + 2 * (c % 2) + b - 1], w1[p][:, c * P:(c + 1) * P],
                                     core.xnT[:, b * SEQ:(b + 1) * SEQ], start=True, stop=True)
                last.then_inc(up_ps.handle, 1)

        def down(pe, e, p, half_e, first=False):
            pe.wait_ge(w2_in[p].handle, w2_in[p].at(16 * (half_e + 1)))
            pe.wait_ge(h_ready.handle, h_ready.at((e + 1) * C))
            for b in range(BATCH):
                if not first:
                    pe.wait_ge(y_read.handle, y_read.at((e - 1) * BATCH + b + 1))
                for t in range(TPB):
                    at = (b * TPB + t) * P
                    for c in range(C):
                        last = pe.matmul(core.bank[6 + b][:, t * P:(t + 1) * P], hT[p][:, c, at:at + P],
                                         w2[p][:, c * D:(c + 1) * D], start=c == 0, stop=c == C - 1)
                last.then_inc(y_ps.handle, 1)

        def gelu(act, e, p, no_down=False):
            if not no_down:
                act.wait_ge(y_ps.handle, y_ps.at((e - 1) * BATCH))
            for c in range(C):
                act.wait_ge(up_ps.handle, up_ps.at(e * C + c + 1))
                act.activation(hT[p][:, c, :].rearrange("p (b s) -> p b s", b=BATCH),
                               core.psum[:, 2 + 2 * (c % 2):4 + 2 * (c % 2), :], ACT.Gelu).then_inc(h_ready.handle, 1)

        def accumulate(dve, e):
            for b in range(BATCH):
                dve.wait_ge(y_ps.handle, y_ps.at(e * BATCH + b + 1))
                for t in range(TPB):
                    at = acc[:, b * TPB + t, :]
                    last = dve.scalar_tensor_tensor(at, core.bank[6 + b][:, t * P:(t + 1) * P],
                                                    gates[:, b * TPB + t, bass.ds(e, 1)], at, ALU.mult, ALU.add)
                last.then_inc(y_read.handle, 1)
                dve.wait_ge(y_read.handle, y_read.at(e * BATCH + b + 1))

        with nc.Block() as block:
            @block.sync
            def _(sp):
                load(sp, 0, 0)
                load(sp, 1, 1)
                with sp.Fori(1, E // 2) as i:
                    for p in range(2):
                        e = i * 2 + p
                        sp.wait_ge(y_ps.handle, y_ps.at((e - 1) * BATCH))
                        load(sp, e, p)

            @block.tensor
            def _(pe):
                norm_tensor(core, pe)
                pe.wait_ge(w_sem, 16)
                router_tensor(core, pe, w[:, L1F["router"]], N, logits_ps)
                pe.wait_ge(exp_in.handle, exp_in.at(1))
                up(pe, 0, 0, 0, first=True)
                up(pe, 1, 1, 0)
                down(pe, 0, 0, 0, first=True)
                with pe.Fori(1, E // 2) as i:
                    up(pe, i * 2, 0, i)
                    down(pe, i * 2 - 1, 1, i - 1)
                    up(pe, i * 2 + 1, 1, i)
                    down(pe, i * 2, 0, i)
                down(pe, E - 1, 1, E // 2 - 1)

            @block.gpsimd
            def _(pool):
                norm_gpsimd(core, pool)

            @block.scalar
            def _(act):
                norm_scalar(core, act)
                act.wait_ge(exp_in.handle, exp_in.at(1))
                act.activation(probs[:, :, :], probs[:, :, :], ACT.Exp).then_inc(exp_out.handle, 1)
                gelu(act, 0, 0, no_down=True)
                gelu(act, 1, 1, no_down=True)
                with act.Fori(1, E // 2) as i:
                    gelu(act, i * 2, 0)
                    gelu(act, i * 2 + 1, 1)

            @block.vector
            def _(dve):
                norm_vector(core, dve)
                link = Chain(dve, chain)
                dve.wait_ge(logits_ps.handle, logits_ps.at(1))
                scores = core.bank[2][:, 0:TILES * N].rearrange("p (t e) -> p t e", t=TILES)
                link(dve.tensor_tensor(rest[:, :, :], scores, spread(w[:, L1F["bias"]], 1, TILES), ALU.add))
                link(dve.tensor_reduce(top[:, :], rest[:, :, :], AXIS.X, ALU.max))
                dve.tensor_tensor(probs[:, :, :], rest[:, :, :], spread(top[:, :], 2, N), ALU.subtract)\
                   .then_inc(exp_in.handle, 1)
                dve.wait_ge(exp_out.handle, exp_out.at(1))
                link(dve.tensor_reduce(top[:, :], probs[:, :, :], AXIS.X, ALU.add))
                link(dve.reciprocal(top[:, :], top[:, :]))
                link(dve.tensor_tensor(probs[:, :, :], probs[:, :, :], spread(top[:, :], 2, N), ALU.mult))
                first, second = choice[:, 0], choice[:, 1]
                first_of_largest(dve, link, first, probs[:, :, :], core.const["iota"], tmp[:, :, :], top[:, :])
                link(dve.scalar_tensor_tensor(rest[:, :, :], first, -BIG_INDEX, probs[:, :, :], ALU.mult, ALU.add))
                first_of_largest(dve, link, second, rest[:, :, :], core.const["iota"], tmp[:, :, :], top[:, :])
                link(dve.tensor_tensor(tmp[:, :, :], first, second, ALU.add))
                link(dve.tensor_tensor(gates[:, :, :], tmp[:, :, :], probs[:, :, :], ALU.mult))
                link(dve.tensor_tensor(acc[:, :, :], core.xn[:, :, :], spread(gates[:, :, E], 2, D), ALU.mult))
                with dve.Fori(0, E // 2) as i:
                    for p in range(2):
                        accumulate(dve, i * 2 + p)
                link(dve.tensor_tensor(core.x[:, :, :], core.x[:, :, :], acc[:, :, :], ALU.add))
                count[0] = link.count
    norm_close(core)
    for s, total in ((logits_ps, 1), (exp_in, 1), (exp_out, 1), (w1_in[0], 16 * E // 2), (w1_in[1], 16 * E // 2),
                     (w2_in[0], 16 * E // 2), (w2_in[1], 16 * E // 2), (up_ps, E * C), (h_ready, E * C),
                     (y_ps, E * BATCH), (y_read, E * BATCH), (chain, count[0])):
        s.close(total)


L2_INNER = 512
L2F = {"gate": slice(0, 512), "up": slice(512, 1024), "down": slice(1024, 1536)}


def quantised_feed_forward(core, w, w_sem):
    nc, sig = core.nc, core.sig
    C = L2_INNER // P
    sums_in, sums_ps, wq_ready, xq_ready = sig("f2_sums"), sig("f2_sums_ps"), sig("f2_wq"), sig("f2_xq")
    xT_ps, xT_ready, gu_ps, gate_ready, gu_read = (sig("f2_xT_ps"), sig("f2_xT"), sig("f2_gu_ps"),
                                                   sig("f2_gate"), sig("f2_gu_read"))
    hq_ready, hT_ps, hT_ready, y_ps, scaled = sig("f2_hq"), sig("f2_hT_ps"), sig("f2_hT"), sig("f2_y_ps"), sig("f2_scaled")
    chain, x_gate_ready = sig("dve_chain"), sig("f2_x_gate")
    count = [0]
    with ExitStack() as ctx:
        def sbuf(name, shape, dt=F32):
            return ctx.enter_context(nc.sbuf_tensor(f"l2_ffn_{name}", shape, dt))
        sizes = sbuf("sizes", [P, 3])
        means = sbuf("means", [P, 3])
        w_scale = sbuf("w_scale", [P, 3])
        rounded = sbuf("rounded", [P, 3, 512])
        wq = sbuf("wq", [P, 3, 512], BF16)
        x_top = sbuf("x_top", [P, TILES])
        x_scale = sbuf("x_scale", [P, TILES])
        x_unit = sbuf("x_unit", [P, TILES])
        x_gate = sbuf("x_gate", [P, TILES])
        x_up = sbuf("x_up", [P, TILES])
        x_round = sbuf("x_round", [P, TILES, D])
        xq = sbuf("xq", [P, TILES, D], BF16)
        xqT = sbuf("xqT", [P, TILES * P], BF16)
        gate = sbuf("gate", [P, TILES, L2_INNER])
        h = sbuf("h", [P, TILES, L2_INNER])
        h_top = sbuf("h_top", [P, TILES])
        h_scale = sbuf("h_scale", [P, TILES])
        h_unit = sbuf("h_unit", [P, TILES])
        hq = sbuf("hq", [P, TILES, L2_INNER], BF16)
        hqT = sbuf("hqT", [P, TILES, C, P], BF16)

        def quantise(dve, link, top, scale, unit, src, rounded_at, dst, last):
            link(dve.tensor_reduce(top, src, AXIS.X, ALU.max, apply_absolute_value=True))
            link(dve.tensor_scalar(top, top, 1e-5, None, ALU.max))
            link(dve.reciprocal(scale, top))
            link(dve.tensor_scalar(scale, scale, 127.0, None, ALU.mult))
            link(dve.tensor_scalar(unit, top, 1.0 / 127.0, None, ALU.mult))
            link(dve.tensor_scalar(rounded_at, src, scale, MAGIC, ALU.mult, ALU.add))
            link(dve.tensor_scalar(rounded_at, rounded_at, -MAGIC, 127.0, ALU.add, ALU.min))
            dve.tensor_scalar(dst, rounded_at, -128.0, None, ALU.max).then_inc(last.handle, 1)

        def down(pe, t):
            pe.wait_ge(hq_ready.handle, hq_ready.at(t + 1))
            if t >= 2:
                pe.wait_ge(scaled.handle, scaled.at(t - 1))
            flat = core.bank[6 + t % 2].bitcast(BF16)
            for c in range(C):
                last = pe.transpose(flat[:, c * P:(c + 1) * P], hq[:, t, c * P:(c + 1) * P], core.ident_bf)
            last.then_inc(hT_ps.handle, 1)
            pe.wait_ge(hT_ready.handle, hT_ready.at(t + 1))
            for c in range(C):
                last = pe.matmul(core.bank[t % 2][:, 0:D], hqT[:, t, c, :], wq[:, 2, c * D:(c + 1) * D],
                                 start=c == 0, stop=c == C - 1)
            last.then_inc(y_ps.handle, 1)

        def hidden_T(act, t):
            act.wait_ge(hT_ps.handle, hT_ps.at(t + 1))
            act.copy(hqT[:, t, :, :], core.bank[6 + t % 2].bitcast(BF16)[:, 0:L2_INNER]
                     .rearrange("p (c t) -> p c t", c=C)).then_inc(hT_ready.handle, 1)

        def output(dve, link, t):
            link(dve.tensor_scalar(h_unit[:, t:t + 1], h_unit[:, t:t + 1], means[:, 2:3], None, ALU.mult))
            dve.wait_ge(y_ps.handle, y_ps.at(t + 1))
            dve.scalar_tensor_tensor(core.x[:, t, :], core.bank[t % 2][:, 0:D], h_unit[:, t:t + 1],
                                     core.x[:, t, :], ALU.mult, ALU.add).then_inc(scaled.handle, 1)

        with nc.Block() as block:
            @block.tensor
            def _(pe):
                norm_tensor(core, pe)
                pe.wait_ge(sums_in.handle, sums_in.at(1))
                pe.matmul(core.bank[2][:, 0:3], core.ones[:, :], sizes[:, :], start=True, stop=True)\
                  .then_inc(sums_ps.handle, 1)
                for t in range(TILES):
                    pe.wait_ge(xq_ready.handle, xq_ready.at(t + 1))
                    if t == 0:
                        pe.wait_ge(core.sig("ln_xnT").handle, core.sig("ln_xnT").at(BATCH))
                    out = core.bank[t // TPB].bitcast(BF16)
                    last = pe.transpose(out[:, (t % TPB) * P:(t % TPB + 1) * P], xq[:, t, :], core.ident_bf)
                    if t % TPB == TPB - 1:
                        last.then_inc(xT_ps.handle, 1)
                pe.wait_ge(wq_ready.handle, wq_ready.at(3))
                for t in range(TILES):
                    pe.wait_ge(xT_ready.handle, xT_ready.at(t // TPB + 1))
                    if t >= 2:
                        pe.wait_ge(gu_read.handle, gu_read.at(t - 1))
                    for k in range(2):
                        last = pe.matmul(core.bank[2 + 2 * (t % 2) + k], xqT[:, t * P:(t + 1) * P], wq[:, k, :],
                                         start=True, stop=True)
                    last.then_inc(gu_ps.handle, 1)
                    if t >= 1:
                        down(pe, t - 1)
                down(pe, TILES - 1)

            @block.gpsimd
            def _(pool):
                norm_gpsimd(core, pool)

            @block.scalar
            def _(act):
                norm_scalar(core, act)
                for b in range(BATCH):
                    act.wait_ge(xT_ps.handle, xT_ps.at(b + 1))
                    act.copy(xqT[:, b * SEQ:(b + 1) * SEQ], core.bank[b].bitcast(BF16)[:, 0:SEQ])\
                       .then_inc(xT_ready.handle, 1)
                act.wait_ge(x_gate_ready.handle, x_gate_ready.at(1))
                for t in range(TILES):
                    act.wait_ge(gu_ps.handle, gu_ps.at(t + 1))
                    act.activation(gate[:, t, :], core.bank[2 + 2 * (t % 2)], ACT.Silu, scale=x_gate[:, t:t + 1])\
                       .then_inc(gate_ready.handle, 1)
                    if t >= 1:
                        hidden_T(act, t - 1)
                hidden_T(act, TILES - 1)

            @block.vector
            def _(dve):
                link = Chain(dve, chain)
                dve.wait_ge(w_sem, 16)
                w3 = w[:, :].rearrange("p (k c) -> p k c", k=3)
                dve.tensor_reduce(sizes[:, :], w3, AXIS.X, ALU.add, apply_absolute_value=True)\
                   .then_inc(sums_in.handle, 1)
                norm_vector(core, dve)
                dve.wait_ge(sums_ps.handle, sums_ps.at(1))
                link(dve.tensor_scalar(means[:, :], core.bank[2][:, 0:3], 1.0 / (P * 512), 1e-5, ALU.mult, ALU.max))
                link(dve.reciprocal(w_scale[:, :], means[:, :]))
                for k in range(3):
                    link(dve.tensor_scalar(rounded[:, k, :], w3[:, k, :], w_scale[:, k:k + 1], MAGIC, ALU.mult, ALU.add))
                    link(dve.tensor_scalar(rounded[:, k, :], rounded[:, k, :], -MAGIC, 1.0, ALU.add, ALU.min))
                    dve.tensor_scalar(wq[:, k, :], rounded[:, k, :], -1.0, None, ALU.max).then_inc(wq_ready.handle, 1)
                xn_done = core.sig("ln_xn")
                dve.wait_ge(xn_done.handle, xn_done.at(TILES))
                for t in range(TILES):
                    quantise(dve, link, x_top[:, t:t + 1], x_scale[:, t:t + 1], x_unit[:, t:t + 1],
                             core.xn[:, t, :], x_round[:, t, :], xq[:, t, :], xq_ready)
                dve.tensor_scalar(x_gate[:, :], x_unit[:, :], means[:, 0:1], None, ALU.mult)\
                   .then_inc(x_gate_ready.handle, 1)
                link(dve.tensor_scalar(x_up[:, :], x_unit[:, :], means[:, 1:2], None, ALU.mult))
                for t in range(TILES):
                    dve.wait_ge(gate_ready.handle, gate_ready.at(t + 1))
                    dve.scalar_tensor_tensor(h[:, t, :], core.bank[3 + 2 * (t % 2)], x_up[:, t:t + 1],
                                             gate[:, t, :], ALU.mult, ALU.mult).then_inc(gu_read.handle, 1)
                    dve.wait_ge(gu_read.handle, gu_read.at(t + 1))
                    quantise(dve, link, h_top[:, t:t + 1], h_scale[:, t:t + 1], h_unit[:, t:t + 1],
                             h[:, t, :], h[:, t, :], hq[:, t, :], hq_ready)
                    if t >= 1:
                        output(dve, link, t - 1)
                output(dve, link, TILES - 1)
                count[0] = link.count

    norm_close(core)
    for s, total in ((sums_in, 1), (x_gate_ready, 1), (sums_ps, 1), (wq_ready, 3), (xq_ready, TILES), (xT_ps, BATCH), (xT_ready, BATCH),
                     (gu_ps, TILES), (gate_ready, TILES), (gu_read, TILES), (hq_ready, TILES), (hT_ps, TILES),
                     (hT_ready, TILES), (y_ps, TILES), (scaled, TILES), (chain, count[0])):
        s.close(total)


L3_EXPERTS, L3_INNER = 16, 256
L3F = {"router": slice(0, 16), "bias": slice(16, 32), "phase": slice(32, 64), "norm": slice(64, 192)}
TURN = 6.283185307179586
SIN_SCALE = 6.2831850


def tanh_cos_experts(core, w, w_sem, up_dram, down_dram):
    nc, sig = core.nc, core.sig
    N = L3_EXPERTS
    UNITS, C = N // 2, 2 * L3_INNER // P
    CE = L3_INNER // P
    logits_ps, logits_read, exp_in, exp_out = sig("f3_logits"), sig("f3_logits_read"), sig("f3_exp_in"), sig("f3_exp_out")
    up_in, down_in = [sig("f3_up_even"), sig("f3_up_odd")], [sig("f3_down_even"), sig("f3_down_odd")]
    f_ps, m_ps, abs_done, exp_done, ln_done = sig("f3_f_ps"), sig("f3_m_ps"), sig("f3_abs"), sig("f3_exp"), sig("f3_ln")
    z_done, u_done, k_done, frac_done = sig("f3_z"), sig("f3_u"), sig("f3_k"), sig("f3_frac")
    tanh_done, sin_done, h_done = sig("f3_tanh"), sig("f3_sin"), sig("f3_h")
    y_ps, y_read, chain, filled = sig("f3_y_ps"), sig("f3_y_read"), sig("dve_chain"), sig("f3_filled")
    mean_sq, rstd = sig("f3_mean_sq"), sig("f3_rstd")
    count = [0]
    with ExitStack() as ctx:
        def sbuf(name, shape, dt=F32):
            return ctx.enter_context(nc.sbuf_tensor(f"l3_ffn_{name}", shape, dt))
        w_up = [sbuf(f"w_up{i}", [P, 2 * C * P]) for i in range(2)]
        w_down = [sbuf(f"w_down{i}", [P, C * D]) for i in range(2)]
        angle = sbuf("angle", [P, C, TILES * P])
        whole = sbuf("whole", [P, C, TILES * P])
        tanh_m = sbuf("tanh_m", [P, C, TILES * P])
        hT = sbuf("hT", [P, C, TILES * P])
        phase = sbuf("phase", [P, N * CE])
        scores = sbuf("scores", [P, TILES, N])
        rest = sbuf("rest", [P, TILES, N])
        tmp = sbuf("tmp", [P, TILES, N])
        choice = sbuf("choice", [P, 2, TILES, N])
        best = sbuf("best", [P, 2, TILES])
        top = sbuf("top", [P, TILES])
        gap = sbuf("gap", [P, TILES])
        gates = sbuf("gates", [P, TILES, N])
        acc = sbuf("acc", [P, TILES, D])
        mean = sbuf("mean", [P, TILES])
        inv_root = sbuf("inv_root", [P, TILES])

        def load_up(sp, u, p):
            sp.dma_start(w_up[p][:, :], up_dram[bass.ds(u, 1), :, :].rearrange("o p c -> (o p) c"))\
              .then_inc(up_in[p].handle, 16)

        def load_down(sp, u, p):
            sp.dma_start(w_down[p][:, :], down_dram[bass.ds(u, 1), :, :].rearrange("o p c -> (o p) c"))\
              .then_inc(down_in[p].handle, 16)

        def pair(c):
            return 3 + 2 * (c % 2) - 1

        def product(pe, p, c, which, done):
            for b in range(BATCH):
                at = (which * C + c) * P
                last = pe.matmul(core.bank[pair(c) + b], w_up[p][:, at:at + P],
                                 core.xnT[:, b * SEQ:(b + 1) * SEQ], start=True, stop=True)
            last.then_inc(done.handle, 1)

        def freq(pe, u, p, c, first=False):
            if c >= 2:
                pe.wait_ge(z_done.handle, z_done.at(u * C + c - 1))
            elif not first:
                pe.wait_ge(tanh_done.handle, tanh_done.at(u * C + c - 1))
            product(pe, p, c, 0, f_ps)

        def mag(pe, u, p, c):
            if c < 2:
                pe.wait_ge(z_done.handle, z_done.at(u * C + c + 3))
            else:
                pe.wait_ge(tanh_done.handle, tanh_done.at(u * C + c - 1))
            product(pe, p, c, 1, m_ps)

        def down(pe, u, p, expert, first=False):
            pe.wait_ge(h_done.handle, h_done.at(u * C + (expert + 1) * CE))
            for b in range(BATCH):
                if expert or not first:
                    n = 2 * BATCH * u + expert * BATCH + b
                    pe.wait_ge(y_read.handle, y_read.at(n - 1))
                for t in range(TPB):
                    at = (b * TPB + t) * P
                    for c in range(expert * CE, (expert + 1) * CE):
                        last = pe.matmul(core.bank[6 + b][:, t * P:(t + 1) * P], hT[:, c, at:at + P],
                                         w_down[p][:, c * D:(c + 1) * D],
                                         start=c == expert * CE, stop=c == (expert + 1) * CE - 1)
                last.then_inc(y_ps.handle, 1)

        def tensor_unit(pe, u, p, half_u, half_next, first=False, last=False):
            if not last:
                pe.wait_ge(up_in[1 - p].handle, up_in[1 - p].at(16 * (half_next + 1)))
                freq(pe, u + 1, 1 - p, 0)
                freq(pe, u + 1, 1 - p, 1)
            pe.wait_ge(down_in[p].handle, down_in[p].at(16 * (half_u + 1)))
            down(pe, u, p, 0, first)
            if not last:
                freq(pe, u + 1, 1 - p, 2)
                freq(pe, u + 1, 1 - p, 3)
            down(pe, u, p, 1, first)
            if not last:
                for c in range(C):
                    mag(pe, u + 1, 1 - p, c)

        def scalar_unit(act, u, first=False):
            for c0 in range(0, C, 2):
                for c in (c0, c0 + 1):
                    act.wait_ge(f_ps.handle, f_ps.at(u * C + c + 1))
                    if not first:
                        act.wait_ge(h_done.handle, h_done.at((u - 1) * C + c + 1))
                    act.activation(angle[:, c, :].rearrange("p (b s) -> p b s", b=BATCH),
                                   core.psum[:, pair(c):pair(c) + 2, :], ACT.Abs).then_inc(abs_done.handle, 1)
                for c in (c0, c0 + 1):
                    act.wait_ge(abs_done.handle, abs_done.at(u * C + c + 1))
                    act.activation(angle[:, c, :], angle[:, c, :], ACT.Exp, scale=-1.0).then_inc(exp_done.handle, 1)
                for c in (c0, c0 + 1):
                    act.wait_ge(exp_done.handle, exp_done.at(u * C + c + 1))
                    act.activation(angle[:, c, :], angle[:, c, :], ACT.Ln, bias=1.0).then_inc(ln_done.handle, 1)
            for c in range(C):
                act.wait_ge(m_ps.handle, m_ps.at(u * C + c + 1))
                act.activation(tanh_m[:, c, :].rearrange("p (b s) -> p b s", b=BATCH),
                               core.psum[:, pair(c):pair(c) + 2, :], ACT.Tanh).then_inc(tanh_done.handle, 1)
            for c in range(C):
                act.wait_ge(frac_done.handle, frac_done.at(u * C + c + 1))
                act.activation(angle[:, c, :], angle[:, c, :], ACT.Sin, scale=SIN_SCALE).then_inc(sin_done.handle, 1)

        def gpsimd_unit(pool, u):
            for c in range(C):
                wait_alone(pool, k_done, u * C + c + 1)
                pool.tensor_tensor(angle[:, c, :], angle[:, c, :], whole[:, c, :], ALU.subtract)\
                    .then_inc(frac_done.handle, 1)

        def wait_alone(pool, signal, n):
            pool.wait_ge(signal.handle, signal.at(n))
            pool.sem_inc(core.sig("pool_paced").handle, 1)

        def angles(dve, u):
            for c in range(C):
                dve.wait_ge(ln_done.handle, ln_done.at(u * C + c + 1))
                at = angle[:, c, :]
                dve.scalar_tensor_tensor(at.rearrange("p (b s) -> p b s", b=BATCH),
                                         core.psum[:, pair(c):pair(c) + 2, :], 0.0,
                                         at.rearrange("p (b s) -> p b s", b=BATCH), ALU.max, ALU.add)\
                   .then_inc(z_done.handle, 1)
                dve.wait_ge(z_done.handle, z_done.at(u * C + c + 1))
                dve.tensor_scalar(at, at, 1.0 / TURN, phase[:, bass.ds(u * C + c, 1)], ALU.mult, ALU.add)\
                   .then_inc(u_done.handle, 1)
                dve.wait_ge(u_done.handle, u_done.at(u * C + c + 1))
                dve.tensor_scalar(whole[:, c, :], at, MAGIC, -MAGIC, ALU.add, ALU.add).then_inc(k_done.handle, 1)

        def hidden(dve, u, first=False):
            for c in range(C):
                dve.wait_ge(sin_done.handle, sin_done.at(u * C + c + 1))
                if not first and c % CE == 0:
                    dve.wait_ge(y_ps.handle, y_ps.at((u - 1) * 2 * BATCH + (c // CE + 1) * BATCH))
                dve.tensor_tensor(hT[:, c, :], tanh_m[:, c, :], angle[:, c, :], ALU.mult).then_inc(h_done.handle, 1)

        def accumulate(dve, u):
            for expert in range(2):
                for b in range(BATCH):
                    n = u * 2 * BATCH + expert * BATCH + b + 1
                    dve.wait_ge(y_ps.handle, y_ps.at(n))
                    for t in range(TPB):
                        at = acc[:, b * TPB + t, :]
                        last = dve.scalar_tensor_tensor(at, core.bank[6 + b][:, t * P:(t + 1) * P],
                                                        gates[:, b * TPB + t, bass.ds(u * 2 + expert, 1)], at,
                                                        ALU.mult, ALU.add)
                    last.then_inc(y_read.handle, 1)
                    dve.wait_ge(y_read.handle, y_read.at(n))

        def vector_unit(dve, u):
            angles(dve, u + 1)
            accumulate(dve, u)
            hidden(dve, u + 1)

        with nc.Block() as block:
            @block.sync
            def _(sp):
                for u in range(2):
                    load_up(sp, u, u)
                    load_down(sp, u, u)
                with sp.Fori(1, UNITS // 2) as i:
                    for p in range(2):
                        u = i * 2 + p
                        sp.wait_ge(m_ps.handle, m_ps.at((u - 1) * C))
                        load_up(sp, u, p)
                        sp.wait_ge(y_ps.handle, y_ps.at((u - 1) * 2 * BATCH))
                        load_down(sp, u, p)

            @block.tensor
            def _(pe):
                norm_tensor(core, pe)
                pe.wait_ge(w_sem, 16)
                router_tensor(core, pe, w[:, L3F["router"]], N, logits_ps)
                pe.wait_ge(logits_read.handle, logits_read.at(1))
                pe.wait_ge(up_in[0].handle, up_in[0].at(16))
                for c in range(C):
                    freq(pe, 0, 0, c, first=True)
                for c in range(C):
                    mag(pe, 0, 0, c)
                tensor_unit(pe, 0, 0, 0, 0, first=True)
                with pe.Fori(1, UNITS // 2) as i:
                    tensor_unit(pe, i * 2 - 1, 1, i - 1, i)
                    tensor_unit(pe, i * 2, 0, i, i)
                tensor_unit(pe, UNITS - 1, 1, UNITS // 2 - 1, 0, last=True)

            @block.gpsimd
            def _(pool):
                norm_gpsimd(core, pool)
                pool.memset(acc[:, :, :], 0.0).then_inc(filled.handle, 1)
                with pool.Fori(0, UNITS // 2) as i:
                    for p in range(2):
                        gpsimd_unit(pool, i * 2 + p)
                pool.wait_ge(mean_sq.handle, mean_sq.at(1))
                pool.tensor_tensor(inv_root[:, :], mean[:, :], core.minus_half[:, 0:1].to_broadcast([P, TILES]),
                                   ALU.pow).then_inc(rstd.handle, 1)

            @block.scalar
            def _(act):
                norm_scalar(core, act)
                act.wait_ge(exp_in.handle, exp_in.at(1))
                act.activation(gap[:, :], gap[:, :], ACT.Exp).then_inc(exp_out.handle, 1)
                scalar_unit(act, 0, first=True)
                scalar_unit(act, 1)
                with act.Fori(1, UNITS // 2) as i:
                    scalar_unit(act, i * 2)
                    scalar_unit(act, i * 2 + 1)

            @block.vector
            def _(dve):
                norm_vector(core, dve)
                link = Chain(dve, chain)
                dve.wait_ge(w_sem, 16)
                link(dve.tensor_scalar(phase[:, :], w[:, L3F["phase"]], 0.1 + TURN / 4, 1.0 / TURN,
                                       ALU.add, ALU.mult))
                dve.wait_ge(logits_ps.handle, logits_ps.at(1))
                dve.tensor_tensor(scores[:, :, :], core.bank[2][:, 0:TILES * N].rearrange("p (t e) -> p t e", t=TILES),
                                  spread(w[:, L3F["bias"]], 1, TILES), ALU.add).then_inc(logits_read.handle, 1)
                dve.wait_ge(logits_read.handle, logits_read.at(1))
                first, second = choice[:, 0], choice[:, 1]
                first_of_largest(dve, link, first, scores[:, :, :], core.const["iota"], tmp[:, :, :], top[:, :])
                link(dve.tensor_reduce(best[:, 0, :], scores[:, :, :], AXIS.X, ALU.max))
                link(dve.scalar_tensor_tensor(rest[:, :, :], first, NEG, scores[:, :, :], ALU.mult, ALU.add))
                link(dve.tensor_reduce(best[:, 1, :], rest[:, :, :], AXIS.X, ALU.max))
                first_of_largest(dve, link, second, rest[:, :, :], core.const["iota"], tmp[:, :, :], top[:, :])
                dve.tensor_tensor(gap[:, :], best[:, 1, :], best[:, 0, :], ALU.subtract).then_inc(exp_in.handle, 1)
                dve.wait_ge(exp_out.handle, exp_out.at(1))
                link(dve.tensor_scalar(top[:, :], gap[:, :], 1.0, None, ALU.add))
                link(dve.reciprocal(top[:, :], top[:, :]))
                link(dve.tensor_tensor(tmp[:, :, :], second, spread(gap[:, :], 2, N), ALU.mult))
                link(dve.tensor_tensor(tmp[:, :, :], tmp[:, :, :], first, ALU.add))
                link(dve.tensor_tensor(gates[:, :, :], tmp[:, :, :], spread(top[:, :], 2, N), ALU.mult))
                dve.wait_ge(filled.handle, filled.at(1))
                angles(dve, 0)
                hidden(dve, 0, first=True)
                with dve.Fori(0, UNITS // 2 - 1) as i:
                    for p in range(2):
                        vector_unit(dve, i * 2 + p)
                vector_unit(dve, UNITS - 2)
                accumulate(dve, UNITS - 1)
                scratch = hT[:, 0, :].rearrange("p (t d) -> p t d", t=TILES)
                dve.wait_ge(y_ps.handle, y_ps.at(UNITS * 2 * BATCH))
                link(dve.tensor_tensor(scratch, acc[:, :, :], acc[:, :, :], ALU.mult))
                link(dve.tensor_reduce(mean[:, :], scratch, AXIS.X, ALU.add))
                dve.tensor_scalar(mean[:, :], mean[:, :], 1.0 / D, 1e-6, ALU.mult, ALU.add).then_inc(mean_sq.handle, 1)
                dve.wait_ge(rstd.handle, rstd.at(1))
                link(dve.tensor_tensor(acc[:, :, :], acc[:, :, :], spread(inv_root[:, :], 2, D), ALU.mult))
                link(dve.tensor_tensor(acc[:, :, :], acc[:, :, :], spread(w[:, L3F["norm"]], 1, TILES), ALU.mult))
                link(dve.tensor_tensor(core.x[:, :, :], core.x[:, :, :], acc[:, :, :], ALU.add))
                count[0] = link.count
    norm_close(core)
    per_chunk = UNITS * C
    for s, total in ((logits_ps, 1), (logits_read, 1), (exp_in, 1), (exp_out, 1), (up_in[0], 8 * UNITS), (up_in[1], 8 * UNITS),
                     (down_in[0], 8 * UNITS), (down_in[1], 8 * UNITS), *[(s, per_chunk) for s in (
                         f_ps, m_ps, abs_done, exp_done, ln_done, z_done, u_done, k_done, frac_done, tanh_done,
                         sin_done, h_done)], (y_ps, UNITS * 2 * BATCH), (y_read, UNITS * 2 * BATCH),
                     (chain, count[0]), (filled, 1), (mean_sq, 1), (rstd, 1)):
        s.close(total)


def constants_layout():
    at, layout = 0, {}
    for name, width in (("ident", P), ("mask_q", P), ("mask_k", P), ("keep_k", P), ("iota", 16),
                        ("rope_cos", 256), ("rope_sin", 256), ("rope_half_cos", 256), ("rope_half_sin", 256),
                        ("head_mask8", 16), ("row_mask8", 512), ("head_mask64", 8), ("row_mask64", 512),
                        ("head_mask32", 4), ("row_mask32", 128)):
        layout[name] = slice(at, at + width)
        at += width
    return layout, at


def decoder(nc, x_in, consts, packs, streamed, out):
    with ExitStack() as ctx:
        core = Core(nc, ctx)
        layout, n_consts = constants_layout()
        const = core.sbuf("constants", [P, n_consts], F32)
        core.const = {name: const[:, cols] for name, cols in layout.items()}
        core.ident, core.keep_k = core.const["ident"], core.const["keep_k"]
        core.rope_cos, core.rope_sin = core.const["rope_cos"], core.const["rope_sin"]
        core.rope_half_cos, core.rope_half_sin = core.const["rope_half_cos"], core.const["rope_half_sin"]
        core.ident_bf_t = core.sbuf("ident_bf", [P, P], BF16)
        core.mask_q_t = core.sbuf("mask_q_bf", [P, P], BF16)
        core.mask_k_t = core.sbuf("mask_k_bf", [P, P], BF16)
        core.ident_bf, core.mask_q, core.mask_k = core.ident_bf_t[:, :], core.mask_q_t[:, :], core.mask_k_t[:, :]
        loaded = ctx.enter_context(nc.semaphore("inputs_loaded"))
        made = ctx.enter_context(nc.semaphore("constants_made"))
        w, w_sem = {}, {}
        for name, ap in packs.items():
            w[name] = core.sbuf(f"w_{name}", [ap.shape[0], ap.shape[1]], F32)
            w_sem[name] = ctx.enter_context(nc.semaphore(f"loaded_{name}"))

        with nc.Block() as block:
            @block.sync
            def _(sp):
                sp.dma_start(core.x[:, :, :], x_in.rearrange("b (t p) d -> p (b t) d", p=P)).then_inc(loaded, 16)
                sp.dma_start(const[:, :], consts).then_inc(loaded, 16)
                for name, ap in packs.items():
                    sp.dma_start(w[name][:, :], ap).then_inc(w_sem[name], 16)

            @block.gpsimd
            def _(pool):
                pool.memset(core.minus_half[:, :], -0.5).then_inc(made, 1)
                pool.memset(core.ones[:, :], 1.0).then_inc(made, 1)

            @block.vector
            def _(dve):
                dve.wait_ge(loaded, 32)
                dve.tensor_copy(core.ident_bf, core.ident).then_inc(made, 1)
                dve.tensor_copy(core.mask_q, core.const["mask_q"]).then_inc(made, 1)
                dve.tensor_copy(core.mask_k, core.const["mask_k"]).then_inc(made, 1)
                dve.wait_ge(made, 5)

        core.kbd, core.vbd = {}, {}
        for cfg in CROSS:
            core.kbd[cfg.name] = core.sbuf(f"{cfg.name}_kbd", [P, BATCH, cfg.chunks, cfg.heads_per_chunk * KEYS], F32)
            core.vbd[cfg.name] = core.sbuf(f"{cfg.name}_vbd", [P, BATCH, max(cfg.chunks, cfg.prob_chunks), P], F32)
        prepare_context(core, CROSS, w, w_sem, w["context"], w_sem["context"])

        run_layers(core, w, w_sem, streamed)

        stored = ctx.enter_context(nc.semaphore("output_stored"))
        with nc.Block() as block:
            @block.sync
            def _(sp):
                sp.dma_start(out.rearrange("b (t p) d -> p (b t) d", p=P), core.x[:, :, :]).then_inc(stored, 16)
                sp.wait_ge(stored, 16)
                for name in packs:
                    sp.wait_ge(w_sem[name], 16)


CROSS = [CrossAttention("l0_xattn", 16, 8, True, True), CrossAttention("l1_xattn", 8, 64, False, False),
         CrossAttention("l2_xattn", 4, 32, False, False), CrossAttention("l3_xattn", 16, 8, True, False)]
SELF = [SelfAttention("l0_attn", "silu", True, 1.0, False),
        SelfAttention("l1_attn", "square", True, 1.0 / DH, True),
        SelfAttention("l2_attn", "plain", False, DH ** -0.5, True),
        SelfAttention("l3_attn", "rope", True, DH ** -0.5, False)]


def run_layers(core, w, w_sem, streamed):
    def attend(layer):
        self_attention(core, SELF[layer], w[SELF[layer].name], w_sem[SELF[layer].name])

    def attend_context(layer):
        cross_attention(core, CROSS[layer], w[CROSS[layer].name], w_sem[CROSS[layer].name])

    attend(0)
    attend_context(0)
    expert_feed_forward(core, w["l0_ffn"], w_sem["l0_ffn"], w["l0_ffn_b1"], w_sem["l0_ffn_b1"])
    attend(1)
    attend_context(1)
    gated_experts(core, w["l1_ffn"], w_sem["l1_ffn"], streamed["l1_w1"], streamed["l1_w2"])
    attend(2)
    attend_context(2)
    quantised_feed_forward(core, w["l2_ffn"], w_sem["l2_ffn"])
    attend(3)
    attend_context(3)
    tanh_cos_experts(core, w["l3_ffn"], w_sem["l3_ffn"], streamed["l3_up"], streamed["l3_down"])


def shape_constants():
    import numpy as np
    layout, n = constants_layout()
    c = np.zeros((P, n), np.float32)
    i = np.arange(P)
    c[:, layout["ident"]] = np.eye(P)
    c[:, layout["mask_q"]] = np.where(i[None, :] > i[:, None], NEG, 0.0)
    c[:, layout["mask_k"]] = np.where(i[None, :] < i[:, None], NEG, 0.0)
    c[:, layout["keep_k"]] = i[None, :] >= i[:, None]
    c[:, layout["iota"]] = np.arange(16)
    pos = (np.arange(TPB)[None, :, None] * P + i[:, None, None]).astype(np.float32)
    inv_freq = (1.0 / np.float32(10000.0) ** (np.arange(0, DH, 2, dtype=np.float32) / DH)).astype(np.float32)
    freqs = pos * inv_freq
    sign = np.where(np.arange(DH) % 2 == 0, -1.0, 1.0)
    for name, angles in (("rope_half", np.concatenate([freqs, freqs], -1)), ("rope", np.repeat(freqs, 2, -1))):
        for fn, f in (("cos", np.cos(angles)), ("sin", np.sin(angles) * sign)):
            c[:, layout[f"{name}_{fn}"]] = np.repeat(f[:, :, None, :], SLOTS, 2).reshape(P, -1)
    for dh, heads_per_chunk in ((8, 16), (64, 2), (32, 4)):
        c[:, layout[f"head_mask{dh}"]][:, :heads_per_chunk] = (i[:, None] // dh) == np.arange(heads_per_chunk)[None, :]
        n_cols = layout[f"row_mask{dh}"].stop - layout[f"row_mask{dh}"].start
        cols = np.arange(n_cols)
        if dh == 8:
            head_of_col, row_base = (cols % 128) // 8, 4 * (cols // 128)
        elif dh == 64:
            head_of_col, row_base = cols // 64, 4 * (cols // 256)
        else:
            head_of_col, row_base = cols // 32, 0 * cols
        c[:, layout[f"row_mask{dh}"]] = (i[:, None] // KEYS + row_base[None, :]) == head_of_col[None, :]
    return c


def packed(inputs):
    import numpy as np

    def get(name):
        return np.asarray(inputs[name])

    def rows(vector):
        return np.broadcast_to(vector.reshape(1, -1), (P, vector.size))

    def qkv(q, k, v):
        cols = []
        for g in range(HG):
            cols += [q[:, g * GH * DH:(g + 1) * GH * DH], k[:, g * GH * DH:(g + 1) * GH * DH]]
        return cols + [v]

    packs = {}
    scales = np.concatenate([get("L0_attn_q_scale").reshape(HG, GH), get("L0_attn_k_scale").reshape(HG, GH)], 1)
    packs["l0_attn"] = [*qkv(get("L0_attn_Wq").T, get("L0_attn_Wk").T, get("L0_attn_Wv").T), get("L0_attn_Wo").T,
                        rows(scales)]
    packs["l1_attn"] = [*qkv(get("L1_attn_Wq").T, get("L1_attn_Wk").T, get("L1_attn_Wv").T), get("L1_attn_Wo").T,
                        *[rows(a[0]) for a in qkv(get("L1_attn_bq")[None], get("L1_attn_bk")[None],
                                                  get("L1_attn_bv")[None])],
                        rows(np.tile(get("L1_attn_norm_w"), SLOTS))]
    packs["l2_attn"] = [*qkv(get("L2_attn_Wq"), get("L2_attn_Wk"), get("L2_attn_Wv")), get("L2_attn_Wout")]
    packs["l3_attn"] = [*qkv(get("L3_attn_qw"), get("L3_attn_kw"), get("L3_attn_vw")), get("L3_attn_ow")]
    ctx = get("ctx_768")
    by_layer = {"l0_xattn": ("L0_xattn_", False), "l1_xattn": ("L1_xattn_", False), "l2_xattn": ("L2_xattn_", True),
                "l3_xattn": ("L3_xattn_", False)}
    packs["context"] = [*[ctx[b].T for b in range(BATCH)],
                        *[ctx[b].T for b in range(BATCH) for _ in range(P // KEYS)]]
    for cfg in CROSS:
        prefix, turned = by_layer[cfg.name]
        wq, wk, wv, wo = [get(prefix + n).T if turned else get(prefix + n) for n in ("Wq", "Wk", "Wv", "Wo")]
        packs["context"] += [wk, wv]
        packs[cfg.name] = [wq, wo.reshape(cfg.chunks, P, D).transpose(1, 0, 2).reshape(P, -1), rows(get(prefix + "bo"))]
        if cfg.biased:
            packs[cfg.name] += [get(prefix + "bq").reshape(cfg.chunks, P).T, get(prefix + "bk").reshape(cfg.chunks, P).T,
                                rows(get(prefix + "bv"))]

    def chunked(a):
        return a.reshape(-1, P, a.shape[-1]).transpose(1, 0, 2).reshape(P, -1)

    packs["l0_ffn"] = [get("L0_ffn_W_router"), *list(get("L0_ffn_W1")), chunked(get("L0_ffn_Wo")),
                       *[rows(get("L0_ffn_" + n)) for n in ("bo", "ln_gamma", "ln_beta")]]
    packs["l0_ffn_b1"] = [get("L0_ffn_b1")]
    packs["l1_ffn"] = [get("L1_ffn_router_w"), rows(get("L1_ffn_router_b"))]
    packs["l2_ffn"] = [get("L2_ffn_w_gate").T, get("L2_ffn_w_up").T, chunked(get("L2_ffn_w_down").T)]
    packs["l3_ffn"] = [get("L3_ffn_router_w").T, rows(get("L3_ffn_router_bias")),
                       get("L3_ffn_bank_phase").reshape(-1, P).T, rows(get("L3_ffn_norm_w"))]
    return {name: np.ascontiguousarray(np.concatenate(cols, 1)) for name, cols in packs.items()}


def experts(inputs):
    import numpy as np

    def get(name):
        return np.asarray(inputs[name])

    def chunked(a):
        return a.reshape(a.shape[0], -1, P, a.shape[-1]).transpose(0, 2, 1, 3).reshape(a.shape[0], P, -1)

    arrays = {"l1_w1": get("L1_ffn_w1"), "l1_w2": chunked(get("L1_ffn_w2"))}

    def unit_columns(a):
        return a.reshape(-1, 2, *a.shape[1:]).transpose(0, 2, 1, 3).reshape(a.shape[0] // 2, a.shape[1], -1)

    down = get("L3_ffn_bank_down")
    arrays["l3_up"] = np.concatenate([unit_columns(get("L3_ffn_bank_freq")), unit_columns(get("L3_ffn_bank_mag"))], 2)
    arrays["l3_down"] = chunked(down.reshape(down.shape[0] // 2, -1, D))
    return {name: np.ascontiguousarray(a) for name, a in arrays.items()}


def kernel(**inputs):
    import numpy as np
    import concourse.bacc as bacc
    from concourse.bass_utils import run_bass_kernel_spmd

    nc = bacc.Bacc("TRN2", target_bir_lowering=False, num_devices=1)
    arrays = {"x": np.ascontiguousarray(inputs["x"]), "consts": shape_constants(), **packed(inputs)}
    by_expert = experts(inputs)
    arrays.update(by_expert)
    aps = {name: nc.dram_tensor(f"in_{name}", a.shape, mybir.dt.from_np(a.dtype), kind="ExternalInput").ap()
           for name, a in arrays.items()}
    out = nc.dram_tensor("out", (BATCH, SEQ, D), F32, kind="ExternalOutput").ap()
    x, consts = aps.pop("x"), aps.pop("consts")
    streamed = {name: aps.pop(name) for name in by_expert}
    decoder(nc, x, consts, aps, streamed, out)
    result = run_bass_kernel_spmd(nc, [{f"in_{name}": a for name, a in arrays.items()}], core_ids=[0])
    return result.results[0]["out"]
```

```python
import concourse.bass as bass
from concourse import mybir
from contextlib import ExitStack

F32 = mybir.dt.float32
BF16 = mybir.dt.bfloat16
ACT = mybir.ActivationFunctionType
ALU = mybir.AluOpType
AXIS = mybir.AxisListType

P = 128
BATCH, SEQ, D = 2, 512, 128
TILES = BATCH * SEQ // P
TPB = SEQ // P
BANK = 512
LN_EPS = 1e-5
HEADS, DH = 16, 8
GH = 4
HG = HEADS // GH
GROUPS = BATCH * HG
SLOTS = 2 * GH
PARTS = 6
SHIFT = PARTS * DH
STACK = 64
NEG = -1e30
KEYS, CTX_D = 32, 96
MAGIC = 12582912.0
BIG_INDEX = 1000.0


def spread(ap, axis, n):
    ap = ap.unsqueeze(axis)
    shape = list(ap.shape)
    shape[axis] = n
    return ap.to_broadcast(shape)


class Signal:

    def __init__(self, handle):
        self.handle, self.base = handle, 0

    def at(self, n):
        return n + self.base

    def close(self, total):
        self.base += total


class Chain:

    def __init__(self, engine, signal):
        self.engine, self.paced, self.count = engine, signal, 0

    def __call__(self, instruction):
        instruction.then_inc(self.paced.handle, 1)
        self.count += 1
        self.engine.wait_ge(self.paced.handle, self.paced.at(self.count))


class Core:

    def __init__(self, nc, ctx):
        self.nc, self.ctx = nc, ctx
        self.signals = {}
        self.x = self.sbuf("x_resid", [P, TILES, D], F32)
        self.xn = self.sbuf("x_normed", [P, TILES, D], F32)
        self.xnT = self.sbuf("x_normed_T", [P, TILES * P], F32)
        self.stats = self.sbuf("bn_stats", [P, TILES, 6], F32)
        self.mean_var = self.sbuf("mean_var", [P, TILES, 2], F32)
        self.var_eps = self.sbuf("var_eps", [P, TILES], F32)
        self.rstd = self.sbuf("rstd", [P, TILES], F32)
        self.minus_half = self.sbuf("minus_half", [P, 1], F32)
        self.ones = self.sbuf("ones", [P, P], F32)
        self.psum = ctx.enter_context(nc.psum_tensor("psum", [P, 8, BANK], F32))
        self.bank = [self.psum[:, i, :] for i in range(8)]

    def sbuf(self, name, shape, dt):
        return self.ctx.enter_context(self.nc.sbuf_tensor(name, shape, dt))

    def sig(self, name):
        if name not in self.signals:
            self.signals[name] = Signal(self.ctx.enter_context(self.nc.semaphore(name)))
        return self.signals[name]



def norm_vector(core, dve):
    x, mv = core.x, core.mean_var
    stats, aggr = core.sig("ln_stats"), core.sig("ln_aggr")
    var_eps, rstd, xn = core.sig("ln_var_eps"), core.sig("ln_rstd"), core.sig("ln_xn")
    for half in range(BATCH):
        tiles = range(half * TPB, (half + 1) * TPB)
        part = slice(half * TPB, (half + 1) * TPB)
        for t in tiles:
            dve.bn_stats(core.stats[:, t, :], x[:, t, :]).then_inc(stats.handle, 1)
        for t in tiles:
            dve.wait_ge(stats.handle, stats.at(t + 1))
            dve.bn_aggr(mv[:, t, :], core.stats[:, t, :]).then_inc(aggr.handle, 1)
        dve.wait_ge(aggr.handle, aggr.at((half + 1) * TPB))
        dve.tensor_scalar(core.var_eps[:, part], mv[:, part, 1], LN_EPS, None, ALU.add)\
           .then_inc(var_eps.handle, 1)
    for half in range(BATCH):
        dve.wait_ge(rstd.handle, rstd.at(half + 1))
        for t in range(half * TPB, (half + 1) * TPB):
            dve.tensor_scalar(core.xn[:, t, :], x[:, t, :], mv[:, t, 0:1], core.rstd[:, t:t + 1],
                              ALU.subtract, ALU.mult).then_inc(xn.handle, 1)


def norm_gpsimd(core, pool):
    var_eps, rstd = core.sig("ln_var_eps"), core.sig("ln_rstd")
    for half in range(BATCH):
        part = slice(half * TPB, (half + 1) * TPB)
        pool.wait_ge(var_eps.handle, var_eps.at(half + 1))
        pool.tensor_tensor(core.rstd[:, part], core.var_eps[:, part],
                           core.minus_half[:, 0:1].to_broadcast([P, TPB]), ALU.pow).then_inc(rstd.handle, 1)


def norm_tensor(core, pe):
    xn, xnT_ps = core.sig("ln_xn"), core.sig("ln_xnT_ps")
    for t in range(TILES):
        pe.wait_ge(xn.handle, xn.at(t + 1))
        last = pe.transpose(core.bank[t // TPB][:, (t % TPB) * P:(t % TPB + 1) * P],
                            core.xn[:, t, :], core.ident)
        if t % TPB == TPB - 1:
            last.then_inc(xnT_ps.handle, 1)


def norm_scalar(core, act):
    xnT_ps, xnT = core.sig("ln_xnT_ps"), core.sig("ln_xnT")
    for half in range(BATCH):
        act.wait_ge(xnT_ps.handle, xnT_ps.at(half + 1))
        act.copy(core.xnT[:, half * SEQ:(half + 1) * SEQ], core.bank[half][:, :]).then_inc(xnT.handle, 1)


def norm_close(core):
    for name, total in (("ln_stats", TILES), ("ln_aggr", TILES), ("ln_var_eps", BATCH), ("ln_rstd", BATCH),
                        ("ln_xn", TILES), ("ln_xnT_ps", BATCH), ("ln_xnT", BATCH)):
        core.sig(name).close(total)


class SelfAttention:

    def __init__(self, name, kind, causal, scale, residual_normed):
        self.name, self.kind, self.causal, self.scale = name, kind, causal, scale
        self.residual_normed = residual_normed


W_QKV, W_OUT = slice(0, 384), slice(384, 512)


def self_attention_project(core, cfg, w, w_sem, qk, v):
    nc = core.nc
    sig = core.sig
    proj, evac, norm_in, norm_out = sig("sa_proj"), sig("sa_evac"), sig("sa_norm_in"), sig("sa_norm_out")
    chain = sig("dve_chain")
    xnT = sig("ln_xnT")
    with ExitStack() as ctx:
        def sbuf(name, shape, dt=F32):
            return ctx.enter_context(nc.sbuf_tensor(f"{cfg.name}_{name}", shape, dt))
        scratch = sbuf("scratch", [P, TILES, SLOTS * HG * DH])
        norm2 = sbuf("norm2", [P, GROUPS * TPB, SLOTS])
        norm1 = sbuf("norm1", [P, GROUPS * TPB, SLOTS])
        factor = sbuf("factor", [P, GROUPS * TPB, SLOTS])
        rows = qk[:, :, :, :].rearrange("p g t (s d) -> p (g t) s d", d=DH)
        scratch_rows = scratch[:, :, :].rearrange("p t (a s d) -> p (t a) s d", s=SLOTS, d=DH)
        counts = {}

        def evacuated(t):
            b, tb = divmod(t, TPB)
            groups = slice(b * HG, (b + 1) * HG)
            return qk[:, groups, tb, :], v[:, groups, tb, :]

        def from_bank(t):
            ps = core.bank[2 + t % 4]
            return (ps[:, 0:256].rearrange("p (g c) -> p g c", g=HG),
                    ps[:, 256:384].rearrange("p (g c) -> p g c", g=HG))

        def head_norms(act):
            act.wait_ge(norm_in.handle, norm_in.at(1))
            act.activation(norm1[:, :, :], norm2[:, :, :], ACT.Sqrt).then_inc(norm_out.handle, 1)

        with nc.Block() as block:
            @block.tensor
            def _(pe):
                norm_tensor(core, pe)
                pe.wait_ge(w_sem, 16)
                for t in range(TILES):
                    if t % TPB == 0:
                        pe.wait_ge(xnT.handle, xnT.at(t // TPB + 1))
                    if t >= 4:
                        pe.wait_ge(evac.handle, evac.at(2 * (t - 3)))
                    pe.matmul(core.bank[2 + t % 4][:, 0:384], core.xnT[:, t * P:(t + 1) * P], w[:, W_QKV],
                              start=True, stop=True).then_inc(proj.handle, 1)

            @block.scalar
            def _(act):
                norm_scalar(core, act)
                if cfg.kind == "square":
                    head_norms(act)
                    return
                func = ACT.Silu if cfg.kind == "silu" else ACT.Copy
                for t in range(TILES):
                    act.wait_ge(proj.handle, proj.at(t + 1))
                    for dst, src in zip(evacuated(t), from_bank(t)):
                        act.activation(dst, src, func).then_inc(evac.handle, 1)
                if cfg.kind == "silu":
                    head_norms(act)

            @block.gpsimd
            def _(pool):
                norm_gpsimd(core, pool)

            @block.vector
            def _(dve):
                norm_vector(core, dve)
                link = Chain(dve, chain)
                if cfg.kind == "square":
                    bias = w[:, 512:896]
                    dve.wait_ge(w_sem, 16)
                    for t in range(TILES):
                        dve.wait_ge(proj.handle, proj.at(t + 1))
                        both = (bias[:, 0:256].rearrange("p (g c) -> p g c", g=HG),
                                bias[:, 256:384].rearrange("p (g c) -> p g c", g=HG))
                        for dst, src, add in zip(evacuated(t), from_bank(t), both):
                            dve.tensor_tensor(dst, src, add, ALU.add).then_inc(evac.handle, 1)
                dve.wait_ge(evac.handle, evac.at(2 * TILES))
                if cfg.kind in ("silu", "square"):
                    link(dve.tensor_tensor(scratch_rows, rows, rows, ALU.mult))
                    link(dve.tensor_reduce(factor[:, :, :], scratch_rows, AXIS.X, ALU.add))
                    if cfg.kind == "silu":
                        dve.tensor_scalar(norm2[:, :, :], factor[:, :, :], 1e-34, None, ALU.max)\
                           .then_inc(norm_in.handle, 1)
                        dve.wait_ge(norm_out.handle, norm_out.at(1))
                        link(dve.tensor_scalar(norm2[:, :, :], norm1[:, :, :], 1e-6, None, ALU.add))
                        link(dve.reciprocal(factor[:, :, :], norm2[:, :, :]))
                        link(dve.tensor_tensor(factor[:, :, :], factor[:, :, :], norm1[:, :, :], ALU.mult))
                        scales = w[:, 512:512 + HG * SLOTS].rearrange("p (g s) -> p g s", g=HG)
                        for b in range(BATCH):
                            at = factor[:, b * HG * TPB:(b + 1) * HG * TPB, :]\
                                .rearrange("p (g t) s -> p g t s", t=TPB)
                            link(dve.tensor_tensor(at, at, spread(scales, 2, TPB), ALU.mult))
                    else:
                        dve.tensor_scalar(norm2[:, :, :], factor[:, :, :], 1.0 / DH, 2.0 ** -23,
                                          ALU.mult, ALU.add).then_inc(norm_in.handle, 1)
                        dve.wait_ge(norm_out.handle, norm_out.at(1))
                        link(dve.reciprocal(factor[:, :, :], norm1[:, :, :]))
                        link(dve.tensor_tensor(norm1[:, :, :], factor[:, :, :], factor[:, :, :], ALU.mult))
                        link(dve.tensor_tensor(norm1[:, :, :], norm1[:, :, :], norm2[:, :, :], ALU.mult))
                        link(dve.tensor_scalar(norm1[:, :, :], norm1[:, :, :], -0.5, 1.5, ALU.mult, ALU.add))
                        link(dve.tensor_tensor(factor[:, :, :], factor[:, :, :], norm1[:, :, :], ALU.mult))
                    link(dve.tensor_tensor(rows, rows, spread(factor[:, :, :], 3, DH), ALU.mult))
                if cfg.kind == "square":
                    per_token = qk[:, :, :, :].rearrange("p g t c -> p (g t) c")
                    link(dve.tensor_tensor(per_token, per_token,
                                           spread(w[:, 896:960], 1, GROUPS * TPB), ALU.mult))
                if cfg.kind in ("square", "rope"):
                    cos, sin = (core.rope_cos, core.rope_sin) if cfg.kind == "rope" \
                        else (core.rope_half_cos, core.rope_half_sin)
                    wide = qk[:, :, :, :].rearrange("p g t c -> p g (t c)")
                    turned = scratch[:, :, :]
                    link(dve.tensor_tensor(turned[:, :, 0::2], wide[:, :, 1::2],
                                           spread(sin[:, 0::2], 1, GROUPS), ALU.mult))
                    link(dve.tensor_tensor(turned[:, :, 1::2], wide[:, :, 0::2],
                                           spread(sin[:, 1::2], 1, GROUPS), ALU.mult))
                    link(dve.tensor_tensor(wide, wide, spread(cos, 1, GROUPS), ALU.mult))
                    link(dve.tensor_tensor(wide, wide, turned, ALU.add))
                counts["chain"] = link.count
    norm_close(core)
    proj.close(TILES)
    evac.close(2 * TILES)
    if cfg.kind in ("silu", "square"):
        norm_in.close(1)
        norm_out.close(1)
    chain.close(counts["chain"])


def self_attention_heads(core, cfg, qk, v, attn):
    nc, sig = core.nc, core.sig
    softmax = cfg.kind != "square"
    stack_k, stack_q, k_ps, q_ps = sig("sa_stack_k"), sig("sa_stack_q"), sig("sa_k_ps"), sig("sa_q_ps")
    k_ready, q_ready = sig("sa_k"), sig("sa_q")
    s_done, max_done, shift = sig("sa_scores"), sig("sa_max"), sig("sa_shift")
    q2_ps, q2_ready, st_done = sig("sa_q2_ps"), sig("sa_q2"), sig("sa_scores_T")
    exp_done, masked, pv_done = sig("sa_exp"), sig("sa_masked"), sig("sa_pv")
    o_copied, o_ps, o_done = sig("sa_o_copied"), sig("sa_o_ps"), sig("sa_o_done")
    pool_chain, dve_chain, filled, zeroed = sig("pool_chain"), sig("dve_chain"), sig("sa_filled"), sig("sa_zeroed")
    inv_done, v_ready = sig("sa_inv"), sig("sa_v")
    first_k, first_q = sig("sa_first_stack_k"), sig("sa_first_stack_q")
    CHAINED, SHIFT_CHAINED = 4, 3
    U = 2 * TPB
    S = 11 if cfg.causal else 16
    Q_READY = PARTS + (1 if softmax else 0)
    LAST = GROUPS - 1

    with ExitStack() as ctx:
        def sbuf(name, shape, dt=F32):
            return ctx.enter_context(nc.sbuf_tensor(f"{cfg.name}_{name}", shape, dt))
        stack = [sbuf(f"stack{i}", [P, TPB, SLOTS, STACK], BF16) for i in range(2)]
        parts = sbuf("parts", [P, 3, TPB, SLOTS, DH], BF16)
        rest = sbuf("rest", [P, TPB, SLOTS, DH])
        first_parts = sbuf("first_parts", [P, 3, TPB, SLOTS, DH], BF16)
        first_rest = sbuf("first_rest", [P, TPB, SLOTS, DH])
        v_now = [sbuf(f"v_now{i}", [P, TPB, GH, 32]) for i in range(2)]
        kT = [sbuf(f"kT{i}", [P, 2, 2, SEQ], BF16) for i in range(2)]
        qT = [sbuf(f"qT{i}", [P, 2, SEQ], BF16) for i in range(2)]
        q2T = [sbuf(f"q2T{i}", [P, 2, SEQ], BF16) for i in range(2)]
        maxes = sbuf("maxes", [P, TPB, GH])
        shift_rest = sbuf("shift_rest", [P, TPB, GH])
        probs = [sbuf(f"probs{i}", [P, GH, SEQ]) for i in range(2)]
        oT = sbuf("oT", [P, SEQ])
        inv = sbuf("inv", [P, TPB, GH])

        def score_steps():
            steps = []
            for qt in range(TPB):
                width = (qt + 1) * P if cfg.causal else SEQ
                heads = 1 if width > BANK // 2 else GH if width == P else 2
                steps += [(qt, h, heads, width) for h in range(0, GH, heads)]
            return steps

        def first_query(kt):
            return kt * P if cfg.causal else 0

        def steps_at(u):
            return range(u * S // U, (u + 1) * S // U)

        def transposed(bank):
            return core.bank[bank][:, :].bitcast(BF16).rearrange("p (a s) -> p a s", a=2)

        def wait_alone(pool, signal, n):
            pool.wait_ge(signal.handle, signal.at(n))
            pool.sem_inc(core.sig("pool_paced").handle, 1)

        def split(engine, link, g, parts, rest):
            src = qk[:, bass.ds(g, 1), :, :].rearrange("p o t (s d) -> p (o t) s d", d=DH)
            h, m, lo = parts[:, 0], parts[:, 1], parts[:, 2]
            link(engine.tensor_copy(h, src))
            link(engine.tensor_tensor(rest[:, :, :, :], src, h, ALU.subtract))
            link(engine.tensor_copy(m, rest[:, :, :, :]))
            link(engine.tensor_tensor(lo, rest[:, :, :, :], m, ALU.subtract))

        def stack_keys(engine, p, parts, done):
            h, m, lo = parts[:, 0], parts[:, 1], parts[:, 2]
            for i, part in enumerate((h, h, h, m, m, lo)):
                engine.tensor_copy(stack[p][:, :, GH:SLOTS, i * DH:(i + 1) * DH], part[:, :, GH:SLOTS, :])\
                      .then_inc(done.handle, 1)

        def stack_queries(engine, p, parts, done):
            h, m, lo = parts[:, 0], parts[:, 1], parts[:, 2]
            if softmax:
                engine.memset(stack[p][:, :, 0:GH, SHIFT:SHIFT + 3], 0.0).then_inc(done.handle, 1)
            for i, part in enumerate((h, m, lo, h, m, h)):
                engine.tensor_copy(stack[p][:, :, 0:GH, i * DH:(i + 1) * DH], part[:, :, 0:GH, :])\
                      .then_inc(done.handle, 1)

        def take_v(pool, g, p):
            if not (isinstance(g, int) and g < 2):
                wait_alone(pool, pv_done, (g - 1) * TPB)
            pool.tensor_copy(v_now[p][:, :, :, 0:DH],
                             v[:, bass.ds(g, 1), :, :].rearrange("p o t (h d) -> p (o t) h d", d=DH))\
                .then_inc(v_ready.handle, 1)

        def make_stack(pool, g, p):
            steps = [(g - 1) * CHAINED]

            def link(instruction):
                instruction.then_inc(pool_chain.handle, 1)
                steps[0] += 1
                wait_alone(pool, pool_chain, steps[0])
            later = not (isinstance(g, int) and g == 1)
            if later:
                wait_alone(pool, stack_q, (g - 1) * Q_READY)
            split(pool, link, g, parts, rest)
            if later:
                wait_alone(pool, k_ps, g - 1)
            stack_keys(pool, p, parts, stack_k)
            take_v(pool, g - 1, 1 - p)
            if later:
                wait_alone(pool, q2_ps if softmax else q_ps, g - 1)
            stack_queries(pool, p, parts, stack_q)

        def transpose_stacks(pe, bank, p, slot, done):
            for pair in range(2):
                for t in range(TPB):
                    last = pe.transpose(transposed(bank)[:, pair, t * P:(t + 1) * P],
                                        stack[p][:, t, slot + 2 * pair:slot + 2 * pair + 2, :], core.ident_bf)
            last.then_inc(done.handle, 1)

        def keys_T(pe, g, p, bank_used, n):
            if bank_used is None and isinstance(g, int) and g == 0:
                pe.wait_ge(first_k.handle, first_k.at(PARTS))
            else:
                pe.wait_ge(stack_k.handle, stack_k.at(g * PARTS))
            if bank_used is not None:
                pe.wait_ge(bank_used.handle, bank_used.at(n))
            transpose_stacks(pe, 7, p, GH, k_ps)

        def queries_T(pe, g, p, start=False):
            if start:
                pe.wait_ge(first_q.handle, first_q.at(Q_READY))
            else:
                pe.wait_ge(stack_q.handle, stack_q.at(g * Q_READY))
                if softmax:
                    pe.wait_ge(max_done.handle, max_done.at(g * S - (S + 1) % 2))
                else:
                    pe.wait_ge(q_ready.handle, q_ready.at(g))
            transpose_stacks(pe, 0, p, 0, q_ps)

        def shifted_T(pe, g, p):
            pe.wait_ge(shift.handle, shift.at(g + 1))
            transpose_stacks(pe, 1, p, 0, q2_ps)

        def scores(pe, g, p, i, first=False):
            qt, first_head, heads, width = score_steps()[i]
            if i == 0:
                pe.wait_ge(k_ready.handle, k_ready.at(2 * (g + 1)))
                pe.wait_ge(q_ready.handle, q_ready.at(g + 1))
            if not (first and i < 2):
                pe.wait_ge(max_done.handle, max_done.at(g * S + i - 1))
            for n in range(heads):
                h = first_head + n
                out = core.bank[i % 2][:, n * width:(n + 1) * width]
                last = pe.matmul(out, qT[p][:, h // 2, qt * P:(qt + 1) * P], kT[p][:, h % 2, h // 2, 0:width],
                                 start=True, stop=not cfg.causal)
                if cfg.causal:
                    last = pe.matmul(out[:, width - P:width], core.ident_bf, core.mask_q, start=False, stop=True)
            last.then_inc(s_done.handle, 1)

        def scores_T(pe, g, p, u, first):
            kt, pair = divmod(u, 2)
            if u == 0:
                if softmax:
                    pe.wait_ge(q2_ready.handle, q2_ready.at(g + 1))
                else:
                    pe.wait_ge(k_ready.handle, k_ready.at(2 * (g + 1)))
                    pe.wait_ge(q_ready.handle, q_ready.at(g + 1))
            if not (first and u < 2):
                pe.wait_ge(exp_done.handle, exp_done.at(g * U + u - 1))
            q_from = first_query(kt)
            for half in range(2):
                src = q2T[p] if softmax else qT[p]
                out = core.bank[2 + 2 * (u % 2) + half]
                masked_here = cfg.causal and softmax
                last = pe.matmul(out[:, 0:SEQ - q_from], kT[p][:, half, pair, kt * P:(kt + 1) * P],
                                 src[:, pair, q_from:SEQ], start=True, stop=not masked_here)
                if masked_here:
                    last = pe.matmul(out[:, 0:P], core.ident_bf, core.mask_k, start=False, stop=True)
            last.then_inc(st_done.handle, 1)

        def values(pe, g, p, kt, first):
            if softmax:
                pe.wait_ge(exp_done.handle, exp_done.at(g * U + 2 * kt + 2))
            else:
                pe.wait_ge(masked.handle, masked.at(g * U + 2 * kt + 2))
            if kt == 0:
                pe.wait_ge(v_ready.handle, v_ready.at(g + 1))
            if kt == 0 and not first:
                pe.wait_ge(o_copied.handle, o_copied.at(g))
            q_from = first_query(kt)
            for h in range(GH):
                last = pe.matmul(core.bank[6][32 * h:32 * h + 32, q_from:SEQ], v_now[p][:, kt, h, :],
                                 probs[kt % 2][:, h, q_from:SEQ], start=kt == 0, stop=kt == TPB - 1,
                                 tile_position=(0, 32 * h))
            last.then_inc(pv_done.handle, 1)

        def output_T(pe, g, bank_used=None, n=0):
            pe.wait_ge(o_copied.handle, o_copied.at(g + 1))
            if bank_used is not None:
                pe.wait_ge(bank_used.handle, bank_used.at(n))
            for t in range(TPB):
                last = pe.transpose(core.bank[7][:, t * P:(t + 1) * P], oT[:, t * P:(t + 1) * P], core.ident)
            last.then_inc(o_ps.handle, 1)

        def tensor_group(pe, g, p, last_but=9, first=False):
            for u in range(U):
                scores_T(pe, g, p, u, first)
                if softmax and last_but >= 1:
                    for i in steps_at(u):
                        scores(pe, g + 1, 1 - p, i)
                if u == 3 and not first:
                    if softmax and last_but >= 1:
                        output_T(pe, g - 1)
                    elif last_but >= 1:
                        output_T(pe, g - 1, k_ready, 2 * (g + 2))
                    else:
                        output_T(pe, g - 1, o_done, g - 1)
                if u == U - 1 and last_but >= 2:
                    if not first:
                        keys_T(pe, g + 2, p, o_done, g)
                    else:
                        keys_T(pe, g + 2, p, k_ready, 4)
                if u % 2 == 1 and u > 1:
                    values(pe, g, p, u // 2 - 1, first)
            values(pe, g, p, TPB - 1, first)
            if last_but >= 2:
                queries_T(pe, g + 2, p)
            if softmax and last_but >= 1:
                shifted_T(pe, g + 1, 1 - p)

        def weights(act, g, u):
            kt, pair = divmod(u, 2)
            act.wait_ge(st_done.handle, st_done.at(g * U + u + 1))
            if not (isinstance(g, int) and g == 0 and kt < 2):
                act.wait_ge(pv_done.handle, pv_done.at(g * TPB + kt - 1))
            q_from = first_query(kt)
            width = SEQ - q_from
            b0 = 2 + 2 * (u % 2)
            src = core.psum[:, b0:b0 + 2, 0:width]
            act.activation(probs[kt % 2][:, 2 * pair:2 * pair + 2, q_from:SEQ], src,
                           ACT.Exp if softmax else ACT.Square, scale=cfg.scale).then_inc(exp_done.handle, 1)

        def copy_keys(act, g, p):
            act.wait_ge(k_ps.handle, k_ps.at(g + 1))
            for half in range(2):
                rows = slice(half * STACK, (half + 1) * STACK)
                act.copy(kT[p][rows, half, :, :], transposed(7)[rows, :, :]).then_inc(k_ready.handle, 1)

        def copy_queries(act, g, p):
            act.wait_ge(q_ps.handle, q_ps.at(g + 1))
            act.copy(qT[p][:, :, :], transposed(0)).then_inc(q_ready.handle, 1)

        def scalar_group(act, g, p, last_but=9):
            for u in range(U):
                weights(act, g, u)
            if last_but >= 2:
                copy_keys(act, g + 2, p)
            act.wait_ge(pv_done.handle, pv_done.at((g + 1) * TPB))
            act.copy(oT[:, :], core.bank[6][:, :]).then_inc(o_copied.handle, 1)
            if last_but >= 2:
                copy_queries(act, g + 2, p)

        def maxima(dve, g, i):
            qt, h, heads, width = score_steps()[i]
            dve.wait_ge(s_done.handle, s_done.at(g * S + i + 1))
            dve.tensor_reduce(maxes[:, qt, h:h + heads],
                              core.bank[i % 2][:, 0:heads * width].rearrange("p (h w) -> p h w", h=heads),
                              AXIS.X, ALU.max).then_inc(max_done.handle, 1)

        def make_shift(dve, g, p):
            link = Chain(dve, dve_chain)
            link.count = CHAINED + g * SHIFT_CHAINED
            dve.wait_ge(max_done.handle, max_done.at((g + 1) * S))
            high, mid, low = [stack[p][:, :, 0:GH, SHIFT + i] for i in range(3)]
            link(dve.tensor_scalar(high, maxes[:, :, :], -1.0, None, ALU.mult))
            link(dve.scalar_tensor_tensor(shift_rest[:, :, :], maxes[:, :, :], -1.0, high, ALU.mult, ALU.subtract))
            link(dve.tensor_copy(mid, shift_rest[:, :, :]))
            dve.tensor_tensor(low, shift_rest[:, :, :], mid, ALU.subtract).then_inc(shift.handle, 1)

        def copy_shifted(dve, g, p):
            dve.wait_ge(q2_ps.handle, q2_ps.at(g + 1))
            dve.tensor_copy(q2T[p][:, :, :], transposed(1)).then_inc(q2_ready.handle, 1)

        def finish(dve, g):
            dve.wait_ge(o_ps.handle, o_ps.at(g + 1))
            out = core.bank[7][:, :].rearrange("p (t h c) -> p t h c", t=TPB, h=GH)
            start = g % HG + (g // HG) * (HG * TPB)
            dst = attn[:, bass.ds(start, TPB, HG), :].rearrange("p t (h d) -> p t h d", d=DH)
            if softmax:
                dve.reciprocal(inv[:, :, :], out[:, :, :, DH]).then_inc(inv_done.handle, 1)
                dve.wait_ge(inv_done.handle, inv_done.at(g + 1))
                dve.tensor_tensor(dst, out[:, :, :, 0:DH], spread(inv[:, :, :], 3, DH), ALU.mult)\
                   .then_inc(o_done.handle, 1)
            else:
                dve.tensor_copy(dst, out[:, :, :, 0:DH]).then_inc(o_done.handle, 1)

        def mask_squares(dve, g, u):
            kt, pair = divmod(u, 2)
            dve.wait_ge(exp_done.handle, exp_done.at(g * U + u + 1))
            at = probs[kt % 2][:, 2 * pair:2 * pair + 2, kt * P:(kt + 1) * P]
            dve.tensor_tensor(at, at, spread(core.keep_k, 1, 2), ALU.mult).then_inc(masked.handle, 1)

        def vector_group(dve, g, p, last_but=9, first=False):
            for u in range(U):
                if not softmax:
                    mask_squares(dve, g, u)
                elif last_but >= 1:
                    for i in steps_at(u):
                        maxima(dve, g + 1, i)
                if u == 4 and not first:
                    finish(dve, g - 1)
            if softmax and last_but >= 1:
                make_shift(dve, g + 1, 1 - p)
                copy_shifted(dve, g + 1, 1 - p)

        with nc.Block() as block:
            @block.gpsimd
            def _(pool):
                for p in range(2):
                    pool.memset(stack[p][:, :, :, SHIFT:STACK], 0.0).then_inc(filled.handle, 1)
                    pool.memset(v_now[p][:, :, :, DH:32], 0.0).then_inc(filled.handle, 1)
                pool.wait_ge(filled.handle, filled.at(4))
                for p in range(2):
                    pool.memset(stack[p][:, :, GH:SLOTS, SHIFT:SHIFT + 3], 1.0).then_inc(filled.handle, 1)
                    pool.memset(v_now[p][:, :, :, DH:DH + 1], 1.0).then_inc(filled.handle, 1)
                pool.wait_ge(filled.handle, filled.at(8))
                make_stack(pool, 1, 1)
                make_stack(pool, 2, 0)
                with pool.Fori(1, GROUPS // 2 - 1) as i:
                    make_stack(pool, i * 2 + 1, 1)
                    make_stack(pool, i * 2 + 2, 0)
                make_stack(pool, LAST, 1)
                take_v(pool, LAST, 1)

            @block.tensor
            def _(pe):
                pe.wait_ge(filled.handle, filled.at(8))
                keys_T(pe, 0, 0, None, 0)
                queries_T(pe, 0, 0, start=True)
                if softmax:
                    pe.wait_ge(zeroed.handle, zeroed.at(4))
                    for i in range(S):
                        scores(pe, 0, 0, i, True)
                keys_T(pe, 1, 1, k_ready, 2)
                queries_T(pe, 1, 1)
                if softmax:
                    shifted_T(pe, 0, 0)
                else:
                    pe.wait_ge(zeroed.handle, zeroed.at(4))
                tensor_group(pe, 0, 0, first=True)
                tensor_group(pe, 1, 1)
                with pe.Fori(1, GROUPS // 2 - 1) as i:
                    for p in range(2):
                        tensor_group(pe, i * 2 + p, p)
                tensor_group(pe, LAST - 1, 0, 1)
                tensor_group(pe, LAST, 1, 0)
                output_T(pe, LAST, o_done, LAST)

            @block.scalar
            def _(act):
                for g in range(2):
                    copy_keys(act, g, g)
                    copy_queries(act, g, g)
                scalar_group(act, 0, 0)
                scalar_group(act, 1, 1)
                with act.Fori(1, GROUPS // 2 - 1) as i:
                    for p in range(2):
                        scalar_group(act, i * 2 + p, p)
                scalar_group(act, LAST - 1, 0, 1)
                scalar_group(act, LAST, 1, 0)

            @block.vector
            def _(dve):
                link = Chain(dve, dve_chain)
                split(dve, link, 0, first_parts, first_rest)
                dve.wait_ge(filled.handle, filled.at(8))
                stack_keys(dve, 0, first_parts, first_k)
                stack_queries(dve, 0, first_parts, first_q)
                for p in range(2):
                    for half in range(2):
                        other = slice((1 - half) * STACK, (2 - half) * STACK)
                        dve.memset(kT[p][other, half, :, :], 0.0).then_inc(zeroed.handle, 1)
                if softmax:
                    for i in range(S):
                        maxima(dve, 0, i)
                    make_shift(dve, 0, 0)
                    copy_shifted(dve, 0, 0)
                vector_group(dve, 0, 0, first=True)
                vector_group(dve, 1, 1)
                with dve.Fori(1, GROUPS // 2 - 1) as i:
                    for p in range(2):
                        vector_group(dve, i * 2 + p, p)
                vector_group(dve, LAST - 1, 0, 1)
                vector_group(dve, LAST, 1, 0)
                finish(dve, LAST)

    for s, total in ((stack_k, LAST * PARTS), (stack_q, LAST * Q_READY), (first_k, PARTS), (first_q, Q_READY), (k_ps, GROUPS), (q_ps, GROUPS),
                     (k_ready, 2 * GROUPS), (q_ready, GROUPS), (st_done, GROUPS * U), (exp_done, GROUPS * U),
                     (pv_done, GROUPS * TPB), (o_copied, GROUPS), (o_ps, GROUPS), (o_done, GROUPS),
                     (v_ready, GROUPS), (filled, 8), (zeroed, 4), (pool_chain, LAST * CHAINED)):
        s.close(total)
    if softmax:
        for s, total in ((s_done, GROUPS * S), (max_done, GROUPS * S), (shift, GROUPS), (q2_ps, GROUPS),
                         (q2_ready, GROUPS), (inv_done, GROUPS)):
            s.close(total)
    else:
        masked.close(GROUPS * U)
    dve_chain.close(CHAINED + (GROUPS * SHIFT_CHAINED if softmax else 0))


def self_attention_out(core, cfg, w, attn):
    nc, sig = core.nc, core.sig
    ps, attnT_ready, done, added = sig("so_ps"), sig("so_attnT"), sig("so_done"), sig("so_added")
    with nc.sbuf_tensor(f"{cfg.name}_attnT", [P, TILES * P], F32) as attnT, nc.Block() as block:
        @block.tensor
        def _(pe):
            for b in range(BATCH):
                for t in range(TPB):
                    last = pe.transpose(core.bank[b][:, t * P:(t + 1) * P],
                                        attn[:, (b * TPB + t) * HG:(b * TPB + t + 1) * HG, :],
                                        core.ident)
                last.then_inc(ps.handle, 1)
            for b in range(BATCH):
                pe.wait_ge(attnT_ready.handle, attnT_ready.at(b + 1))
                for t in range(TPB):
                    at = (b * TPB + t) * P
                    last = pe.matmul(core.bank[2 + b][:, t * P:(t + 1) * P], attnT[:, at:at + P], w[:, W_OUT],
                                     start=True, stop=True)
                last.then_inc(done.handle, 1)

        @block.scalar
        def _(act):
            for b in range(BATCH):
                act.wait_ge(ps.handle, ps.at(b + 1))
                act.copy(attnT[:, b * SEQ:(b + 1) * SEQ], core.bank[b][:, :]).then_inc(attnT_ready.handle, 1)

        @block.vector
        def _(dve):
            if cfg.residual_normed:
                dve.tensor_tensor(core.x[:, :, :], core.x[:, :, :], core.xn[:, :, :], ALU.add)\
                   .then_inc(added.handle, 1)
                dve.wait_ge(added.handle, added.at(1))
            for b in range(BATCH):
                dve.wait_ge(done.handle, done.at(b + 1))
                xb = core.x[:, b * TPB:(b + 1) * TPB, :]
                dve.tensor_tensor(xb, xb, core.bank[2 + b][:, :].rearrange("p (t d) -> p t d", t=TPB),
                                  ALU.add).then_inc(added.handle, 1)
    ps.close(BATCH)
    attnT_ready.close(BATCH)
    done.close(BATCH)
    added.close(BATCH + (1 if cfg.residual_normed else 0))


def self_attention(core, cfg, w, w_sem):
    with core.nc.sbuf_tensor(f"{cfg.name}_qk", [P, GROUPS, TPB, SLOTS * DH], F32) as qk, \
            core.nc.sbuf_tensor(f"{cfg.name}_v", [P, GROUPS, TPB, GH * DH], F32) as v, \
            core.nc.sbuf_tensor(f"{cfg.name}_attn", [P, TILES * HG, GH * DH], F32) as attn:
        self_attention_project(core, cfg, w, w_sem, qk, v)
        self_attention_heads(core, cfg, qk, v, attn)
        self_attention_out(core, cfg, w, attn)


class CrossAttention:

    def __init__(self, name, heads, dh, biased, guarded):
        self.name, self.heads, self.dh, self.biased, self.guarded = name, heads, dh, biased, guarded
        self.inner = heads * dh
        self.chunks = self.inner // P
        self.heads_per_chunk = P // dh
        self.prob_chunks = heads * KEYS // P
        self.scale = dh ** -0.5
        at, self.cols = 0, {}
        for part, width in (("wq", self.inner), ("wo", self.inner), ("bo", D), ("bq", self.chunks),
                            ("bk", self.chunks), ("bv", self.inner)):
            if part in ("bq", "bk", "bv") and not biased:
                continue
            self.cols[part] = slice(at, at + width)
            at += width

    def prob_chunks_of(self, c):
        if self.chunks == 1:
            return range(self.prob_chunks)
        return [c * self.heads_per_chunk // (P // KEYS)]

    def v_block(self, c, pk):
        return pk if self.chunks == 1 else c


def prepare_context(core, cfgs, w, w_sem, ctx_w, ctx_sem):
    nc, sig = core.nc, core.sig
    k_done, v_done, chain = sig("cx_k"), sig("cx_v"), sig("dve_chain")
    ctxT, ctx4 = ctx_w[:, 0:BATCH * KEYS], ctx_w[:, BATCH * KEYS:BATCH * KEYS + BATCH * P]
    at = BATCH * KEYS + BATCH * P
    wk, wv = {}, {}
    for cfg in cfgs:
        wk[cfg.name] = ctx_w[:, at:at + cfg.inner]
        wv[cfg.name] = ctx_w[:, at + cfg.inner:at + 2 * cfg.inner]
        at += 2 * cfg.inner
    k_ps, v_ps, k_at, v_at = {}, {}, 0, 0
    for cfg in cfgs:
        k_ps[cfg.name] = core.bank[0][:, k_at:k_at + cfg.chunks * BATCH * KEYS]
        k_at += cfg.chunks * BATCH * KEYS
        for b in range(BATCH):
            v_ps[cfg.name, b] = core.bank[3 + b][:, :] if cfg.inner == BANK \
                else core.bank[1 + b][:, v_at:v_at + cfg.inner]
        v_at += 0 if cfg.inner == BANK else cfg.inner
    with nc.sbuf_tensor("cx_k_rows", [P, 4, BATCH * KEYS], F32) as k_rows, \
            nc.sbuf_tensor("cx_v_rows", [P, BANK], F32) as v_rows, nc.Block() as block:
        count = [0]

        @block.tensor
        def _(pe):
            pe.wait_ge(ctx_sem, 16)
            for cfg in cfgs:
                for c in range(cfg.chunks):
                    last = pe.matmul(k_ps[cfg.name][:, c * BATCH * KEYS:(c + 1) * BATCH * KEYS],
                                     wk[cfg.name][:, c * P:(c + 1) * P], ctxT, start=True, stop=True)
                last.then_inc(k_done.handle, 1)
                for b in range(BATCH):
                    last = pe.matmul(v_ps[cfg.name, b], ctx4[:, b * P:(b + 1) * P], wv[cfg.name],
                                     start=True, stop=True)
                last.then_inc(v_done.handle, 1)

        @block.vector
        def _(dve):
            link = Chain(dve, chain)
            for n, cfg in enumerate(cfgs):
                hc, dh = cfg.heads_per_chunk, cfg.dh
                kbd, vbd = core.kbd[cfg.name], core.vbd[cfg.name]
                pack, cols = w[cfg.name], cfg.cols
                dve.wait_ge(k_done.handle, k_done.at(len(cfgs)))
                dve.wait_ge(w_sem[cfg.name], 16)
                for c in range(cfg.chunks):
                    src = k_ps[cfg.name][:, c * BATCH * KEYS:(c + 1) * BATCH * KEYS]
                    if cfg.biased:
                        bk = pack[:, cols["bk"].start + c:cols["bk"].start + c + 1]
                        link(dve.tensor_scalar(k_rows[:, c, :], src, bk, cfg.scale, ALU.add, ALU.mult))
                    else:
                        link(dve.tensor_scalar(k_rows[:, c, :], src, cfg.scale, None, ALU.mult))
                    for b in range(BATCH):
                        link(dve.tensor_tensor(kbd[:, b, c, :].rearrange("p (h k) -> p h k", h=hc),
                                               spread(k_rows[:, c, b * KEYS:(b + 1) * KEYS], 1, hc),
                                               spread(core.const[f"head_mask{dh}"][:, 0:hc], 2, KEYS), ALU.mult))
                dve.wait_ge(v_done.handle, v_done.at(len(cfgs)))
                for b in range(BATCH):
                    src = v_ps[cfg.name, b]
                    if cfg.biased:
                        link(dve.tensor_tensor(v_rows[:, 0:cfg.inner], src, pack[:, cols["bv"]], ALU.add))
                    else:
                        link(dve.tensor_copy(v_rows[:, 0:cfg.inner], src))
                    mask = core.const[f"row_mask{dh}"].rearrange("p (a c) -> p a c", c=P)
                    rows = spread(v_rows[:, 0:P], 1, cfg.prob_chunks) if cfg.chunks == 1 \
                        else v_rows[:, :].rearrange("p (a c) -> p a c", c=P)
                    link(dve.tensor_tensor(vbd[:, b, :, :], rows, mask, ALU.mult))
            count[0] = link.count
    k_done.close(len(cfgs))
    v_done.close(len(cfgs))
    chain.close(count[0])


def cross_attention(core, cfg, w, w_sem):
    nc, sig = core.nc, core.sig
    H, C, PK = cfg.heads, cfg.chunks, cfg.prob_chunks
    q_ps, q_ready, s_ps, minus_max = sig("xa_q_ps"), sig("xa_q"), sig("xa_scores"), sig("xa_minus_max")
    exp_done, prob, pT_ps, pT_ready = sig("xa_exp"), sig("xa_prob"), sig("xa_pT_ps"), sig("xa_pT")
    o_ps, o_ready, out_ps, chain = sig("xa_o_ps"), sig("xa_o"), sig("xa_out_ps"), sig("dve_chain")
    nan_in, nan_ps, xnT = sig("xa_nan_in"), sig("xa_nan_ps"), sig("ln_xnT")
    kbd, vbd, cols = core.kbd[cfg.name], core.vbd[cfg.name], cfg.cols
    WIDTH = H * KEYS
    count = [0]
    with ExitStack() as ctx:
        def sbuf(name, shape, dt=F32):
            return ctx.enter_context(nc.sbuf_tensor(f"{cfg.name}_{name}", shape, dt))
        qT = sbuf("qT", [P, C, TILES * P])
        clipped = sbuf("clipped", [P, 2, WIDTH])
        top = sbuf("top", [P, TILES, H])
        probs = sbuf("probs", [P, TILES, H, KEYS])
        sums = sbuf("sums", [P, TILES, H])
        inv = sbuf("inv", [P, TILES, H])
        pT = sbuf("pT", [P, PK, TILES * P])
        oT = sbuf("oT", [P, C, TILES * P])
        odd = sbuf("odd", [P, TILES * H])
        odd_rows = sbuf("odd_rows", [P, 1])
        flag = sbuf("flag", [P, 1])
        share = sbuf("share", [P, 1])

        with nc.Block() as block:
            @block.tensor
            def _(pe):
                norm_tensor(core, pe)
                pe.wait_ge(w_sem, 16)
                for half in range(BATCH):
                    pe.wait_ge(xnT.handle, xnT.at(half + 1))
                    for c in range(C):
                        n = half * C + c
                        if n >= 4:
                            pe.wait_ge(q_ready.handle, q_ready.at(n - 3))
                        pe.matmul(core.bank[2 + n % 4], w[:, cols["wq"]][:, c * P:(c + 1) * P],
                                  core.xnT[:, half * SEQ:(half + 1) * SEQ], start=True, stop=True)\
                          .then_inc(q_ps.handle, 1)
                for t in range(TILES):
                    b = t // TPB
                    pe.wait_ge(q_ready.handle, q_ready.at((b + 1) * C))
                    if t >= 2:
                        pe.wait_ge(minus_max.handle, minus_max.at(t - 1))
                    for c in range(C):
                        width = WIDTH // C
                        last = pe.matmul(core.bank[6 + t % 2][:, c * width:(c + 1) * width],
                                         qT[:, c, t * P:(t + 1) * P], kbd[:, b, c, :], start=True, stop=True)
                    last.then_inc(s_ps.handle, 1)
                if cfg.guarded:
                    pe.wait_ge(nan_in.handle, nan_in.at(1))
                    pe.matmul(core.bank[6][:, 0:1], core.ones[:, :], odd_rows[:, :], start=True, stop=True)\
                      .then_inc(nan_ps.handle, 1)
                for t in range(TILES):
                    pe.wait_ge(prob.handle, prob.at(t + 1))
                    if t >= 2:
                        pe.wait_ge(pT_ready.handle, pT_ready.at(t - 1))
                    for k in range(PK):
                        last = pe.transpose(core.bank[t % 2][:, k * P:(k + 1) * P],
                                            probs[:, t, k * 4:(k + 1) * 4, :].rearrange("p h k -> p (h k)"),
                                            core.ident)
                    last.then_inc(pT_ps.handle, 1)
                    if t % TPB == TPB - 1:
                        b = t // TPB
                        pe.wait_ge(pT_ready.handle, pT_ready.at(t + 1))
                        for c in range(C):
                            n = b * C + c
                            if n >= 2:
                                pe.wait_ge(o_ready.handle, o_ready.at(n - 1))
                            chunks = list(cfg.prob_chunks_of(c))
                            for k in chunks:
                                last = pe.matmul(core.bank[2 + n % 2], vbd[:, b, cfg.v_block(c, k), :],
                                                 pT[:, k, b * SEQ:(b + 1) * SEQ],
                                                 start=k == chunks[0], stop=k == chunks[-1])
                            last.then_inc(o_ps.handle, 1)
                for b in range(BATCH):
                    pe.wait_ge(o_ready.handle, o_ready.at((b + 1) * C))
                    for t in range(TPB):
                        at = (b * TPB + t) * P
                        for c in range(C):
                            last = pe.matmul(core.bank[4 + b][:, t * P:(t + 1) * P], oT[:, c, at:at + P],
                                             w[:, cols["wo"]][:, c * D:(c + 1) * D],
                                             start=c == 0, stop=c == C - 1)
                    last.then_inc(out_ps.handle, 1)

            @block.gpsimd
            def _(pool):
                norm_gpsimd(core, pool)

            @block.scalar
            def _(act):
                norm_scalar(core, act)
                for n in range(BATCH * C):
                    half, c = divmod(n, C)
                    act.wait_ge(q_ps.handle, q_ps.at(n + 1))
                    dst, src = qT[:, c, half * SEQ:(half + 1) * SEQ], core.bank[2 + n % 4]
                    if cfg.biased:
                        at = cols["bq"].start + c
                        act.activation(dst, src, ACT.Identity, bias=w[:, at:at + 1]).then_inc(q_ready.handle, 1)
                    else:
                        act.copy(dst, src).then_inc(q_ready.handle, 1)
                for t in range(TILES):
                    act.wait_ge(minus_max.handle, minus_max.at(t + 1))
                    act.activation(probs[:, t, :, :], probs[:, t, :, :], ACT.Exp).then_inc(exp_done.handle, 1)
                for t in range(TILES):
                    act.wait_ge(pT_ps.handle, pT_ps.at(t + 1))
                    act.copy(pT[:, :, t * P:(t + 1) * P],
                             core.bank[t % 2][:, 0:PK * P].rearrange("p (k c) -> p k c", k=PK))\
                       .then_inc(pT_ready.handle, 1)
                    if t % TPB == TPB - 1:
                        b = t // TPB
                        for c in range(C):
                            n = b * C + c
                            act.wait_ge(o_ps.handle, o_ps.at(n + 1))
                            act.copy(oT[:, c, b * SEQ:(b + 1) * SEQ], core.bank[2 + n % 2])\
                               .then_inc(o_ready.handle, 1)

            @block.vector
            def _(dve):
                norm_vector(core, dve)
                link = Chain(dve, chain)

                def normalise(t):
                    dve.wait_ge(exp_done.handle, exp_done.at(t + 1))
                    link(dve.tensor_reduce(sums[:, t, :], probs[:, t, :, :], AXIS.X, ALU.add))
                    link(dve.reciprocal(inv[:, t, :], sums[:, t, :]))
                    done = dve.tensor_tensor(probs[:, t, :, :], probs[:, t, :, :], spread(inv[:, t, :], 2, KEYS),
                                             ALU.mult)
                    if cfg.guarded:
                        link(done)
                    else:
                        done.then_inc(prob.handle, 1)

                for t in range(TILES):
                    dve.wait_ge(s_ps.handle, s_ps.at(t + 1))
                    src = core.bank[6 + t % 2][:, 0:WIDTH]
                    if cfg.guarded:
                        link(dve.tensor_scalar(clipped[:, t % 2, :], src, -1e4, 1e4, ALU.max, ALU.min))
                        src = clipped[:, t % 2, :]
                    src = src.rearrange("p (h k) -> p h k", h=H)
                    link(dve.tensor_reduce(top[:, t, :], src, AXIS.X, ALU.max))
                    dve.tensor_tensor(probs[:, t, :, :], src, spread(top[:, t, :], 2, KEYS), ALU.subtract)\
                       .then_inc(minus_max.handle, 1)
                    if t >= 1:
                        normalise(t - 1)
                normalise(TILES - 1)
                if cfg.guarded:
                    all_sums = sums[:, :, :].rearrange("p t h -> p (t h)")
                    link(dve.memset(share[:, :], 1.0 / KEYS))
                    link(dve.tensor_tensor(odd[:, :], all_sums, all_sums, ALU.not_equal))
                    dve.tensor_reduce(odd_rows[:, :], odd[:, :], AXIS.X, ALU.max).then_inc(nan_in.handle, 1)
                    dve.wait_ge(nan_ps.handle, nan_ps.at(1))
                    link(dve.tensor_copy(flag[:, :], core.bank[6][:, 0:1]))
                    flat = probs[:, :, :, :].rearrange("p t h k -> p (t h k)")
                    n = TILES * WIDTH
                    dve.copy_predicated(flat, flag[:, :].bitcast(mybir.dt.uint32).to_broadcast([P, n]),
                                        share[:, :].to_broadcast([P, n])).then_inc(prob.handle, TILES)
                link(dve.tensor_tensor(core.x[:, :, :], core.x[:, :, :], spread(w[:, cols["bo"]], 1, TILES),
                                       ALU.add))
                for b in range(BATCH):
                    dve.wait_ge(out_ps.handle, out_ps.at(b + 1))
                    xb = core.x[:, b * TPB:(b + 1) * TPB, :]
                    link(dve.tensor_tensor(xb, xb, core.bank[4 + b].rearrange("p (t d) -> p t d", t=TPB),
                                           ALU.add))
                count[0] = link.count
    norm_close(core)
    for s, total in ((q_ps, BATCH * C), (q_ready, BATCH * C), (s_ps, TILES), (minus_max, TILES),
                     (exp_done, TILES), (prob, TILES), (pT_ps, TILES), (pT_ready, TILES),
                     (o_ps, BATCH * C), (o_ready, BATCH * C), (out_ps, BATCH)):
        s.close(total)
    if cfg.guarded:
        nan_in.close(1)
        nan_ps.close(1)
    chain.close(count[0])


def first_of_largest(dve, link, onehot, scores, iota, tmp, top):
    n = scores.shape[2]
    indices = spread(iota[:, 0:n], 1, TILES)
    link(dve.tensor_reduce(top, scores, AXIS.X, ALU.max))
    link(dve.tensor_tensor(tmp, scores, spread(top, 2, n), ALU.is_lt))
    link(dve.scalar_tensor_tensor(tmp, tmp, BIG_INDEX, indices, ALU.mult, ALU.add))
    link(dve.tensor_reduce(top, tmp, AXIS.X, ALU.min))
    link(dve.tensor_tensor(onehot, tmp, spread(top, 2, n), ALU.is_equal))


def router_tensor(core, pe, router, n, done):
    xnT = core.sig("ln_xnT")
    for t in range(TILES):
        if t % TPB == 0:
            pe.wait_ge(xnT.handle, xnT.at(t // TPB + 1))
        last = pe.matmul(core.bank[2][:, t * n:(t + 1) * n], core.xnT[:, t * P:(t + 1) * P], router,
                         start=True, stop=True)
    last.then_inc(done.handle, 1)


L0_EXPERTS, L0_INNER = 4, 512
L0F = {"router": slice(0, 4), "w1": slice(4, 2052), "wo": slice(2052, 2564), "bo": slice(2564, 2692),
       "gamma": slice(2692, 2820), "beta": slice(2820, 2948)}


def expert_feed_forward(core, w, w_sem, b1, b1_sem):
    nc, sig = core.nc, core.sig
    E, C = L0_EXPERTS, L0_INNER // P
    logits_ps, picked, masked = sig("f0_logits"), sig("f0_picked"), sig("f0_masked")
    mT_ps, mT_ready, oT_ps, oT_ready = sig("f0_mT_ps"), sig("f0_mT"), sig("f0_oT_ps"), sig("f0_oT")
    h_ps, h_ready, y_ps = sig("f0_h_ps"), sig("f0_h"), sig("f0_y_ps")
    var_eps, rstd, chain = sig("f0_var_eps"), sig("f0_rstd"), sig("dve_chain")
    count = [0]
    with ExitStack() as ctx:
        def sbuf(name, shape, dt=F32):
            return ctx.enter_context(nc.sbuf_tensor(f"l0_ffn_{name}", shape, dt))
        onehot = sbuf("onehot", [P, TILES, E])
        tmp = sbuf("tmp", [P, TILES, E])
        top = sbuf("top", [P, TILES])
        masked_x = sbuf("masked_x", [P, E, TILES, D])
        masked_xT = sbuf("masked_xT", [P, E, TILES * P])
        onehotT = sbuf("onehotT", [E, TILES * P])
        hT = sbuf("hT", [P, C, TILES * P])
        y = sbuf("y", [P, TILES, D])
        y_stats = sbuf("y_stats", [P, TILES, 6])
        y_mv = sbuf("y_mv", [P, TILES, 2])
        y_var = sbuf("y_var", [P, TILES])
        y_rstd = sbuf("y_rstd", [P, TILES])

        with nc.Block() as block:
            @block.tensor
            def _(pe):
                norm_tensor(core, pe)
                pe.wait_ge(w_sem, 16)
                router_tensor(core, pe, w[:, L0F["router"]], E, logits_ps)
                pe.wait_ge(picked.handle, picked.at(1))
                for b in range(BATCH):
                    for t in range(TPB):
                        last = pe.transpose(core.bank[2 + b][0:E, t * P:(t + 1) * P],
                                            onehot[:, b * TPB + t, :], core.ident)
                    last.then_inc(oT_ps.handle, 1)
                for e in range(E):
                    pe.wait_ge(masked.handle, masked.at(e + 1))
                    for b in range(BATCH):
                        n = e * BATCH + b
                        if n >= 2:
                            pe.wait_ge(mT_ready.handle, mT_ready.at(n - 1))
                        for t in range(TPB):
                            last = pe.transpose(core.bank[b][:, t * P:(t + 1) * P],
                                                masked_x[:, e, b * TPB + t, :], core.ident)
                        last.then_inc(mT_ps.handle, 1)
                pe.wait_ge(mT_ready.handle, mT_ready.at(E * BATCH))
                pe.wait_ge(oT_ready.handle, oT_ready.at(BATCH))
                pe.wait_ge(b1_sem, 16)
                for c in range(C):
                    for b in range(BATCH):
                        n = c * BATCH + b
                        if n >= 4:
                            pe.wait_ge(h_ready.handle, h_ready.at(n - 3))
                        out = core.bank[4 + n % 4]
                        cols = slice(b * SEQ, (b + 1) * SEQ)
                        for e in range(E):
                            at = e * L0_INNER + c * P
                            pe.matmul(out, w[:, L0F["w1"]][:, at:at + P], masked_xT[:, e, cols],
                                      start=e == 0, stop=False)
                        pe.matmul(out, b1[:, c * P:(c + 1) * P], onehotT[:, cols], start=False, stop=True)\
                          .then_inc(h_ps.handle, 1)
                pe.wait_ge(h_ready.handle, h_ready.at(C * BATCH))
                for b in range(BATCH):
                    for t in range(TPB):
                        at = (b * TPB + t) * P
                        for c in range(C):
                            last = pe.matmul(core.bank[2 + b][:, t * P:(t + 1) * P], hT[:, c, at:at + P],
                                             w[:, L0F["wo"]][:, c * D:(c + 1) * D], start=c == 0, stop=c == C - 1)
                    last.then_inc(y_ps.handle, 1)

            @block.gpsimd
            def _(pool):
                norm_gpsimd(core, pool)
                pool.wait_ge(var_eps.handle, var_eps.at(1))
                pool.tensor_tensor(y_rstd[:, :], y_var[:, :], core.minus_half[:, 0:1].to_broadcast([P, TILES]),
                                   ALU.pow).then_inc(rstd.handle, 1)

            @block.scalar
            def _(act):
                norm_scalar(core, act)
                for b in range(BATCH):
                    act.wait_ge(oT_ps.handle, oT_ps.at(b + 1))
                    act.copy(onehotT[:, b * SEQ:(b + 1) * SEQ], core.bank[2 + b][0:E, :])\
                       .then_inc(oT_ready.handle, 1)
                for n in range(L0_EXPERTS * BATCH):
                    e, b = divmod(n, BATCH)
                    act.wait_ge(mT_ps.handle, mT_ps.at(n + 1))
                    act.copy(masked_xT[:, e, b * SEQ:(b + 1) * SEQ], core.bank[b]).then_inc(mT_ready.handle, 1)
                for n in range(C * BATCH):
                    c, b = divmod(n, BATCH)
                    act.wait_ge(h_ps.handle, h_ps.at(n + 1))
                    act.activation(hT[:, c, b * SEQ:(b + 1) * SEQ], core.bank[4 + n % 4], ACT.Gelu)\
                       .then_inc(h_ready.handle, 1)

            @block.vector
            def _(dve):
                norm_vector(core, dve)
                link = Chain(dve, chain)
                dve.wait_ge(logits_ps.handle, logits_ps.at(1))
                first_of_largest(dve, link, onehot[:, :, :],
                                 core.bank[2][:, 0:TILES * E].rearrange("p (t e) -> p t e", t=TILES),
                                 core.const["iota"], tmp[:, :, :], top[:, :])
                dve.memset(y_var[:, :], 0.0).then_inc(picked.handle, 1)
                for e in range(E):
                    dve.tensor_tensor(masked_x[:, e, :, :], core.xn[:, :, :], spread(onehot[:, :, e], 2, D),
                                      ALU.mult).then_inc(masked.handle, 1)
                link(dve.tensor_tensor(y[:, :, :], core.xn[:, :, :], spread(w[:, L0F["bo"]], 1, TILES), ALU.add))
                for b in range(BATCH):
                    dve.wait_ge(y_ps.handle, y_ps.at(b + 1))
                    yb = y[:, b * TPB:(b + 1) * TPB, :]
                    link(dve.tensor_tensor(yb, yb, core.bank[2 + b].rearrange("p (t d) -> p t d", t=TPB), ALU.add))
                for t in range(TILES):
                    link(dve.bn_stats(y_stats[:, t, :], y[:, t, :]))
                    link(dve.bn_aggr(y_mv[:, t, :], y_stats[:, t, :]))
                dve.wait_ge(picked.handle, picked.at(1))
                dve.tensor_scalar(y_var[:, :], y_mv[:, :, 1], 1e-12, None, ALU.add).then_inc(var_eps.handle, 1)
                dve.wait_ge(rstd.handle, rstd.at(1))
                for t in range(TILES):
                    link(dve.tensor_scalar(y[:, t, :], y[:, t, :], y_mv[:, t, 0:1], y_rstd[:, t:t + 1],
                                           ALU.subtract, ALU.mult))
                link(dve.tensor_tensor(y[:, :, :], y[:, :, :], spread(w[:, L0F["gamma"]], 1, TILES), ALU.mult))
                link(dve.tensor_tensor(y[:, :, :], y[:, :, :], spread(w[:, L0F["beta"]], 1, TILES), ALU.add))
                link(dve.tensor_tensor(core.x[:, :, :], core.x[:, :, :], y[:, :, :], ALU.add))
                count[0] = link.count
    norm_close(core)
    for s, total in ((logits_ps, 1), (picked, 1), (masked, E), (mT_ps, E * BATCH), (mT_ready, E * BATCH),
                     (oT_ps, BATCH), (oT_ready, BATCH), (h_ps, C * BATCH), (h_ready, C * BATCH), (y_ps, BATCH),
                     (var_eps, 1), (rstd, 1), (chain, count[0])):
        s.close(total)


L1_EXPERTS, L1_INNER = 8, 512
L1F = {"router": slice(0, 9), "bias": slice(9, 18)}


def gated_experts(core, w, w_sem, w1_dram, w2_dram):
    nc, sig = core.nc, core.sig
    E, N, C = L1_EXPERTS, L1_EXPERTS + 1, L1_INNER // P
    logits_ps, exp_in, exp_out, gates_ready = sig("f1_logits"), sig("f1_exp_in"), sig("f1_exp_out"), sig("f1_gates")
    w1_in, w2_in = [sig("f1_w1_even"), sig("f1_w1_odd")], [sig("f1_w2_even"), sig("f1_w2_odd")]
    up_ps, h_ready, y_ps, y_read, chain = sig("f1_up_ps"), sig("f1_h"), sig("f1_y_ps"), sig("f1_y_read"), sig("dve_chain")
    count = [0]
    with ExitStack() as ctx:
        def sbuf(name, shape, dt=F32):
            return ctx.enter_context(nc.sbuf_tensor(f"l1_ffn_{name}", shape, dt))
        w1 = [sbuf(f"w1_{i}", [P, L1_INNER]) for i in range(2)]
        w2 = [sbuf(f"w2_{i}", [P, C * D]) for i in range(2)]
        hT = [sbuf(f"hT{i}", [P, C, TILES * P]) for i in range(2)]
        probs = sbuf("probs", [P, TILES, N])
        rest = sbuf("rest", [P, TILES, N])
        tmp = sbuf("tmp", [P, TILES, N])
        choice = sbuf("choice", [P, 2, TILES, N])
        top = sbuf("top", [P, TILES])
        gates = sbuf("gates", [P, TILES, N])
        acc = sbuf("acc", [P, TILES, D])

        def load(sp, e, p):
            sp.dma_start(w1[p][:, :], w1_dram[bass.ds(e, 1), :, :].rearrange("o p c -> (o p) c"))\
              .then_inc(w1_in[p].handle, 16)
            sp.dma_start(w2[p][:, :], w2_dram[bass.ds(e, 1), :, :].rearrange("o p c -> (o p) c"))\
              .then_inc(w2_in[p].handle, 16)

        def up(pe, e, p, half_e, first=False):
            pe.wait_ge(w1_in[p].handle, w1_in[p].at(16 * (half_e + 1)))
            for c in range(C):
                if not (first and c < 2):
                    pe.wait_ge(h_ready.handle, h_ready.at(e * C + c - 1))
                for b in range(BATCH):
                    last = pe.matmul(core.bank[3 + 2 * (c % 2) + b - 1], w1[p][:, c * P:(c + 1) * P],
                                     core.xnT[:, b * SEQ:(b + 1) * SEQ], start=True, stop=True)
                last.then_inc(up_ps.handle, 1)

        def down(pe, e, p, half_e, first=False):
            pe.wait_ge(w2_in[p].handle, w2_in[p].at(16 * (half_e + 1)))
            pe.wait_ge(h_ready.handle, h_ready.at((e + 1) * C))
            for b in range(BATCH):
                if not first:
                    pe.wait_ge(y_read.handle, y_read.at((e - 1) * BATCH + b + 1))
                for t in range(TPB):
                    at = (b * TPB + t) * P
                    for c in range(C):
                        last = pe.matmul(core.bank[6 + b][:, t * P:(t + 1) * P], hT[p][:, c, at:at + P],
                                         w2[p][:, c * D:(c + 1) * D], start=c == 0, stop=c == C - 1)
                last.then_inc(y_ps.handle, 1)

        def gelu(act, e, p, no_down=False):
            if not no_down:
                act.wait_ge(y_ps.handle, y_ps.at((e - 1) * BATCH))
            for c in range(C):
                act.wait_ge(up_ps.handle, up_ps.at(e * C + c + 1))
                act.activation(hT[p][:, c, :].rearrange("p (b s) -> p b s", b=BATCH),
                               core.psum[:, 2 + 2 * (c % 2):4 + 2 * (c % 2), :], ACT.Gelu).then_inc(h_ready.handle, 1)

        def accumulate(dve, e):
            for b in range(BATCH):
                dve.wait_ge(y_ps.handle, y_ps.at(e * BATCH + b + 1))
                for t in range(TPB):
                    at = acc[:, b * TPB + t, :]
                    last = dve.scalar_tensor_tensor(at, core.bank[6 + b][:, t * P:(t + 1) * P],
                                                    gates[:, b * TPB + t, bass.ds(e, 1)], at, ALU.mult, ALU.add)
                last.then_inc(y_read.handle, 1)
                dve.wait_ge(y_read.handle, y_read.at(e * BATCH + b + 1))

        with nc.Block() as block:
            @block.sync
            def _(sp):
                load(sp, 0, 0)
                load(sp, 1, 1)
                with sp.Fori(1, E // 2) as i:
                    for p in range(2):
                        e = i * 2 + p
                        sp.wait_ge(y_ps.handle, y_ps.at((e - 1) * BATCH))
                        load(sp, e, p)

            @block.tensor
            def _(pe):
                norm_tensor(core, pe)
                pe.wait_ge(w_sem, 16)
                router_tensor(core, pe, w[:, L1F["router"]], N, logits_ps)
                pe.wait_ge(exp_in.handle, exp_in.at(1))
                up(pe, 0, 0, 0, first=True)
                up(pe, 1, 1, 0)
                down(pe, 0, 0, 0, first=True)
                with pe.Fori(1, E // 2) as i:
                    up(pe, i * 2, 0, i)
                    down(pe, i * 2 - 1, 1, i - 1)
                    up(pe, i * 2 + 1, 1, i)
                    down(pe, i * 2, 0, i)
                down(pe, E - 1, 1, E // 2 - 1)

            @block.gpsimd
            def _(pool):
                norm_gpsimd(core, pool)

            @block.scalar
            def _(act):
                norm_scalar(core, act)
                act.wait_ge(exp_in.handle, exp_in.at(1))
                act.activation(probs[:, :, :], probs[:, :, :], ACT.Exp).then_inc(exp_out.handle, 1)
                gelu(act, 0, 0, no_down=True)
                gelu(act, 1, 1, no_down=True)
                with act.Fori(1, E // 2) as i:
                    gelu(act, i * 2, 0)
                    gelu(act, i * 2 + 1, 1)

            @block.vector
            def _(dve):
                norm_vector(core, dve)
                link = Chain(dve, chain)
                dve.wait_ge(logits_ps.handle, logits_ps.at(1))
                scores = core.bank[2][:, 0:TILES * N].rearrange("p (t e) -> p t e", t=TILES)
                link(dve.tensor_tensor(rest[:, :, :], scores, spread(w[:, L1F["bias"]], 1, TILES), ALU.add))
                link(dve.tensor_reduce(top[:, :], rest[:, :, :], AXIS.X, ALU.max))
                dve.tensor_tensor(probs[:, :, :], rest[:, :, :], spread(top[:, :], 2, N), ALU.subtract)\
                   .then_inc(exp_in.handle, 1)
                dve.wait_ge(exp_out.handle, exp_out.at(1))
                link(dve.tensor_reduce(top[:, :], probs[:, :, :], AXIS.X, ALU.add))
                link(dve.reciprocal(top[:, :], top[:, :]))
                link(dve.tensor_tensor(probs[:, :, :], probs[:, :, :], spread(top[:, :], 2, N), ALU.mult))
                first, second = choice[:, 0], choice[:, 1]
                first_of_largest(dve, link, first, probs[:, :, :], core.const["iota"], tmp[:, :, :], top[:, :])
                link(dve.scalar_tensor_tensor(rest[:, :, :], first, -BIG_INDEX, probs[:, :, :], ALU.mult, ALU.add))
                first_of_largest(dve, link, second, rest[:, :, :], core.const["iota"], tmp[:, :, :], top[:, :])
                link(dve.tensor_tensor(tmp[:, :, :], first, second, ALU.add))
                link(dve.tensor_tensor(gates[:, :, :], tmp[:, :, :], probs[:, :, :], ALU.mult))
                link(dve.tensor_tensor(acc[:, :, :], core.xn[:, :, :], spread(gates[:, :, E], 2, D), ALU.mult))
                with dve.Fori(0, E // 2) as i:
                    for p in range(2):
                        accumulate(dve, i * 2 + p)
                link(dve.tensor_tensor(core.x[:, :, :], core.x[:, :, :], acc[:, :, :], ALU.add))
                count[0] = link.count
    norm_close(core)
    for s, total in ((logits_ps, 1), (exp_in, 1), (exp_out, 1), (w1_in[0], 16 * E // 2), (w1_in[1], 16 * E // 2),
                     (w2_in[0], 16 * E // 2), (w2_in[1], 16 * E // 2), (up_ps, E * C), (h_ready, E * C),
                     (y_ps, E * BATCH), (y_read, E * BATCH), (chain, count[0])):
        s.close(total)


L2_INNER = 512
L2F = {"gate": slice(0, 512), "up": slice(512, 1024), "down": slice(1024, 1536)}


def quantised_feed_forward(core, w, w_sem):
    nc, sig = core.nc, core.sig
    C = L2_INNER // P
    sums_in, sums_ps, wq_ready, xq_ready = sig("f2_sums"), sig("f2_sums_ps"), sig("f2_wq"), sig("f2_xq")
    xT_ps, xT_ready, gu_ps, gate_ready, gu_read = (sig("f2_xT_ps"), sig("f2_xT"), sig("f2_gu_ps"),
                                                   sig("f2_gate"), sig("f2_gu_read"))
    hq_ready, hT_ps, hT_ready, y_ps, scaled = sig("f2_hq"), sig("f2_hT_ps"), sig("f2_hT"), sig("f2_y_ps"), sig("f2_scaled")
    chain, x_gate_ready = sig("dve_chain"), sig("f2_x_gate")
    count = [0]
    with ExitStack() as ctx:
        def sbuf(name, shape, dt=F32):
            return ctx.enter_context(nc.sbuf_tensor(f"l2_ffn_{name}", shape, dt))
        sizes = sbuf("sizes", [P, 3])
        means = sbuf("means", [P, 3])
        w_scale = sbuf("w_scale", [P, 3])
        rounded = sbuf("rounded", [P, 3, 512])
        wq = sbuf("wq", [P, 3, 512], BF16)
        x_top = sbuf("x_top", [P, TILES])
        x_scale = sbuf("x_scale", [P, TILES])
        x_unit = sbuf("x_unit", [P, TILES])
        x_gate = sbuf("x_gate", [P, TILES])
        x_up = sbuf("x_up", [P, TILES])
        x_round = sbuf("x_round", [P, TILES, D])
        xq = sbuf("xq", [P, TILES, D], BF16)
        xqT = sbuf("xqT", [P, TILES * P], BF16)
        gate = sbuf("gate", [P, TILES, L2_INNER])
        h = sbuf("h", [P, TILES, L2_INNER])
        h_top = sbuf("h_top", [P, TILES])
        h_scale = sbuf("h_scale", [P, TILES])
        h_unit = sbuf("h_unit", [P, TILES])
        hq = sbuf("hq", [P, TILES, L2_INNER], BF16)
        hqT = sbuf("hqT", [P, TILES, C, P], BF16)

        def quantise(dve, link, top, scale, unit, src, rounded_at, dst, last):
            link(dve.tensor_reduce(top, src, AXIS.X, ALU.max, apply_absolute_value=True))
            link(dve.tensor_scalar(top, top, 1e-5, None, ALU.max))
            link(dve.reciprocal(scale, top))
            link(dve.tensor_scalar(scale, scale, 127.0, None, ALU.mult))
            link(dve.tensor_scalar(unit, top, 1.0 / 127.0, None, ALU.mult))
            link(dve.tensor_scalar(rounded_at, src, scale, MAGIC, ALU.mult, ALU.add))
            link(dve.tensor_scalar(rounded_at, rounded_at, -MAGIC, 127.0, ALU.add, ALU.min))
            dve.tensor_scalar(dst, rounded_at, -128.0, None, ALU.max).then_inc(last.handle, 1)

        def down(pe, t):
            pe.wait_ge(hq_ready.handle, hq_ready.at(t + 1))
            if t >= 2:
                pe.wait_ge(scaled.handle, scaled.at(t - 1))
            flat = core.bank[6 + t % 2].bitcast(BF16)
            for c in range(C):
                last = pe.transpose(flat[:, c * P:(c + 1) * P], hq[:, t, c * P:(c + 1) * P], core.ident_bf)
            last.then_inc(hT_ps.handle, 1)
            pe.wait_ge(hT_ready.handle, hT_ready.at(t + 1))
            for c in range(C):
                last = pe.matmul(core.bank[t % 2][:, 0:D], hqT[:, t, c, :], wq[:, 2, c * D:(c + 1) * D],
                                 start=c == 0, stop=c == C - 1)
            last.then_inc(y_ps.handle, 1)

        def hidden_T(act, t):
            act.wait_ge(hT_ps.handle, hT_ps.at(t + 1))
            act.copy(hqT[:, t, :, :], core.bank[6 + t % 2].bitcast(BF16)[:, 0:L2_INNER]
                     .rearrange("p (c t) -> p c t", c=C)).then_inc(hT_ready.handle, 1)

        def output(dve, link, t):
            link(dve.tensor_scalar(h_unit[:, t:t + 1], h_unit[:, t:t + 1], means[:, 2:3], None, ALU.mult))
            dve.wait_ge(y_ps.handle, y_ps.at(t + 1))
            dve.scalar_tensor_tensor(core.x[:, t, :], core.bank[t % 2][:, 0:D], h_unit[:, t:t + 1],
                                     core.x[:, t, :], ALU.mult, ALU.add).then_inc(scaled.handle, 1)

        with nc.Block() as block:
            @block.tensor
            def _(pe):
                norm_tensor(core, pe)
                pe.wait_ge(sums_in.handle, sums_in.at(1))
                pe.matmul(core.bank[2][:, 0:3], core.ones[:, :], sizes[:, :], start=True, stop=True)\
                  .then_inc(sums_ps.handle, 1)
                for t in range(TILES):
                    pe.wait_ge(xq_ready.handle, xq_ready.at(t + 1))
                    if t == 0:
                        pe.wait_ge(core.sig("ln_xnT").handle, core.sig("ln_xnT").at(BATCH))
                    out = core.bank[t // TPB].bitcast(BF16)
                    last = pe.transpose(out[:, (t % TPB) * P:(t % TPB + 1) * P], xq[:, t, :], core.ident_bf)
                    if t % TPB == TPB - 1:
                        last.then_inc(xT_ps.handle, 1)
                pe.wait_ge(wq_ready.handle, wq_ready.at(3))
                for t in range(TILES):
                    pe.wait_ge(xT_ready.handle, xT_ready.at(t // TPB + 1))
                    if t >= 2:
                        pe.wait_ge(gu_read.handle, gu_read.at(t - 1))
                    for k in range(2):
                        last = pe.matmul(core.bank[2 + 2 * (t % 2) + k], xqT[:, t * P:(t + 1) * P], wq[:, k, :],
                                         start=True, stop=True)
                    last.then_inc(gu_ps.handle, 1)
                    if t >= 1:
                        down(pe, t - 1)
                down(pe, TILES - 1)

            @block.gpsimd
            def _(pool):
                norm_gpsimd(core, pool)

            @block.scalar
            def _(act):
                norm_scalar(core, act)
                for b in range(BATCH):
                    act.wait_ge(xT_ps.handle, xT_ps.at(b + 1))
                    act.copy(xqT[:, b * SEQ:(b + 1) * SEQ], core.bank[b].bitcast(BF16)[:, 0:SEQ])\
                       .then_inc(xT_ready.handle, 1)
                act.wait_ge(x_gate_ready.handle, x_gate_ready.at(1))
                for t in range(TILES):
                    act.wait_ge(gu_ps.handle, gu_ps.at(t + 1))
                    act.activation(gate[:, t, :], core.bank[2 + 2 * (t % 2)], ACT.Silu, scale=x_gate[:, t:t + 1])\
                       .then_inc(gate_ready.handle, 1)
                    if t >= 1:
                        hidden_T(act, t - 1)
                hidden_T(act, TILES - 1)

            @block.vector
            def _(dve):
                link = Chain(dve, chain)
                dve.wait_ge(w_sem, 16)
                w3 = w[:, :].rearrange("p (k c) -> p k c", k=3)
                dve.tensor_reduce(sizes[:, :], w3, AXIS.X, ALU.add, apply_absolute_value=True)\
                   .then_inc(sums_in.handle, 1)
                norm_vector(core, dve)
                dve.wait_ge(sums_ps.handle, sums_ps.at(1))
                link(dve.tensor_scalar(means[:, :], core.bank[2][:, 0:3], 1.0 / (P * 512), 1e-5, ALU.mult, ALU.max))
                link(dve.reciprocal(w_scale[:, :], means[:, :]))
                for k in range(3):
                    link(dve.tensor_scalar(rounded[:, k, :], w3[:, k, :], w_scale[:, k:k + 1], MAGIC, ALU.mult, ALU.add))
                    link(dve.tensor_scalar(rounded[:, k, :], rounded[:, k, :], -MAGIC, 1.0, ALU.add, ALU.min))
                    dve.tensor_scalar(wq[:, k, :], rounded[:, k, :], -1.0, None, ALU.max).then_inc(wq_ready.handle, 1)
                xn_done = core.sig("ln_xn")
                dve.wait_ge(xn_done.handle, xn_done.at(TILES))
                for t in range(TILES):
                    quantise(dve, link, x_top[:, t:t + 1], x_scale[:, t:t + 1], x_unit[:, t:t + 1],
                             core.xn[:, t, :], x_round[:, t, :], xq[:, t, :], xq_ready)
                dve.tensor_scalar(x_gate[:, :], x_unit[:, :], means[:, 0:1], None, ALU.mult)\
                   .then_inc(x_gate_ready.handle, 1)
                link(dve.tensor_scalar(x_up[:, :], x_unit[:, :], means[:, 1:2], None, ALU.mult))
                for t in range(TILES):
                    dve.wait_ge(gate_ready.handle, gate_ready.at(t + 1))
                    dve.scalar_tensor_tensor(h[:, t, :], core.bank[3 + 2 * (t % 2)], x_up[:, t:t + 1],
                                             gate[:, t, :], ALU.mult, ALU.mult).then_inc(gu_read.handle, 1)
                    dve.wait_ge(gu_read.handle, gu_read.at(t + 1))
                    quantise(dve, link, h_top[:, t:t + 1], h_scale[:, t:t + 1], h_unit[:, t:t + 1],
                             h[:, t, :], h[:, t, :], hq[:, t, :], hq_ready)
                    if t >= 1:
                        output(dve, link, t - 1)
                output(dve, link, TILES - 1)
                count[0] = link.count

    norm_close(core)
    for s, total in ((sums_in, 1), (x_gate_ready, 1), (sums_ps, 1), (wq_ready, 3), (xq_ready, TILES), (xT_ps, BATCH), (xT_ready, BATCH),
                     (gu_ps, TILES), (gate_ready, TILES), (gu_read, TILES), (hq_ready, TILES), (hT_ps, TILES),
                     (hT_ready, TILES), (y_ps, TILES), (scaled, TILES), (chain, count[0])):
        s.close(total)


L3_EXPERTS, L3_INNER = 16, 256
L3F = {"router": slice(0, 16), "bias": slice(16, 32), "phase": slice(32, 64), "norm": slice(64, 192)}
TURN = 6.283185307179586
SIN_SCALE = 6.2831850

SURE = 25.0


def tanh_cos_experts(core, w, w_sem, up_dram, down_dram):
    nc, sig = core.nc, core.sig
    N = L3_EXPERTS
    C = L3_INNER // P
    BUFS = 4
    logits_ps, logits_read, exp_in, exp_out = sig("f3_logits"), sig("f3_logits_read"), sig("f3_exp_in"), sig("f3_exp_out")
    up_in, down_in = [[sig(f"f3_{name}{i}") for i in range(BUFS)] for name in ("up", "down")]
    f_ps, m_ps, bounded, exp_done, ln_done = sig("f3_f_ps"), sig("f3_m_ps"), sig("f3_bounded"), sig("f3_exp"), sig("f3_ln")
    z_done, u_done, k_done, frac_done = sig("f3_z"), sig("f3_u"), sig("f3_k"), sig("f3_frac")
    tanh_done, sin_done, h_done = sig("f3_tanh"), sig("f3_sin"), sig("f3_h")
    y_ps, y_read, chain, filled = sig("f3_y_ps"), sig("f3_y_read"), sig("dve_chain"), sig("f3_filled")
    mean_sq, rstd = sig("f3_mean_sq"), sig("f3_rstd")
    count = [0]
    with ExitStack() as ctx:
        def sbuf(name, shape, dt=F32):
            return ctx.enter_context(nc.sbuf_tensor(f"l3_ffn_{name}", shape, dt))
        w_up = [sbuf(f"w_up{i}", [P, 2 * C * P]) for i in range(BUFS)]
        w_down = [sbuf(f"w_down{i}", [P, C * D]) for i in range(BUFS)]
        angle = [sbuf(f"angle{i}", [P, C, TILES * P]) for i in range(2)]
        whole = sbuf("whole", [P, C, TILES * P])
        sine = sbuf("sine", [P, C, TILES * P])
        hidden = [sbuf(f"hidden{i}", [P, C, TILES * P]) for i in range(BUFS)]
        phase = sbuf("phase", [P, N * C])
        scores = sbuf("scores", [P, TILES, N])
        rest = sbuf("rest", [P, TILES, N])
        tmp = sbuf("tmp", [P, TILES, N])
        choice = sbuf("choice", [P, 2, TILES, N])
        best = sbuf("best", [P, 2, TILES])
        top = sbuf("top", [P, TILES])
        gap = sbuf("gap", [P, TILES])
        gates = sbuf("gates", [P, TILES, N])
        acc = sbuf("acc", [P, TILES, D])
        mean = sbuf("mean", [P, TILES])
        inv_root = sbuf("inv_root", [P, TILES])

        def at_least(e, n):
            return not isinstance(e, int) or e >= n

        def load(sp, e, j):
            sp.dma_start(w_up[j][:, :], up_dram[bass.ds(e, 1), :, :].rearrange("o p c -> (o p) c"))\
              .then_inc(up_in[j].handle, 16)
            if at_least(e, BUFS):
                sp.wait_ge(y_ps.handle, y_ps.at((e - BUFS + 1) * BATCH))
            sp.dma_start(w_down[j][:, :], down_dram[bass.ds(e, 1), :, :].rearrange("o p c -> (o p) c"))\
              .then_inc(down_in[j].handle, 16)

        def product(pe, j, c, which, bank, done):
            for b in range(BATCH):
                at = (which * C + c) * P
                last = pe.matmul(core.bank[bank + b], w_up[j][:, at:at + P],
                                 core.xnT[:, b * SEQ:(b + 1) * SEQ], start=True, stop=True)
            last.then_inc(done.handle, 1)

        def freq(pe, e, j, c):
            if at_least(e, 1):
                pe.wait_ge(z_done.handle, z_done.at((e - 1) * C + c + 1))
            product(pe, j, c, 0, 2 + 2 * c, f_ps)

        def mag(pe, e, j, c):
            if at_least(e, 1) or c > 0:
                pe.wait_ge(tanh_done.handle, tanh_done.at(e * C + c))
            product(pe, j, c, 1, 0, m_ps)

        def down(pe, e, j, turn, b):
            pe.wait_ge(down_in[j].handle, down_in[j].at(16 * (turn + 1)))
            pe.wait_ge(h_done.handle, h_done.at((e + 1) * C))
            if at_least(e, 1):
                pe.wait_ge(y_read.handle, y_read.at(e * BATCH + b - 1))
            for t in range(TPB):
                at = (b * TPB + t) * P
                for c in range(C):
                    last = pe.matmul(core.bank[6 + b][:, t * P:(t + 1) * P], hidden[j][:, c, at:at + P],
                                     w_down[j][:, c * D:(c + 1) * D], start=c == 0, stop=c == C - 1)
            last.then_inc(y_ps.handle, 1)

        def tensor_step(pe, e, j, turn):
            j_next, turn_next = (j + 1) % BUFS, turn + (j + 1) // BUFS
            more = not isinstance(e, int) or e < N - 1
            if more:
                pe.wait_ge(up_in[j_next].handle, up_in[j_next].at(16 * (turn_next + 1)))
                mag(pe, e + 1, j_next, 0)
                for c in range(C):
                    freq(pe, e + 1, j_next, c)
            if at_least(e, 2):
                before = ((j - 2) % BUFS, turn - (1 if j < 2 else 0))
                down(pe, e - 2, *before, 0)
            if more:
                mag(pe, e + 1, j_next, 1)
            if at_least(e, 2):
                down(pe, e - 2, *before, 1)

        def tanh(act, e, j, c):
            act.wait_ge(m_ps.handle, m_ps.at(e * C + c + 1))
            if at_least(e, BUFS):
                act.wait_ge(y_ps.handle, y_ps.at((e - BUFS + 1) * BATCH))
            act.activation(hidden[j][:, c, :].rearrange("p (b s) -> p b s", b=BATCH),
                           core.psum[:, 0:BATCH, :], ACT.Tanh).then_inc(tanh_done.handle, 1)

        def sines(act, e, j):
            for c in range(C):
                act.wait_ge(frac_done.handle, frac_done.at(e * C + c + 1))
                if at_least(e, 1):
                    act.wait_ge(h_done.handle, h_done.at((e - 1) * C + c + 1))
                act.activation(sine[:, c, :], angle[j % 2][:, c, :], ACT.Sin, scale=SIN_SCALE)\
                   .then_inc(sin_done.handle, 1)

        def scalar_step(act, e, j):
            at = angle[j % 2]
            tanh(act, e, j, 0)
            for c in range(C):
                act.wait_ge(bounded.handle, bounded.at(e * C + c + 1))
                act.activation(at[:, c, :], at[:, c, :], ACT.Exp).then_inc(exp_done.handle, 1)
            tanh(act, e, j, 1)
            for c in range(C):
                act.wait_ge(exp_done.handle, exp_done.at(e * C + c + 1))
                act.activation(at[:, c, :], at[:, c, :], ACT.Ln, bias=1.0).then_inc(ln_done.handle, 1)
            if at_least(e, 1):
                sines(act, e - 1, j - 1)

        def f_of(c):
            return core.psum[:, 2 + 2 * c:4 + 2 * c, :]

        def by_batch(at):
            return at.rearrange("p (b s) -> p b s", b=BATCH)

        def bound(dve, e, j):
            for c in range(C):
                dve.wait_ge(f_ps.handle, f_ps.at(e * C + c + 1))
                if at_least(e, 2):
                    dve.wait_ge(sin_done.handle, sin_done.at((e - 2) * C + c + 1))
                dve.tensor_scalar(by_batch(angle[j % 2][:, c, :]), f_of(c), SURE, None, ALU.min)\
                   .then_inc(bounded.handle, 1)

        def softplus(dve, e, j, c):
            at = by_batch(angle[j % 2][:, c, :])
            dve.wait_ge(ln_done.handle, ln_done.at(e * C + c + 1))
            dve.scalar_tensor_tensor(at, f_of(c), 1.0, at, ALU.mult, ALU.max).then_inc(z_done.handle, 1)

        def turns(dve, e, j, c):
            at = angle[j % 2][:, c, :]
            dve.wait_ge(z_done.handle, z_done.at(e * C + c + 1))
            dve.tensor_scalar(at, at, 1.0 / TURN, phase[:, bass.ds(e * C + c, 1)], ALU.mult, ALU.add)\
               .then_inc(u_done.handle, 1)
            dve.wait_ge(u_done.handle, u_done.at(e * C + c + 1))
            if at_least(e, 1):
                dve.wait_ge(frac_done.handle, frac_done.at((e - 1) * C + c + 1))
            dve.tensor_scalar(whole[:, c, :], at, MAGIC, -MAGIC, ALU.add, ALU.add).then_inc(k_done.handle, 1)

        def accumulate(dve, e):
            for b in range(BATCH):
                n = e * BATCH + b + 1
                dve.wait_ge(y_ps.handle, y_ps.at(n))
                if at_least(e, 1):
                    dve.wait_ge(y_read.handle, y_read.at(n - BATCH))
                for t in range(TPB):
                    at = acc[:, b * TPB + t, :]
                    last = dve.scalar_tensor_tensor(at, core.bank[6 + b][:, t * P:(t + 1) * P],
                                                    gates[:, b * TPB + t, bass.ds(e, 1)], at, ALU.mult, ALU.add)
                last.then_inc(y_read.handle, 1)

        def vector_step(dve, e, j):
            for c in range(C):
                softplus(dve, e, j, c)
            turns(dve, e, j, 0)
            if not isinstance(e, int) or e < N - 1:
                bound(dve, e + 1, j + 1)
            turns(dve, e, j, 1)
            if at_least(e, 2):
                accumulate(dve, e - 2)

        def wait_alone(pool, signal, n):
            pool.wait_ge(signal.handle, signal.at(n))
            pool.sem_inc(core.sig("pool_paced").handle, 1)

        def times_sine(pool, e, j):
            for c in range(C):
                wait_alone(pool, sin_done, e * C + c + 1)
                at = hidden[j % BUFS][:, c, :]
                pool.tensor_tensor(at, at, sine[:, c, :], ALU.mult).then_inc(h_done.handle, 1)

        def gpsimd_step(pool, e, j):
            for c in range(C):
                wait_alone(pool, k_done, e * C + c + 1)
                at = angle[j % 2][:, c, :]
                pool.tensor_tensor(at, at, whole[:, c, :], ALU.subtract).then_inc(frac_done.handle, 1)
            if at_least(e, 1):
                times_sine(pool, e - 1, j - 1)

        def every_step(engine, step):
            for j in range(BUFS):
                step(j, j, 0)
            with engine.Fori(1, N // BUFS - 1) as i:
                for j in range(BUFS):
                    step(i * BUFS + j, j, i)
            for j in range(BUFS):
                step(N - BUFS + j, j, N // BUFS - 1)

        with nc.Block() as block:
            @block.sync
            def _(sp):
                for e in range(BUFS):
                    load(sp, e, e)
                with sp.Fori(1, N // BUFS) as i:
                    for j in range(BUFS):
                        sp.wait_ge(m_ps.handle, m_ps.at((i * BUFS + j - BUFS + 1) * C))
                        load(sp, i * BUFS + j, j)

            @block.tensor
            def _(pe):
                norm_tensor(core, pe)
                pe.wait_ge(w_sem, 16)
                router_tensor(core, pe, w[:, L3F["router"]], N, logits_ps)
                pe.wait_ge(logits_read.handle, logits_read.at(1))
                pe.wait_ge(up_in[0].handle, up_in[0].at(16))
                for c in range(C):
                    freq(pe, 0, 0, c)
                for c in range(C):
                    mag(pe, 0, 0, c)
                every_step(pe, lambda e, j, turn: tensor_step(pe, e, j, turn))
                for e in (N - 2, N - 1):
                    for b in range(BATCH):
                        down(pe, e, e % BUFS, e // BUFS, b)

            @block.gpsimd
            def _(pool):
                norm_gpsimd(core, pool)
                pool.memset(acc[:, :, :], 0.0).then_inc(filled.handle, 1)
                every_step(pool, lambda e, j, turn: gpsimd_step(pool, e, j))
                times_sine(pool, N - 1, BUFS - 1)
                pool.wait_ge(mean_sq.handle, mean_sq.at(1))
                pool.tensor_tensor(inv_root[:, :], mean[:, :], core.minus_half[:, 0:1].to_broadcast([P, TILES]),
                                   ALU.pow).then_inc(rstd.handle, 1)

            @block.scalar
            def _(act):
                norm_scalar(core, act)
                act.wait_ge(exp_in.handle, exp_in.at(1))
                act.activation(gap[:, :], gap[:, :], ACT.Exp).then_inc(exp_out.handle, 1)
                every_step(act, lambda e, j, turn: scalar_step(act, e, j))
                sines(act, N - 1, BUFS - 1)

            @block.vector
            def _(dve):
                norm_vector(core, dve)
                link = Chain(dve, chain)
                dve.wait_ge(w_sem, 16)
                link(dve.tensor_scalar(phase[:, :], w[:, L3F["phase"]], 0.1 + TURN / 4, 1.0 / TURN,
                                       ALU.add, ALU.mult))
                dve.wait_ge(logits_ps.handle, logits_ps.at(1))
                dve.tensor_tensor(scores[:, :, :], core.bank[2][:, 0:TILES * N].rearrange("p (t e) -> p t e", t=TILES),
                                  spread(w[:, L3F["bias"]], 1, TILES), ALU.add).then_inc(logits_read.handle, 1)
                dve.wait_ge(logits_read.handle, logits_read.at(1))
                first, second = choice[:, 0], choice[:, 1]
                first_of_largest(dve, link, first, scores[:, :, :], core.const["iota"], tmp[:, :, :], top[:, :])
                link(dve.tensor_reduce(best[:, 0, :], scores[:, :, :], AXIS.X, ALU.max))
                link(dve.scalar_tensor_tensor(rest[:, :, :], first, NEG, scores[:, :, :], ALU.mult, ALU.add))
                link(dve.tensor_reduce(best[:, 1, :], rest[:, :, :], AXIS.X, ALU.max))
                first_of_largest(dve, link, second, rest[:, :, :], core.const["iota"], tmp[:, :, :], top[:, :])
                dve.tensor_tensor(gap[:, :], best[:, 1, :], best[:, 0, :], ALU.subtract).then_inc(exp_in.handle, 1)
                dve.wait_ge(exp_out.handle, exp_out.at(1))
                link(dve.tensor_scalar(top[:, :], gap[:, :], 1.0, None, ALU.add))
                link(dve.reciprocal(top[:, :], top[:, :]))
                link(dve.tensor_tensor(tmp[:, :, :], second, spread(gap[:, :], 2, N), ALU.mult))
                link(dve.tensor_tensor(tmp[:, :, :], tmp[:, :, :], first, ALU.add))
                link(dve.tensor_tensor(gates[:, :, :], tmp[:, :, :], spread(top[:, :], 2, N), ALU.mult))
                dve.wait_ge(filled.handle, filled.at(1))
                bound(dve, 0, 0)
                every_step(dve, lambda e, j, turn: vector_step(dve, e, j))
                accumulate(dve, N - 2)
                accumulate(dve, N - 1)
                dve.wait_ge(y_read.handle, y_read.at(N * BATCH))
                scratch = whole[:, 0, :].rearrange("p (t d) -> p t d", t=TILES)
                link(dve.tensor_tensor(scratch, acc[:, :, :], acc[:, :, :], ALU.mult))
                link(dve.tensor_reduce(mean[:, :], scratch, AXIS.X, ALU.add))
                dve.tensor_scalar(mean[:, :], mean[:, :], 1.0 / D, 1e-6, ALU.mult, ALU.add).then_inc(mean_sq.handle, 1)
                dve.wait_ge(rstd.handle, rstd.at(1))
                link(dve.tensor_tensor(acc[:, :, :], acc[:, :, :], spread(inv_root[:, :], 2, D), ALU.mult))
                link(dve.tensor_tensor(acc[:, :, :], acc[:, :, :], spread(w[:, L3F["norm"]], 1, TILES), ALU.mult))
                link(dve.tensor_tensor(core.x[:, :, :], core.x[:, :, :], acc[:, :, :], ALU.add))
                count[0] = link.count
    norm_close(core)
    for s, total in ((logits_ps, 1), (logits_read, 1), (exp_in, 1), (exp_out, 1),
                     *[(s, 16 * N // BUFS) for s in up_in + down_in],
                     *[(s, N * C) for s in (f_ps, m_ps, bounded, exp_done, ln_done, z_done, u_done, k_done,
                                            frac_done, tanh_done, sin_done, h_done)],
                     (y_ps, N * BATCH), (y_read, N * BATCH), (chain, count[0]), (filled, 1), (mean_sq, 1), (rstd, 1)):
        s.close(total)


def constants_layout():
    at, layout = 0, {}
    for name, width in (("ident", P), ("mask_q", P), ("mask_k", P), ("keep_k", P), ("iota", 16),
                        ("rope_cos", 256), ("rope_sin", 256), ("rope_half_cos", 256), ("rope_half_sin", 256),
                        ("head_mask8", 16), ("row_mask8", 512), ("head_mask64", 8), ("row_mask64", 512),
                        ("head_mask32", 4), ("row_mask32", 128)):
        layout[name] = slice(at, at + width)
        at += width
    return layout, at


def decoder(nc, x_in, consts, packs, streamed, out):
    with ExitStack() as ctx:
        core = Core(nc, ctx)
        layout, n_consts = constants_layout()
        const = core.sbuf("constants", [P, n_consts], F32)
        core.const = {name: const[:, cols] for name, cols in layout.items()}
        core.ident, core.keep_k = core.const["ident"], core.const["keep_k"]
        core.rope_cos, core.rope_sin = core.const["rope_cos"], core.const["rope_sin"]
        core.rope_half_cos, core.rope_half_sin = core.const["rope_half_cos"], core.const["rope_half_sin"]
        core.ident_bf_t = core.sbuf("ident_bf", [P, P], BF16)
        core.mask_q_t = core.sbuf("mask_q_bf", [P, P], BF16)
        core.mask_k_t = core.sbuf("mask_k_bf", [P, P], BF16)
        core.ident_bf, core.mask_q, core.mask_k = core.ident_bf_t[:, :], core.mask_q_t[:, :], core.mask_k_t[:, :]
        loaded = ctx.enter_context(nc.semaphore("inputs_loaded"))
        made = ctx.enter_context(nc.semaphore("constants_made"))
        w, w_sem = {}, {}
        for name, ap in packs.items():
            w[name] = core.sbuf(f"w_{name}", [ap.shape[0], ap.shape[1]], F32)
            w_sem[name] = ctx.enter_context(nc.semaphore(f"loaded_{name}"))

        with nc.Block() as block:
            @block.sync
            def _(sp):
                sp.dma_start(core.x[:, :, :], x_in.rearrange("b (t p) d -> p (b t) d", p=P)).then_inc(loaded, 16)
                sp.dma_start(const[:, :], consts).then_inc(loaded, 16)
                for name, ap in packs.items():
                    sp.dma_start(w[name][:, :], ap).then_inc(w_sem[name], 16)

            @block.gpsimd
            def _(pool):
                pool.memset(core.minus_half[:, :], -0.5).then_inc(made, 1)
                pool.memset(core.ones[:, :], 1.0).then_inc(made, 1)

            @block.vector
            def _(dve):
                dve.wait_ge(loaded, 32)
                dve.tensor_copy(core.ident_bf, core.ident).then_inc(made, 1)
                dve.tensor_copy(core.mask_q, core.const["mask_q"]).then_inc(made, 1)
                dve.tensor_copy(core.mask_k, core.const["mask_k"]).then_inc(made, 1)
                dve.wait_ge(made, 5)

        core.kbd, core.vbd = {}, {}
        for cfg in CROSS:
            core.kbd[cfg.name] = core.sbuf(f"{cfg.name}_kbd", [P, BATCH, cfg.chunks, cfg.heads_per_chunk * KEYS], F32)
            core.vbd[cfg.name] = core.sbuf(f"{cfg.name}_vbd", [P, BATCH, max(cfg.chunks, cfg.prob_chunks), P], F32)
        prepare_context(core, CROSS, w, w_sem, w["context"], w_sem["context"])

        run_layers(core, w, w_sem, streamed)

        stored = ctx.enter_context(nc.semaphore("output_stored"))
        with nc.Block() as block:
            @block.sync
            def _(sp):
                sp.dma_start(out.rearrange("b (t p) d -> p (b t) d", p=P), core.x[:, :, :]).then_inc(stored, 16)
                sp.wait_ge(stored, 16)
                for name in packs:
                    sp.wait_ge(w_sem[name], 16)


CROSS = [CrossAttention("l0_xattn", 16, 8, True, True), CrossAttention("l1_xattn", 8, 64, False, False),
         CrossAttention("l2_xattn", 4, 32, False, False), CrossAttention("l3_xattn", 16, 8, True, False)]
SELF = [SelfAttention("l0_attn", "silu", True, 1.0, False),
        SelfAttention("l1_attn", "square", True, 1.0 / DH, True),
        SelfAttention("l2_attn", "plain", False, DH ** -0.5, True),
        SelfAttention("l3_attn", "rope", True, DH ** -0.5, False)]


def run_layers(core, w, w_sem, streamed):
    def attend(layer):
        self_attention(core, SELF[layer], w[SELF[layer].name], w_sem[SELF[layer].name])

    def attend_context(layer):
        cross_attention(core, CROSS[layer], w[CROSS[layer].name], w_sem[CROSS[layer].name])

    attend(0)
    attend_context(0)
    expert_feed_forward(core, w["l0_ffn"], w_sem["l0_ffn"], w["l0_ffn_b1"], w_sem["l0_ffn_b1"])
    attend(1)
    attend_context(1)
    gated_experts(core, w["l1_ffn"], w_sem["l1_ffn"], streamed["l1_w1"], streamed["l1_w2"])
    attend(2)
    attend_context(2)
    quantised_feed_forward(core, w["l2_ffn"], w_sem["l2_ffn"])
    attend(3)
    attend_context(3)
    tanh_cos_experts(core, w["l3_ffn"], w_sem["l3_ffn"], streamed["l3_up"], streamed["l3_down"])


def shape_constants():
    import numpy as np
    layout, n = constants_layout()
    c = np.zeros((P, n), np.float32)
    i = np.arange(P)
    c[:, layout["ident"]] = np.eye(P)
    c[:, layout["mask_q"]] = np.where(i[None, :] > i[:, None], NEG, 0.0)
    c[:, layout["mask_k"]] = np.where(i[None, :] < i[:, None], NEG, 0.0)
    c[:, layout["keep_k"]] = i[None, :] >= i[:, None]
    c[:, layout["iota"]] = np.arange(16)
    pos = (np.arange(TPB)[None, :, None] * P + i[:, None, None]).astype(np.float32)
    inv_freq = (1.0 / np.float32(10000.0) ** (np.arange(0, DH, 2, dtype=np.float32) / DH)).astype(np.float32)
    freqs = pos * inv_freq
    sign = np.where(np.arange(DH) % 2 == 0, -1.0, 1.0)
    for name, angles in (("rope_half", np.concatenate([freqs, freqs], -1)), ("rope", np.repeat(freqs, 2, -1))):
        for fn, f in (("cos", np.cos(angles)), ("sin", np.sin(angles) * sign)):
            c[:, layout[f"{name}_{fn}"]] = np.repeat(f[:, :, None, :], SLOTS, 2).reshape(P, -1)
    for dh, heads_per_chunk in ((8, 16), (64, 2), (32, 4)):
        c[:, layout[f"head_mask{dh}"]][:, :heads_per_chunk] = (i[:, None] // dh) == np.arange(heads_per_chunk)[None, :]
        n_cols = layout[f"row_mask{dh}"].stop - layout[f"row_mask{dh}"].start
        cols = np.arange(n_cols)
        if dh == 8:
            head_of_col, row_base = (cols % 128) // 8, 4 * (cols // 128)
        elif dh == 64:
            head_of_col, row_base = cols // 64, 4 * (cols // 256)
        else:
            head_of_col, row_base = cols // 32, 0 * cols
        c[:, layout[f"row_mask{dh}"]] = (i[:, None] // KEYS + row_base[None, :]) == head_of_col[None, :]
    return c


def packed(inputs):
    import numpy as np

    def get(name):
        return np.asarray(inputs[name])

    def rows(vector):
        return np.broadcast_to(vector.reshape(1, -1), (P, vector.size))

    def qkv(q, k, v):
        cols = []
        for g in range(HG):
            cols += [q[:, g * GH * DH:(g + 1) * GH * DH], k[:, g * GH * DH:(g + 1) * GH * DH]]
        return cols + [v]

    packs = {}
    scales = np.concatenate([get("L0_attn_q_scale").reshape(HG, GH), get("L0_attn_k_scale").reshape(HG, GH)], 1)
    packs["l0_attn"] = [*qkv(get("L0_attn_Wq").T, get("L0_attn_Wk").T, get("L0_attn_Wv").T), get("L0_attn_Wo").T,
                        rows(scales)]
    packs["l1_attn"] = [*qkv(get("L1_attn_Wq").T, get("L1_attn_Wk").T, get("L1_attn_Wv").T), get("L1_attn_Wo").T,
                        *[rows(a[0]) for a in qkv(get("L1_attn_bq")[None], get("L1_attn_bk")[None],
                                                  get("L1_attn_bv")[None])],
                        rows(np.tile(get("L1_attn_norm_w"), SLOTS))]
    packs["l2_attn"] = [*qkv(get("L2_attn_Wq"), get("L2_attn_Wk"), get("L2_attn_Wv")), get("L2_attn_Wout")]
    packs["l3_attn"] = [*qkv(get("L3_attn_qw"), get("L3_attn_kw"), get("L3_attn_vw")), get("L3_attn_ow")]
    ctx = get("ctx_768")
    by_layer = {"l0_xattn": ("L0_xattn_", False), "l1_xattn": ("L1_xattn_", False), "l2_xattn": ("L2_xattn_", True),
                "l3_xattn": ("L3_xattn_", False)}
    packs["context"] = [*[ctx[b].T for b in range(BATCH)],
                        *[ctx[b].T for b in range(BATCH) for _ in range(P // KEYS)]]
    for cfg in CROSS:
        prefix, turned = by_layer[cfg.name]
        wq, wk, wv, wo = [get(prefix + n).T if turned else get(prefix + n) for n in ("Wq", "Wk", "Wv", "Wo")]
        packs["context"] += [wk, wv]
        packs[cfg.name] = [wq, wo.reshape(cfg.chunks, P, D).transpose(1, 0, 2).reshape(P, -1), rows(get(prefix + "bo"))]
        if cfg.biased:
            packs[cfg.name] += [get(prefix + "bq").reshape(cfg.chunks, P).T, get(prefix + "bk").reshape(cfg.chunks, P).T,
                                rows(get(prefix + "bv"))]

    def chunked(a):
        return a.reshape(-1, P, a.shape[-1]).transpose(1, 0, 2).reshape(P, -1)

    packs["l0_ffn"] = [get("L0_ffn_W_router"), *list(get("L0_ffn_W1")), chunked(get("L0_ffn_Wo")),
                       *[rows(get("L0_ffn_" + n)) for n in ("bo", "ln_gamma", "ln_beta")]]
    packs["l0_ffn_b1"] = [get("L0_ffn_b1")]
    packs["l1_ffn"] = [get("L1_ffn_router_w"), rows(get("L1_ffn_router_b"))]
    packs["l2_ffn"] = [get("L2_ffn_w_gate").T, get("L2_ffn_w_up").T, chunked(get("L2_ffn_w_down").T)]
    packs["l3_ffn"] = [get("L3_ffn_router_w").T, rows(get("L3_ffn_router_bias")),
                       get("L3_ffn_bank_phase").reshape(-1, P).T, rows(get("L3_ffn_norm_w"))]
    return {name: np.ascontiguousarray(np.concatenate(cols, 1)) for name, cols in packs.items()}


def experts(inputs):
    import numpy as np

    def get(name):
        return np.asarray(inputs[name])

    def chunked(a):
        return a.reshape(a.shape[0], -1, P, a.shape[-1]).transpose(0, 2, 1, 3).reshape(a.shape[0], P, -1)

    arrays = {"l1_w1": get("L1_ffn_w1"), "l1_w2": chunked(get("L1_ffn_w2"))}

    arrays["l3_up"] = np.concatenate([get("L3_ffn_bank_freq"), get("L3_ffn_bank_mag")], 2)
    arrays["l3_down"] = chunked(get("L3_ffn_bank_down"))
    return {name: np.ascontiguousarray(a) for name, a in arrays.items()}


def kernel(**inputs):
    import numpy as np
    import concourse.bacc as bacc
    from concourse.bass_utils import run_bass_kernel_spmd

    nc = bacc.Bacc("TRN2", target_bir_lowering=False, num_devices=1)
    arrays = {"x": np.ascontiguousarray(inputs["x"]), "consts": shape_constants(), **packed(inputs)}
    by_expert = experts(inputs)
    arrays.update(by_expert)
    aps = {name: nc.dram_tensor(f"in_{name}", a.shape, mybir.dt.from_np(a.dtype), kind="ExternalInput").ap()
           for name, a in arrays.items()}
    out = nc.dram_tensor("out", (BATCH, SEQ, D), F32, kind="ExternalOutput").ap()
    x, consts = aps.pop("x"), aps.pop("consts")
    streamed = {name: aps.pop(name) for name in by_expert}
    decoder(nc, x, consts, aps, streamed, out)
    result = run_bass_kernel_spmd(nc, [{f"in_{name}": a for name, a in arrays.items()}], core_ids=[0])
    return result.results[0]["out"]
```

```python
import concourse.bass as bass
from concourse import mybir
from contextlib import ExitStack

F32 = mybir.dt.float32
BF16 = mybir.dt.bfloat16
ACT = mybir.ActivationFunctionType
ALU = mybir.AluOpType
AXIS = mybir.AxisListType

P = 128
BATCH, SEQ, D = 2, 512, 128
TILES = BATCH * SEQ // P
TPB = SEQ // P
BANK = 512
LN_EPS = 1e-5
HEADS, DH = 16, 8
GH = 4
HG = HEADS // GH
GROUPS = BATCH * HG
SLOTS = 2 * GH
PARTS = 6
SHIFT = PARTS * DH
STACK = 64
NEG = -1e30
KEYS, CTX_D = 32, 96
MAGIC = 12582912.0
BIG_INDEX = 1000.0


def spread(ap, axis, n):
    ap = ap.unsqueeze(axis)
    shape = list(ap.shape)
    shape[axis] = n
    return ap.to_broadcast(shape)


class Signal:

    def __init__(self, handle):
        self.handle, self.base = handle, 0

    def at(self, n):
        return n + self.base

    def close(self, total):
        self.base += total


class Chain:

    def __init__(self, engine, signal):
        self.engine, self.paced, self.count = engine, signal, 0

    def begin(self, instruction):
        instruction.then_inc(self.paced.handle, 1)
        self.count += 1

    def finish(self):
        self.engine.wait_ge(self.paced.handle, self.paced.at(self.count))

    def __call__(self, instruction):
        self.begin(instruction)
        self.finish()


class Core:

    def __init__(self, nc, ctx):
        self.nc, self.ctx = nc, ctx
        self.signals = {}
        self.x = self.sbuf("x_resid", [P, TILES, D], F32)
        self.xn = self.sbuf("x_normed", [P, TILES, D], F32)
        self.xnT = self.sbuf("x_normed_T", [P, TILES * P], F32)
        self.stats = self.sbuf("bn_stats", [P, TILES, 6], F32)
        self.mean_var = self.sbuf("mean_var", [P, TILES, 2], F32)
        self.var_eps = self.sbuf("var_eps", [P, TILES], F32)
        self.rstd = self.sbuf("rstd", [P, TILES], F32)
        self.minus_half = self.sbuf("minus_half", [P, 1], F32)
        self.ones = self.sbuf("ones", [P, P], F32)
        self.psum = ctx.enter_context(nc.psum_tensor("psum", [P, 8, BANK], F32))
        self.bank = [self.psum[:, i, :] for i in range(8)]

    def sbuf(self, name, shape, dt):
        return self.ctx.enter_context(self.nc.sbuf_tensor(name, shape, dt))

    def sig(self, name):
        if name not in self.signals:
            self.signals[name] = Signal(self.ctx.enter_context(self.nc.semaphore(name)))
        return self.signals[name]



def norm_vector(core, dve):
    x, mv = core.x, core.mean_var
    stats, aggr = core.sig("ln_stats"), core.sig("ln_aggr")
    var_eps, rstd, xn = core.sig("ln_var_eps"), core.sig("ln_rstd"), core.sig("ln_xn")
    for half in range(BATCH):
        tiles = range(half * TPB, (half + 1) * TPB)
        part = slice(half * TPB, (half + 1) * TPB)
        for t in tiles:
            dve.bn_stats(core.stats[:, t, :], x[:, t, :]).then_inc(stats.handle, 1)
        for t in tiles:
            dve.wait_ge(stats.handle, stats.at(t + 1))
            dve.bn_aggr(mv[:, t, :], core.stats[:, t, :]).then_inc(aggr.handle, 1)
        dve.wait_ge(aggr.handle, aggr.at((half + 1) * TPB))
        dve.tensor_scalar(core.var_eps[:, part], mv[:, part, 1], LN_EPS, None, ALU.add)\
           .then_inc(var_eps.handle, 1)
    for half in range(BATCH):
        dve.wait_ge(rstd.handle, rstd.at(half + 1))
        for t in range(half * TPB, (half + 1) * TPB):
            dve.tensor_scalar(core.xn[:, t, :], x[:, t, :], mv[:, t, 0:1], core.rstd[:, t:t + 1],
                              ALU.subtract, ALU.mult).then_inc(xn.handle, 1)


def norm_gpsimd(core, pool):
    var_eps, rstd = core.sig("ln_var_eps"), core.sig("ln_rstd")
    for half in range(BATCH):
        part = slice(half * TPB, (half + 1) * TPB)
        pool.wait_ge(var_eps.handle, var_eps.at(half + 1))
        pool.tensor_tensor(core.rstd[:, part], core.var_eps[:, part],
                           core.minus_half[:, 0:1].to_broadcast([P, TPB]), ALU.pow).then_inc(rstd.handle, 1)


def norm_tensor(core, pe):
    xn, xnT_ps = core.sig("ln_xn"), core.sig("ln_xnT_ps")
    for t in range(TILES):
        pe.wait_ge(xn.handle, xn.at(t + 1))
        last = pe.transpose(core.bank[t // TPB][:, (t % TPB) * P:(t % TPB + 1) * P],
                            core.xn[:, t, :], core.ident)
        if t % TPB == TPB - 1:
            last.then_inc(xnT_ps.handle, 1)


def norm_scalar(core, act):
    xnT_ps, xnT = core.sig("ln_xnT_ps"), core.sig("ln_xnT")
    for half in range(BATCH):
        act.wait_ge(xnT_ps.handle, xnT_ps.at(half + 1))
        act.copy(core.xnT[:, half * SEQ:(half + 1) * SEQ], core.bank[half][:, :]).then_inc(xnT.handle, 1)


def norm_close(core):
    for name, total in (("ln_stats", TILES), ("ln_aggr", TILES), ("ln_var_eps", BATCH), ("ln_rstd", BATCH),
                        ("ln_xn", TILES), ("ln_xnT_ps", BATCH), ("ln_xnT", BATCH)):
        core.sig(name).close(total)


class SelfAttention:

    def __init__(self, name, kind, causal, scale, residual_normed):
        self.name, self.kind, self.causal, self.scale = name, kind, causal, scale
        self.residual_normed = residual_normed


W_QKV, W_OUT = slice(0, 384), slice(384, 512)


def self_attention_project(core, cfg, w, w_sem, qk, v):
    nc = core.nc
    sig = core.sig
    proj, evac, norm_in, norm_out = sig("sa_proj"), sig("sa_evac"), sig("sa_norm_in"), sig("sa_norm_out")
    chain = sig("dve_chain")
    xnT, squared, tabled = sig("ln_xnT"), sig("sa_squared"), sig("sa_tabled")
    with ExitStack() as ctx:
        def sbuf(name, shape, dt=F32):
            return ctx.enter_context(nc.sbuf_tensor(f"{cfg.name}_{name}", shape, dt))
        scratch = sbuf("scratch", [P, TILES, SLOTS * HG * DH])
        norm2 = sbuf("norm2", [P, GROUPS * TPB, SLOTS])
        norm1 = sbuf("norm1", [P, GROUPS * TPB, SLOTS])
        factor = sbuf("factor", [P, GROUPS * TPB, SLOTS])
        rows = qk[:, :, :, :].rearrange("p g t (s d) -> p (g t) s d", d=DH)
        scratch_rows = scratch[:, :, :].rearrange("p t (a s d) -> p (t a) s d", s=SLOTS, d=DH)
        squares = sbuf("squares", [P, GROUPS * TPB, SLOTS, DH]) if cfg.kind == "square" else scratch_rows
        tables = sbuf("tables", [P, 2, TPB, SLOTS * DH])
        counts = {}

        def evacuated(t):
            b, tb = divmod(t, TPB)
            groups = slice(b * HG, (b + 1) * HG)
            return qk[:, groups, tb, :], v[:, groups, tb, :]

        def from_bank(t):
            ps = core.bank[2 + t % 4]
            return (ps[:, 0:256].rearrange("p (g c) -> p g c", g=HG),
                    ps[:, 256:384].rearrange("p (g c) -> p g c", g=HG))

        def head_norms(act):
            for b in range(BATCH):
                act.wait_ge(norm_in.handle, norm_in.at(b + 1))
                act.activation(norm1[:, of(b), :], norm2[:, of(b), :], ACT.Sqrt).then_inc(norm_out.handle, 1)

        def of(b):
            return slice(b * HG * TPB, (b + 1) * HG * TPB)

        def add_biases(dve, b):
            bias = w[:, 512:896]
            both = (bias[:, 0:256].rearrange("p (g c) -> p g c", g=HG),
                    bias[:, 256:384].rearrange("p (g c) -> p g c", g=HG))
            for t in range(b * TPB, (b + 1) * TPB):
                dve.wait_ge(proj.handle, proj.at(t + 1))
                for dst, src, add in zip(evacuated(t), from_bank(t), both):
                    dve.tensor_tensor(dst, src, add, ALU.add).then_inc(evac.handle, 1)

        def sum_squares(dve, link, b):
            if cfg.kind == "silu":
                link(dve.tensor_tensor(squares[:, of(b)], rows[:, of(b)], rows[:, of(b)], ALU.mult))
            else:
                dve.wait_ge(squared.handle, squared.at(b + 1))
            link(dve.tensor_reduce(factor[:, of(b), :], squares[:, of(b)], AXIS.X, ALU.add))
            if cfg.kind == "silu":
                last = dve.tensor_scalar(norm2[:, of(b), :], factor[:, of(b), :], 1e-34, None, ALU.max)
            else:
                last = dve.tensor_scalar(norm2[:, of(b), :], factor[:, of(b), :], 1.0 / DH, 2.0 ** -23,
                                         ALU.mult, ALU.add)
            last.then_inc(norm_in.handle, 1)

        def rotate(dve, link, b):
            if cfg.kind == "square":
                dve.wait_ge(tabled.handle, tabled.at(3))
                cos, sin = [tables[:, i].rearrange("p t c -> p (t c)") for i in range(2)]
            else:
                cos, sin = core.rope_cos, core.rope_sin
            groups = slice(b * HG, (b + 1) * HG)
            wide = qk[:, groups, :, :].rearrange("p g t c -> p g (t c)")
            turned = scratch[:, groups, :]
            for i in range(2):
                link(dve.tensor_tensor(turned[:, :, i::2], wide[:, :, 1 - i::2],
                                       spread(sin[:, i::2], 1, HG), ALU.mult))
            link(dve.tensor_tensor(wide, wide, spread(cos, 1, HG), ALU.mult))
            link(dve.tensor_tensor(wide, wide, turned, ALU.add))

        def scale_heads(dve, link, b):
            dve.wait_ge(norm_out.handle, norm_out.at(b + 1))
            root, square, scale = [a[:, of(b), :] for a in (norm1, norm2, factor)]
            if cfg.kind == "silu":
                link(dve.tensor_scalar(square, root, 1e-6, None, ALU.add))
                link(dve.reciprocal(scale, square))
                link(dve.tensor_tensor(scale, scale, root, ALU.mult))
                scales = w[:, 512:512 + HG * SLOTS].rearrange("p (g s) -> p g s", g=HG)
                by_group = scale.rearrange("p (g t) s -> p g t s", t=TPB)
                link(dve.tensor_tensor(by_group, by_group, spread(scales, 2, TPB), ALU.mult))
            else:
                link(dve.reciprocal(scale, root))
                link(dve.tensor_tensor(root, scale, scale, ALU.mult))
                link(dve.tensor_tensor(root, root, square, ALU.mult))
                link(dve.tensor_scalar(root, root, -0.5, 1.5, ALU.mult, ALU.add))
                link(dve.tensor_tensor(scale, scale, root, ALU.mult))
            link(dve.tensor_tensor(rows[:, of(b)], rows[:, of(b)], spread(scale, 3, DH), ALU.mult))

        with nc.Block() as block:
            @block.tensor
            def _(pe):
                norm_tensor(core, pe)
                pe.wait_ge(w_sem, 16)
                for t in range(TILES):
                    if t % TPB == 0:
                        pe.wait_ge(xnT.handle, xnT.at(t // TPB + 1))
                    if t >= 4:
                        pe.wait_ge(evac.handle, evac.at(2 * (t - 3)))
                    pe.matmul(core.bank[2 + t % 4][:, 0:384], core.xnT[:, t * P:(t + 1) * P], w[:, W_QKV],
                              start=True, stop=True).then_inc(proj.handle, 1)

            @block.scalar
            def _(act):
                norm_scalar(core, act)
                if cfg.kind == "square":
                    for b in range(BATCH):
                        act.wait_ge(evac.handle, evac.at(2 * TPB * (b + 1)))
                        act.activation(squares[:, of(b)], rows[:, of(b)], ACT.Square).then_inc(squared.handle, 1)
                    head_norms(act)
                    return
                func = ACT.Silu if cfg.kind == "silu" else ACT.Copy
                for t in range(TILES):
                    act.wait_ge(proj.handle, proj.at(t + 1))
                    for dst, src in zip(evacuated(t), from_bank(t)):
                        act.activation(dst, src, func).then_inc(evac.handle, 1)
                if cfg.kind == "silu":
                    head_norms(act)

            @block.gpsimd
            def _(pool):
                norm_gpsimd(core, pool)
                if cfg.kind == "square":
                    pool.wait_ge(w_sem, 16)
                    norm_w = w[:, 896:960]
                    sin = core.rope_half_sin.rearrange("p (t c) -> p t c", t=TPB)
                    pool.tensor_tensor(tables[:, 0], core.rope_half_cos.rearrange("p (t c) -> p t c", t=TPB),
                                       spread(norm_w, 1, TPB), ALU.mult).then_inc(tabled.handle, 1)
                    for i in range(2):
                        pool.tensor_tensor(tables[:, 1, :, i::2], sin[:, :, i::2],
                                           spread(norm_w[:, 1 - i::2], 1, TPB), ALU.mult).then_inc(tabled.handle, 1)

            @block.vector
            def _(dve):
                norm_vector(core, dve)
                link = Chain(dve, chain)
                if cfg.kind == "square":
                    dve.wait_ge(w_sem, 16)
                for b in range(BATCH):
                    if cfg.kind == "square":
                        add_biases(dve, b)
                    dve.wait_ge(evac.handle, evac.at(2 * TPB * (b + 1)))
                    if cfg.kind in ("silu", "square"):
                        sum_squares(dve, link, b)
                    if cfg.kind in ("square", "rope"):
                        rotate(dve, link, b)
                if cfg.kind in ("silu", "square"):
                    for b in range(BATCH):
                        scale_heads(dve, link, b)
                counts["chain"] = link.count
    norm_close(core)
    proj.close(TILES)
    evac.close(2 * TILES)
    if cfg.kind in ("silu", "square"):
        norm_in.close(BATCH)
        norm_out.close(BATCH)
    if cfg.kind == "square":
        squared.close(BATCH)
        tabled.close(3)
    chain.close(counts["chain"])


def self_attention_heads(core, cfg, qk, v, attn):
    nc, sig = core.nc, core.sig
    softmax = cfg.kind != "square"
    stack_k, stack_q, k_ps, q_ps = sig("sa_stack_k"), sig("sa_stack_q"), sig("sa_k_ps"), sig("sa_q_ps")
    k_ready, q_ready = sig("sa_k"), sig("sa_q")
    s_done, max_done, shift = sig("sa_scores"), sig("sa_max"), sig("sa_shift")
    q2_ps, q2_ready, st_done = sig("sa_q2_ps"), sig("sa_q2"), sig("sa_scores_T")
    exp_done, masked, pv_done = sig("sa_exp"), sig("sa_masked"), sig("sa_pv")
    o_copied, o_ps, o_done = sig("sa_o_copied"), sig("sa_o_ps"), sig("sa_o_done")
    pool_chain, dve_chain, filled, zeroed = sig("pool_chain"), sig("dve_chain"), sig("sa_filled"), sig("sa_zeroed")
    inv_done, v_ready = sig("sa_inv"), sig("sa_v")
    first_k, first_q = sig("sa_first_stack_k"), sig("sa_first_stack_q")
    CHAINED, SHIFT_CHAINED = 4, 3
    U = 2 * TPB
    S = 12 if cfg.causal else 16
    Q_READY = PARTS + (1 if softmax else 0)
    LAST = GROUPS - 1
    EARLY = 4
    OUTPUT_AT, KEYS_AT, QUERIES_AT = (1, 2, 4) if softmax else (1, 3, 6)

    with ExitStack() as ctx:
        def sbuf(name, shape, dt=F32):
            return ctx.enter_context(nc.sbuf_tensor(f"{cfg.name}_{name}", shape, dt))
        stack = [sbuf(f"stack{i}", [P, TPB, SLOTS, STACK], BF16) for i in range(2)]
        parts = sbuf("parts", [P, 3, TPB, SLOTS, DH], BF16)
        rest = sbuf("rest", [P, TPB, SLOTS, DH])
        first_parts = sbuf("first_parts", [P, 3, TPB, SLOTS, DH], BF16)
        first_rest = sbuf("first_rest", [P, TPB, SLOTS, DH])
        v_now = [sbuf(f"v_now{i}", [P, TPB, GH, 32]) for i in range(2)]
        kT = sbuf("kT", [P, 3, 2, 2, SEQ], BF16)
        qT = sbuf("qT", [P, 3, 2, SEQ], BF16)
        q2T = [sbuf(f"q2T{i}", [P, 2, SEQ], BF16) for i in range(2)]
        maxes = sbuf("maxes", [P, TPB, GH])
        shift_rest = sbuf("shift_rest", [P, TPB, GH])
        probs = [sbuf(f"probs{i}", [P, GH, SEQ]) for i in range(2)]
        oT = sbuf("oT", [P, SEQ])
        inv = sbuf("inv", [P, TPB, GH])

        def score_steps():
            steps = []
            for qt in range(TPB):
                width = (qt + 1) * P if cfg.causal else SEQ
                heads = 1 if width > BANK // 2 else 2
                steps += [(qt, h, heads, width) for h in range(0, GH, heads)]
            return steps

        def first_query(kt):
            return kt * P if cfg.causal else 0

        def steps_at(g, u, last_but):
            turn = U - EARLY // 2
            if u >= turn:
                return [(g + 2, i) for i in range(2 * (u - turn), 2 * (u - turn + 1))] if last_but >= 2 else []
            spread_over = turn - 1
            first, last = [EARLY + n * (S - EARLY) // spread_over for n in (u - 1, u)]
            return [(g + 1, i) for i in range(first, last)] if last_but >= 1 else []

        def keys_of(g, half, pair, rows, cols):
            return kT[rows, bass.ds(g % 3, 1), half, pair, cols].rearrange("p o s -> p (o s)")

        def queries_of(g, pair, cols):
            return qT[:, bass.ds(g % 3, 1), pair, cols].rearrange("p o s -> p (o s)")

        def transposed(bank):
            return core.bank[bank][:, :].bitcast(BF16).rearrange("p (a s) -> p a s", a=2)

        def wait_alone(pool, signal, n):
            pool.wait_ge(signal.handle, signal.at(n))
            pool.sem_inc(core.sig("pool_paced").handle, 1)

        def split(engine, link, g, parts, rest):
            src = qk[:, bass.ds(g, 1), :, :].rearrange("p o t (s d) -> p (o t) s d", d=DH)
            h, m, lo = parts[:, 0], parts[:, 1], parts[:, 2]
            link(engine.tensor_copy(h, src))
            link(engine.tensor_tensor(rest[:, :, :, :], src, h, ALU.subtract))
            link(engine.tensor_copy(m, rest[:, :, :, :]))
            link(engine.tensor_tensor(lo, rest[:, :, :, :], m, ALU.subtract))

        def stack_keys(dve, p, parts, done):
            h, m, lo = parts[:, 0], parts[:, 1], parts[:, 2]
            for i, part in enumerate((h, h, h, m, m, lo)):
                dve.tensor_copy(stack[p][:, :, GH:SLOTS, i * DH:(i + 1) * DH], part[:, :, GH:SLOTS, :])\
                   .then_inc(done.handle, 1)

        def stack_queries(engine, p, parts, done):
            h, m, lo = parts[:, 0], parts[:, 1], parts[:, 2]
            if softmax:
                engine.memset(stack[p][:, :, 0:GH, SHIFT:SHIFT + 3], 0.0).then_inc(done.handle, 1)
            for i, part in enumerate((h, m, lo, h, m, h)):
                engine.tensor_copy(stack[p][:, :, 0:GH, i * DH:(i + 1) * DH], part[:, :, 0:GH, :])\
                      .then_inc(done.handle, 1)

        def take_v(pool, g, p):
            if not (isinstance(g, int) and g < 2):
                wait_alone(pool, pv_done, (g - 1) * TPB)
            pool.tensor_copy(v_now[p][:, :, :, 0:DH],
                             v[:, bass.ds(g, 1), :, :].rearrange("p o t (h d) -> p (o t) h d", d=DH))\
                .then_inc(v_ready.handle, 1)

        def make_stack(pool, g, p):
            steps = [(g - 1) * CHAINED]

            def link(instruction):
                instruction.then_inc(pool_chain.handle, 1)
                steps[0] += 1
                wait_alone(pool, pool_chain, steps[0])
            later = not (isinstance(g, int) and g == 1)
            if later:
                wait_alone(pool, stack_q, (g - 1) * Q_READY)
                wait_alone(pool, stack_k, (g - 1) * PARTS)
            split(pool, link, g, parts, rest)
            take_v(pool, g - 1, 1 - p)
            if softmax:
                if later:
                    wait_alone(pool, q2_ps, g - 1)
                stack_queries(pool, p, parts, stack_q)

        def transpose_stacks(pe, bank, p, slot, done):
            for pair in range(2):
                for t in range(TPB):
                    last = pe.transpose(transposed(bank)[:, pair, t * P:(t + 1) * P],
                                        stack[p][:, t, slot + 2 * pair:slot + 2 * pair + 2, :], core.ident_bf)
            last.then_inc(done.handle, 1)

        def keys_T(pe, g, p, bank_used, n):
            if isinstance(g, int) and g == 0:
                pe.wait_ge(first_k.handle, first_k.at(PARTS))
            else:
                pe.wait_ge(stack_k.handle, stack_k.at(g * PARTS))
            if bank_used is not None:
                pe.wait_ge(bank_used.handle, bank_used.at(n))
            transpose_stacks(pe, 7, p, GH, k_ps)

        def queries_T(pe, g, p):
            if isinstance(g, int) and g == 0:
                pe.wait_ge(first_q.handle, first_q.at(Q_READY))
            else:
                pe.wait_ge(stack_q.handle, stack_q.at(g * Q_READY))
            pe.wait_ge(k_ready.handle, k_ready.at(2 * (g + 1)))
            transpose_stacks(pe, 7, p, 0, q_ps)

        def shifted_T(pe, g, p, bank_used, n):
            pe.wait_ge(shift.handle, shift.at(g + 1))
            pe.wait_ge(bank_used.handle, bank_used.at(n))
            transpose_stacks(pe, 7, p, 0, q2_ps)

        def scores(pe, g, i, first=False):
            qt, first_head, heads, width = score_steps()[i]
            if i == 0:
                pe.wait_ge(k_ready.handle, k_ready.at(2 * (g + 1)))
                pe.wait_ge(q_ready.handle, q_ready.at(g + 1))
            if not (first and i < 2):
                pe.wait_ge(max_done.handle, max_done.at(g * S + i - 1))
            for n in range(heads):
                h = first_head + n
                out = core.bank[i % 2][:, n * width:(n + 1) * width]
                last = pe.matmul(out, queries_of(g, h // 2, slice(qt * P, (qt + 1) * P)),
                                 keys_of(g, h % 2, h // 2, slice(None), slice(0, width)),
                                 start=True, stop=not cfg.causal)
                if cfg.causal:
                    last = pe.matmul(out[:, width - P:width], core.ident_bf, core.mask_q, start=False, stop=True)
            last.then_inc(s_done.handle, 1)

        def scores_T(pe, g, p, u, first):
            kt, pair = divmod(u, 2)
            if u == 0:
                if softmax:
                    pe.wait_ge(q2_ready.handle, q2_ready.at(g + 1))
                else:
                    pe.wait_ge(k_ready.handle, k_ready.at(2 * (g + 1)))
                    pe.wait_ge(q_ready.handle, q_ready.at(g + 1))
            if not (first and u < 2):
                pe.wait_ge(exp_done.handle, exp_done.at(g * U + u - 1))
            q_from = first_query(kt)
            for half in range(2):
                src = q2T[p][:, pair, q_from:SEQ] if softmax else queries_of(g, pair, slice(q_from, SEQ))
                out = core.bank[2 + 2 * (u % 2) + half]
                masked_here = cfg.causal and softmax
                last = pe.matmul(out[:, 0:SEQ - q_from],
                                 keys_of(g, half, pair, slice(None), slice(kt * P, (kt + 1) * P)), src,
                                 start=True, stop=not masked_here)
                if masked_here:
                    last = pe.matmul(out[:, 0:P], core.ident_bf, core.mask_k, start=False, stop=True)
            last.then_inc(st_done.handle, 1)

        def values(pe, g, p, kt, first):
            if softmax:
                pe.wait_ge(exp_done.handle, exp_done.at(g * U + 2 * kt + 2))
            else:
                pe.wait_ge(masked.handle, masked.at(g * U + 2 * kt + 2))
            if kt == 0:
                pe.wait_ge(v_ready.handle, v_ready.at(g + 1))
            if kt == 0 and not first:
                pe.wait_ge(o_copied.handle, o_copied.at(g))
            q_from = first_query(kt)
            for h in range(GH):
                last = pe.matmul(core.bank[6][32 * h:32 * h + 32, q_from:SEQ], v_now[p][:, kt, h, :],
                                 probs[kt % 2][:, h, q_from:SEQ], start=kt == 0, stop=kt == TPB - 1,
                                 tile_position=(0, 32 * h))
            last.then_inc(pv_done.handle, 1)

        def output_T(pe, g, bank_used=None, n=0):
            pe.wait_ge(o_copied.handle, o_copied.at(g + 1))
            if bank_used is not None:
                pe.wait_ge(bank_used.handle, bank_used.at(n))
            for t in range(TPB):
                last = pe.transpose(core.bank[7][:, t * P:(t + 1) * P], oT[:, t * P:(t + 1) * P], core.ident)
            last.then_inc(o_ps.handle, 1)

        def tensor_group(pe, g, p, last_but=9, first=False):
            for u in range(1, U):
                scores_T(pe, g, p, u, first)
                for step in steps_at(g, u, last_but) if softmax else ():
                    scores(pe, *step)
                if u == OUTPUT_AT and not first:
                    if softmax:
                        output_T(pe, g - 1)
                    elif last_but >= 1:
                        output_T(pe, g - 1, q_ready, g + 2)
                    else:
                        output_T(pe, g - 1, o_done, g - 1)
                if u == KEYS_AT and last_but >= 2:
                    if not first:
                        keys_T(pe, g + 2, p, o_done, g)
                    else:
                        keys_T(pe, g + 2, p, q_ready, 2)
                if u == QUERIES_AT and last_but >= 2:
                    queries_T(pe, g + 2, p)
                if u == U - EARLY // 2 and softmax and last_but >= 1:
                    shifted_T(pe, g + 1, 1 - p, *((q_ready, g + 3) if last_but >= 2 else (o_done, g)))
                if u % 2 == 1 and u > 1:
                    values(pe, g, p, u // 2 - 1, first)
            if last_but >= 1:
                scores_T(pe, g + 1, 1 - p, 0, False)
            values(pe, g, p, TPB - 1, first)

        def weights(act, g, u):
            kt, pair = divmod(u, 2)
            act.wait_ge(st_done.handle, st_done.at(g * U + u + 1))
            if not (isinstance(g, int) and g == 0 and kt < 2):
                act.wait_ge(pv_done.handle, pv_done.at(g * TPB + kt - 1))
            q_from = first_query(kt)
            width = SEQ - q_from
            b0 = 2 + 2 * (u % 2)
            src = core.psum[:, b0:b0 + 2, 0:width]
            act.activation(probs[kt % 2][:, 2 * pair:2 * pair + 2, q_from:SEQ], src,
                           ACT.Exp if softmax else ACT.Square, scale=cfg.scale).then_inc(exp_done.handle, 1)

        def copy_keys(act, g):
            act.wait_ge(k_ps.handle, k_ps.at(g + 1))
            for half in range(2):
                rows = slice(half * STACK, (half + 1) * STACK)
                act.copy(kT[rows, bass.ds(g % 3, 1), half, :, :].rearrange("p o a s -> p (o a) s"),
                         transposed(7)[rows, :, :]).then_inc(k_ready.handle, 1)

        def copy_queries(act, g):
            act.wait_ge(q_ps.handle, q_ps.at(g + 1))
            act.copy(qT[:, bass.ds(g % 3, 1), :, :].rearrange("p o a s -> p (o a) s"), transposed(7))\
               .then_inc(q_ready.handle, 1)

        def scalar_group(act, g, last_but=9):
            for u in range(1, U):
                weights(act, g, u)
                if u == KEYS_AT and last_but >= 2:
                    copy_keys(act, g + 2)
                if u == QUERIES_AT and last_but >= 2:
                    copy_queries(act, g + 2)
            if last_but >= 1:
                weights(act, g + 1, 0)
            act.wait_ge(pv_done.handle, pv_done.at((g + 1) * TPB))
            act.copy(oT[:, :], core.bank[6][:, :]).then_inc(o_copied.handle, 1)

        def maxima(dve, g, i):
            qt, h, heads, width = score_steps()[i]
            dve.wait_ge(s_done.handle, s_done.at(g * S + i + 1))
            if i == 0 and not (isinstance(g, int) and g == 0):
                dve.wait_ge(shift.handle, shift.at(g))
            dve.tensor_reduce(maxes[:, qt, h:h + heads],
                              core.bank[i % 2][:, 0:heads * width].rearrange("p (h w) -> p h w", h=heads),
                              AXIS.X, ALU.max).then_inc(max_done.handle, 1)

        def make_shift(dve, g, p):
            link = Chain(dve, dve_chain)
            link.count = CHAINED + g * SHIFT_CHAINED
            dve.wait_ge(max_done.handle, max_done.at((g + 1) * S))
            high, mid, low = [stack[p][:, :, 0:GH, SHIFT + i] for i in range(3)]
            link(dve.tensor_scalar(high, maxes[:, :, :], -1.0, None, ALU.mult))
            link(dve.scalar_tensor_tensor(shift_rest[:, :, :], maxes[:, :, :], -1.0, high, ALU.mult, ALU.subtract))
            link(dve.tensor_copy(mid, shift_rest[:, :, :]))
            dve.tensor_tensor(low, shift_rest[:, :, :], mid, ALU.subtract).then_inc(shift.handle, 1)

        def copy_shifted(dve, g, p):
            dve.wait_ge(q2_ps.handle, q2_ps.at(g + 1))
            dve.tensor_copy(q2T[p][:, :, :], transposed(7)).then_inc(q2_ready.handle, 1)

        def finish(dve, g):
            dve.wait_ge(o_ps.handle, o_ps.at(g + 1))
            out = core.bank[7][:, :].rearrange("p (t h c) -> p t h c", t=TPB, h=GH)
            start = g % HG + (g // HG) * (HG * TPB)
            dst = attn[:, bass.ds(start, TPB, HG), :].rearrange("p t (h d) -> p t h d", d=DH)
            if softmax:
                dve.reciprocal(inv[:, :, :], out[:, :, :, DH]).then_inc(inv_done.handle, 1)
                dve.wait_ge(inv_done.handle, inv_done.at(g + 1))
                dve.tensor_tensor(dst, out[:, :, :, 0:DH], spread(inv[:, :, :], 3, DH), ALU.mult)\
                   .then_inc(o_done.handle, 1)
            else:
                dve.tensor_copy(dst, out[:, :, :, 0:DH]).then_inc(o_done.handle, 1)

        def mask_squares(dve, g, u):
            kt, pair = divmod(u, 2)
            dve.wait_ge(exp_done.handle, exp_done.at(g * U + u + 1))
            at = probs[kt % 2][:, 2 * pair:2 * pair + 2, kt * P:(kt + 1) * P]
            dve.tensor_tensor(at, at, spread(core.keep_k, 1, 2), ALU.mult).then_inc(masked.handle, 1)

        def vector_keys(dve, g, p):
            dve.wait_ge(pool_chain.handle, pool_chain.at(g * CHAINED))
            if not (isinstance(g, int) and g < 2):
                dve.wait_ge(k_ps.handle, k_ps.at(g - 1))
            stack_keys(dve, p, parts, stack_k)
            if not softmax:
                if not (isinstance(g, int) and g < 2):
                    dve.wait_ge(q_ps.handle, q_ps.at(g - 1))
                stack_queries(dve, p, parts, stack_q)

        def vector_group(dve, g, p, last_but=9, first=False):
            if last_but >= 2:
                vector_keys(dve, g + 2, p)
            if not softmax:
                mask_squares(dve, g, 0)
            for u in range(1, U):
                if not softmax:
                    mask_squares(dve, g, u)
                if softmax and u == U - EARLY // 2 and last_but >= 1:
                    make_shift(dve, g + 1, 1 - p)
                for step in steps_at(g, u, last_but) if softmax else ():
                    maxima(dve, *step)
                if softmax and u == U - EARLY // 2 and last_but >= 1:
                    copy_shifted(dve, g + 1, 1 - p)
                if u == OUTPUT_AT and not first:
                    finish(dve, g - 1)

        with nc.Block() as block:
            @block.gpsimd
            def _(pool):
                for p in range(2):
                    pool.memset(stack[p][:, :, :, SHIFT:STACK], 0.0).then_inc(filled.handle, 1)
                    pool.memset(v_now[p][:, :, :, DH:32], 0.0).then_inc(filled.handle, 1)
                pool.wait_ge(filled.handle, filled.at(4))
                for p in range(2):
                    pool.memset(stack[p][:, :, GH:SLOTS, SHIFT:SHIFT + 3], 1.0).then_inc(filled.handle, 1)
                    pool.memset(v_now[p][:, :, :, DH:DH + 1], 1.0).then_inc(filled.handle, 1)
                pool.wait_ge(filled.handle, filled.at(8))
                make_stack(pool, 1, 1)
                make_stack(pool, 2, 0)
                with pool.Fori(1, GROUPS // 2 - 1) as i:
                    make_stack(pool, i * 2 + 1, 1)
                    make_stack(pool, i * 2 + 2, 0)
                make_stack(pool, LAST, 1)
                take_v(pool, LAST, 1)

            @block.tensor
            def _(pe):
                pe.wait_ge(filled.handle, filled.at(8))
                keys_T(pe, 0, 0, None, 0)
                queries_T(pe, 0, 0)
                pe.wait_ge(zeroed.handle, zeroed.at(6))
                for i in range(S if softmax else 0):
                    scores(pe, 0, i, True)
                    if i == 1:
                        keys_T(pe, 1, 1, q_ready, 1)
                    if i == 5:
                        queries_T(pe, 1, 1)
                if not softmax:
                    keys_T(pe, 1, 1, q_ready, 1)
                    queries_T(pe, 1, 1)
                if softmax:
                    for i in range(EARLY):
                        scores(pe, 1, i)
                        if i == 1:
                            shifted_T(pe, 0, 0, q_ready, 2)
                scores_T(pe, 0, 0, 0, True)
                tensor_group(pe, 0, 0, first=True)
                tensor_group(pe, 1, 1)
                with pe.Fori(1, GROUPS // 2 - 1) as i:
                    for p in range(2):
                        tensor_group(pe, i * 2 + p, p)
                tensor_group(pe, LAST - 1, 0, 1)
                tensor_group(pe, LAST, 1, 0)
                output_T(pe, LAST, o_done, LAST)

            @block.scalar
            def _(act):
                for g in range(2):
                    copy_keys(act, g)
                    copy_queries(act, g)
                weights(act, 0, 0)
                scalar_group(act, 0)
                scalar_group(act, 1)
                with act.Fori(1, GROUPS // 2 - 1) as i:
                    for p in range(2):
                        scalar_group(act, i * 2 + p)
                scalar_group(act, LAST - 1, 1)
                scalar_group(act, LAST, 0)

            @block.vector
            def _(dve):
                link = Chain(dve, dve_chain)
                split(dve, link, 0, first_parts, first_rest)
                dve.wait_ge(filled.handle, filled.at(8))
                stack_keys(dve, 0, first_parts, first_k)
                stack_queries(dve, 0, first_parts, first_q)
                for i in range(3):
                    for half in range(2):
                        other = slice((1 - half) * STACK, (2 - half) * STACK)
                        dve.memset(kT[other, i, half, :, :], 0.0).then_inc(zeroed.handle, 1)
                vector_keys(dve, 1, 1)
                if softmax:
                    for i in range(S):
                        maxima(dve, 0, i)
                    make_shift(dve, 0, 0)
                    for i in range(EARLY):
                        maxima(dve, 1, i)
                        if i == 1:
                            copy_shifted(dve, 0, 0)
                vector_group(dve, 0, 0, first=True)
                vector_group(dve, 1, 1)
                with dve.Fori(1, GROUPS // 2 - 1) as i:
                    for p in range(2):
                        vector_group(dve, i * 2 + p, p)
                vector_group(dve, LAST - 1, 0, 1)
                vector_group(dve, LAST, 1, 0)
                finish(dve, LAST)

    for s, total in ((stack_k, LAST * PARTS), (stack_q, LAST * Q_READY), (first_k, PARTS), (first_q, Q_READY),
                     (k_ps, GROUPS), (q_ps, GROUPS),
                     (k_ready, 2 * GROUPS), (q_ready, GROUPS), (st_done, GROUPS * U), (exp_done, GROUPS * U),
                     (pv_done, GROUPS * TPB), (o_copied, GROUPS), (o_ps, GROUPS), (o_done, GROUPS),
                     (v_ready, GROUPS), (filled, 8), (zeroed, 6), (pool_chain, LAST * CHAINED)):
        s.close(total)
    if softmax:
        for s, total in ((s_done, GROUPS * S), (max_done, GROUPS * S), (shift, GROUPS), (q2_ps, GROUPS),
                         (q2_ready, GROUPS), (inv_done, GROUPS)):
            s.close(total)
    else:
        masked.close(GROUPS * U)
    dve_chain.close(CHAINED + (GROUPS * SHIFT_CHAINED if softmax else 0))


def self_attention_out(core, cfg, w, attn):
    nc, sig = core.nc, core.sig
    ps, attnT_ready, done, added = sig("so_ps"), sig("so_attnT"), sig("so_done"), sig("so_added")
    with nc.sbuf_tensor(f"{cfg.name}_attnT", [P, TILES * P], F32) as attnT, nc.Block() as block:
        @block.tensor
        def _(pe):
            for b in range(BATCH):
                for t in range(TPB):
                    last = pe.transpose(core.bank[b][:, t * P:(t + 1) * P],
                                        attn[:, (b * TPB + t) * HG:(b * TPB + t + 1) * HG, :],
                                        core.ident)
                last.then_inc(ps.handle, 1)
            for b in range(BATCH):
                pe.wait_ge(attnT_ready.handle, attnT_ready.at(b + 1))
                for t in range(TPB):
                    at = (b * TPB + t) * P
                    last = pe.matmul(core.bank[2 + b][:, t * P:(t + 1) * P], attnT[:, at:at + P], w[:, W_OUT],
                                     start=True, stop=True)
                last.then_inc(done.handle, 1)

        @block.scalar
        def _(act):
            for b in range(BATCH):
                act.wait_ge(ps.handle, ps.at(b + 1))
                act.copy(attnT[:, b * SEQ:(b + 1) * SEQ], core.bank[b][:, :]).then_inc(attnT_ready.handle, 1)

        @block.vector
        def _(dve):
            if cfg.residual_normed:
                dve.tensor_tensor(core.x[:, :, :], core.x[:, :, :], core.xn[:, :, :], ALU.add)\
                   .then_inc(added.handle, 1)
                dve.wait_ge(added.handle, added.at(1))
            for b in range(BATCH):
                dve.wait_ge(done.handle, done.at(b + 1))
                xb = core.x[:, b * TPB:(b + 1) * TPB, :]
                dve.tensor_tensor(xb, xb, core.bank[2 + b][:, :].rearrange("p (t d) -> p t d", t=TPB),
                                  ALU.add).then_inc(added.handle, 1)
    ps.close(BATCH)
    attnT_ready.close(BATCH)
    done.close(BATCH)
    added.close(BATCH + (1 if cfg.residual_normed else 0))


def self_attention(core, cfg, w, w_sem):
    with core.nc.sbuf_tensor(f"{cfg.name}_qk", [P, GROUPS, TPB, SLOTS * DH], F32) as qk, \
            core.nc.sbuf_tensor(f"{cfg.name}_v", [P, GROUPS, TPB, GH * DH], F32) as v, \
            core.nc.sbuf_tensor(f"{cfg.name}_attn", [P, TILES * HG, GH * DH], F32) as attn:
        self_attention_project(core, cfg, w, w_sem, qk, v)
        self_attention_heads(core, cfg, qk, v, attn)
        self_attention_out(core, cfg, w, attn)


class CrossAttention:

    def __init__(self, name, heads, dh, biased, guarded):
        self.name, self.heads, self.dh, self.biased, self.guarded = name, heads, dh, biased, guarded
        self.inner = heads * dh
        self.chunks = self.inner // P
        self.heads_per_chunk = P // dh
        self.prob_chunks = heads * KEYS // P
        self.scale = dh ** -0.5
        at, self.cols = 0, {}
        for part, width in (("wq", self.inner), ("wo", self.inner), ("bo", D), ("bq", self.chunks),
                            ("bk", self.chunks), ("bv", self.inner)):
            if part in ("bq", "bk", "bv") and not biased:
                continue
            self.cols[part] = slice(at, at + width)
            at += width

    def prob_chunks_of(self, c):
        if self.chunks == 1:
            return range(self.prob_chunks)
        return [c * self.heads_per_chunk // (P // KEYS)]

    def v_block(self, c, pk):
        return pk if self.chunks == 1 else c


def prepare_context(core, cfgs, w, w_sem, ctx_w, ctx_sem):
    nc, sig = core.nc, core.sig
    k_done, v_done, chain = sig("cx_k"), sig("cx_v"), sig("dve_chain")
    v_copied, v_biased, v_made = sig("cx_v_copied"), sig("cx_v_biased"), sig("cx_v_made")
    ctxT, ctx4 = ctx_w[:, 0:BATCH * KEYS], ctx_w[:, BATCH * KEYS:BATCH * KEYS + BATCH * P]
    at = BATCH * KEYS + BATCH * P
    wk, wv = {}, {}
    for cfg in cfgs:
        wk[cfg.name] = ctx_w[:, at:at + cfg.inner]
        wv[cfg.name] = ctx_w[:, at + cfg.inner:at + 2 * cfg.inner]
        at += 2 * cfg.inner
    k_ps, v_ps, k_at, v_at = {}, {}, 0, 0
    for cfg in cfgs:
        k_ps[cfg.name] = core.bank[0][:, k_at:k_at + cfg.chunks * BATCH * KEYS]
        k_at += cfg.chunks * BATCH * KEYS
        for b in range(BATCH):
            v_ps[cfg.name, b] = core.bank[3 + b][:, :] if cfg.inner == BANK \
                else core.bank[1 + b][:, v_at:v_at + cfg.inner]
        v_at += 0 if cfg.inner == BANK else cfg.inner
    with nc.sbuf_tensor("cx_k_rows", [P, len(cfgs), 4, BATCH * KEYS], F32) as k_rows, \
            nc.sbuf_tensor("cx_v_rows", [P, len(cfgs), BATCH, BANK], F32) as v_rows, nc.Block() as block:
        count = [0]
        on_gpsimd, on_vector = range(0, 2), range(2, len(cfgs))
        biased = [n for n in on_gpsimd if cfgs[n].biased]

        @block.tensor
        def _(pe):
            pe.wait_ge(ctx_sem, 16)
            for cfg in cfgs:
                for c in range(cfg.chunks):
                    last = pe.matmul(k_ps[cfg.name][:, c * BATCH * KEYS:(c + 1) * BATCH * KEYS],
                                     wk[cfg.name][:, c * P:(c + 1) * P], ctxT, start=True, stop=True)
                last.then_inc(k_done.handle, 1)
                for b in range(BATCH):
                    last = pe.matmul(v_ps[cfg.name, b], ctx4[:, b * P:(b + 1) * P], wv[cfg.name],
                                     start=True, stop=True)
                last.then_inc(v_done.handle, 1)

        @block.scalar
        def _(act):
            act.wait_ge(v_done.handle, v_done.at(len(cfgs)))
            for n, cfg in enumerate(cfgs):
                for b in range(BATCH):
                    act.copy(v_rows[:, n, b, 0:cfg.inner], v_ps[cfg.name, b]).then_inc(v_copied.handle, 1)

        def mask_values(engine, n, b):
            cfg = cfgs[n]
            rows = v_rows[:, n, b, 0:cfg.inner]
            mask = core.const[f"row_mask{cfg.dh}"].rearrange("p (a c) -> p a c", c=P)
            rows = spread(rows, 1, cfg.prob_chunks) if cfg.chunks == 1 else rows.rearrange("p (a c) -> p a c", c=P)
            return engine.tensor_tensor(core.vbd[cfg.name][:, b, :, :], rows, mask, ALU.mult)

        def add_value_bias(engine, n, b):
            rows = v_rows[:, n, b, 0:cfgs[n].inner]
            return engine.tensor_tensor(rows, rows, w[cfgs[n].name][:, cfgs[n].cols["bv"]], ALU.add)

        @block.gpsimd
        def _(pool):
            for n in on_gpsimd:
                for b in range(BATCH):
                    pool.wait_ge(v_copied.handle, v_copied.at(n * BATCH + b + 1))
                    if cfgs[n].biased:
                        pool.wait_ge(w_sem[cfgs[n].name], 16)
                        add_value_bias(pool, n, b).then_inc(v_biased.handle, 1)
                        pool.wait_ge(v_biased.handle, v_biased.at(biased.index(n) * BATCH + b + 1))
                    mask_values(pool, n, b).then_inc(v_made.handle, 1)

        @block.vector
        def _(dve):
            link = Chain(dve, chain)
            dve.wait_ge(k_done.handle, k_done.at(len(cfgs)))
            for n, cfg in enumerate(cfgs):
                pack, cols = w[cfg.name], cfg.cols
                dve.wait_ge(w_sem[cfg.name], 16)
                for c in range(cfg.chunks):
                    src = k_ps[cfg.name][:, c * BATCH * KEYS:(c + 1) * BATCH * KEYS]
                    if cfg.biased:
                        bk = pack[:, cols["bk"].start + c:cols["bk"].start + c + 1]
                        link.begin(dve.tensor_scalar(k_rows[:, n, c, :], src, bk, cfg.scale, ALU.add, ALU.mult))
                    else:
                        link.begin(dve.tensor_scalar(k_rows[:, n, c, :], src, cfg.scale, None, ALU.mult))
            link.finish()
            for n, cfg in enumerate(cfgs):
                hc = cfg.heads_per_chunk
                for c in range(cfg.chunks):
                    for b in range(BATCH):
                        link.begin(dve.tensor_tensor(
                            core.kbd[cfg.name][:, b, c, :].rearrange("p (h k) -> p h k", h=hc),
                            spread(k_rows[:, n, c, b * KEYS:(b + 1) * KEYS], 1, hc),
                            spread(core.const[f"head_mask{cfg.dh}"][:, 0:hc], 2, KEYS), ALU.mult))
            for n in on_vector:
                dve.wait_ge(v_copied.handle, v_copied.at((n + 1) * BATCH))
                if cfgs[n].biased:
                    for b in range(BATCH):
                        link.begin(add_value_bias(dve, n, b))
                    link.finish()
                for b in range(BATCH):
                    link.begin(mask_values(dve, n, b))
            link.finish()
            count[0] = link.count
    k_done.close(len(cfgs))
    v_done.close(len(cfgs))
    for s, total in ((v_copied, len(cfgs) * BATCH), (v_biased, len(biased) * BATCH), (v_made, len(on_gpsimd) * BATCH)):
        s.close(total)
    chain.close(count[0])


def cross_attention(core, cfg, w, w_sem):
    nc, sig = core.nc, core.sig
    H, C, PK = cfg.heads, cfg.chunks, cfg.prob_chunks
    q_ps, q_ready, s_ps, clip_done, minus_max = (sig("xa_q_ps"), sig("xa_q"), sig("xa_scores"), sig("xa_clip"),
                                                 sig("xa_minus_max"))
    top_done, x_biased = sig("xa_top"), sig("xa_x_biased")
    exp_done, inv_done, prob, pT_ps, pT_ready = (sig("xa_exp"), sig("xa_inv"), sig("xa_prob"), sig("xa_pT_ps"),
                                                 sig("xa_pT"))
    o_ps, o_ready, out_ps, out_read, chain = (sig("xa_o_ps"), sig("xa_o"), sig("xa_out_ps"), sig("xa_out_read"),
                                              sig("dve_chain"))
    nan_in, nan_ps, replaced, xnT = sig("xa_nan_in"), sig("xa_nan_ps"), sig("xa_replaced"), sig("ln_xnT")
    kbd, vbd, cols = core.kbd[cfg.name], core.vbd[cfg.name], cfg.cols
    WIDTH = H * KEYS
    STEPS = TILES + 4
    count = [0]
    with ExitStack() as ctx:
        def sbuf(name, shape, dt=F32):
            return ctx.enter_context(nc.sbuf_tensor(f"{cfg.name}_{name}", shape, dt))
        qT = sbuf("qT", [P, C, TILES * P])
        clipped = sbuf("clipped", [P, 2, WIDTH])
        top = sbuf("top", [P, TILES, H])
        probs = sbuf("probs", [P, TILES, H, KEYS])
        sums = sbuf("sums", [P, TILES, H])
        inv = sbuf("inv", [P, TILES, H])
        pT = sbuf("pT", [P, PK, TILES * P])
        oT = sbuf("oT", [P, C, TILES * P])
        odd = sbuf("odd", [P, TILES * H])
        odd_rows = sbuf("odd_rows", [P, 1])
        verdict = sbuf("verdict", [P, 1 + BATCH])
        share = sbuf("share", [P, 1])

        def by_head(at):
            return at.rearrange("p (h k) -> p h k", h=H)

        def queries(pe, half):
            pe.wait_ge(xnT.handle, xnT.at(half + 1))
            for c in range(C):
                n = half * C + c
                if n >= 4:
                    pe.wait_ge(q_ready.handle, q_ready.at(n - 3))
                pe.matmul(core.bank[2 + n % 4], w[:, cols["wq"]][:, c * P:(c + 1) * P],
                          core.xnT[:, half * SEQ:(half + 1) * SEQ], start=True, stop=True).then_inc(q_ps.handle, 1)

        def scores(pe, t):
            b = t // TPB
            pe.wait_ge(q_ready.handle, q_ready.at((b + 1) * C))
            if t >= 2:
                read = clip_done if cfg.guarded else minus_max
                pe.wait_ge(read.handle, read.at(t - 1))
            width = WIDTH // C
            for c in range(C):
                last = pe.matmul(core.bank[6 + t % 2][:, c * width:(c + 1) * width],
                                 qT[:, c, t * P:(t + 1) * P], kbd[:, b, c, :], start=True, stop=True)
            last.then_inc(s_ps.handle, 1)

        def probs_T(pe, t):
            pe.wait_ge(prob.handle, prob.at(t + 1))
            if t >= 2:
                pe.wait_ge(pT_ready.handle, pT_ready.at(t - 1))
            for k in range(PK):
                last = pe.transpose(core.bank[t % 2][:, k * P:(k + 1) * P],
                                    probs[:, t, k * 4:(k + 1) * 4, :].rearrange("p h k -> p (h k)"), core.ident)
            last.then_inc(pT_ps.handle, 1)

        def head_outputs(pe, t):
            pe.wait_ge(pT_ready.handle, pT_ready.at(t + 1))
            if t == 0:
                pe.wait_ge(q_ready.handle, q_ready.at(BATCH * C))
            if t >= 2:
                pe.wait_ge(o_ready.handle, o_ready.at(t - 1))
            for c in range(C):
                chunks = list(cfg.prob_chunks_of(c))
                for k in chunks:
                    last = pe.matmul(core.bank[2 + t % 2][:, c * P:(c + 1) * P],
                                     vbd[:, t // TPB, cfg.v_block(c, k), :], pT[:, k, t * P:(t + 1) * P],
                                     start=k == chunks[0], stop=k == chunks[-1])
            last.then_inc(o_ps.handle, 1)

        def project(pe, t):
            pe.wait_ge(o_ready.handle, o_ready.at(t + 1))
            if t >= 2:
                pe.wait_ge(out_read.handle, out_read.at(t - 1))
            for c in range(C):
                last = pe.matmul(core.bank[4 + t % 2][:, 0:D], oT[:, c, t * P:(t + 1) * P],
                                 w[:, cols["wo"]][:, c * D:(c + 1) * D], start=c == 0, stop=c == C - 1)
            last.then_inc(out_ps.handle, 1)

        def project_queries(act, n):
            half, c = divmod(n, C)
            act.wait_ge(q_ps.handle, q_ps.at(n + 1))
            dst, src = qT[:, c, half * SEQ:(half + 1) * SEQ], core.bank[2 + n % 4]
            if cfg.biased:
                at = cols["bq"].start + c
                act.activation(dst, src, ACT.Identity, bias=w[:, at:at + 1]).then_inc(q_ready.handle, 1)
            else:
                act.copy(dst, src).then_inc(q_ready.handle, 1)

        def maxima(dve, link, t):
            dve.wait_ge(s_ps.handle, s_ps.at(t + 1))
            src = core.bank[6 + t % 2][:, 0:WIDTH]
            if cfg.guarded:
                if t >= 2:
                    dve.wait_ge(minus_max.handle, minus_max.at(t - 1))
                dve.tensor_scalar(clipped[:, t % 2, :], src, -1e4, 1e4, ALU.max, ALU.min)\
                   .then_inc(clip_done.handle, 1)
                dve.wait_ge(clip_done.handle, clip_done.at(t + 1))
                src = clipped[:, t % 2, :]
            dve.tensor_reduce(top[:, t, :], by_head(src), AXIS.X, ALU.max).then_inc(top_done.handle, 1)
            if not cfg.guarded:
                dve.wait_ge(top_done.handle, top_done.at(t + 1))
                dve.tensor_tensor(probs[:, t, :, :], by_head(src), spread(top[:, t, :], 2, KEYS), ALU.subtract)\
                   .then_inc(minus_max.handle, 1)

        def inverse_sums(dve, link, t):
            dve.wait_ge(exp_done.handle, exp_done.at(t + 1))
            link(dve.tensor_reduce(sums[:, t, :], probs[:, t, :, :], AXIS.X, ALU.add))
            dve.reciprocal(inv[:, t, :], sums[:, t, :]).then_inc(inv_done.handle, 1)

        def add(dve, t):
            if t == 0:
                dve.wait_ge(x_biased.handle, x_biased.at(1))
            dve.wait_ge(out_ps.handle, out_ps.at(t + 1))
            dve.tensor_tensor(core.x[:, t, :], core.x[:, t, :], core.bank[4 + t % 2][:, 0:D], ALU.add)\
               .then_inc(out_read.handle, 1)

        def replace(dve, link):
            all_sums = sums[:, :, :].rearrange("p t h -> p (t h)")
            link(dve.memset(share[:, :], 1.0 / KEYS))
            link(dve.tensor_tensor(odd[:, :], all_sums, all_sums, ALU.not_equal))
            dve.tensor_reduce(odd_rows[:, :], odd[:, :], AXIS.X, ALU.max).then_inc(nan_in.handle, 1)
            dve.wait_ge(nan_ps.handle, nan_ps.at(1))
            link(dve.tensor_copy(verdict[:, :], core.bank[6][:, 0:1 + BATCH]))
            flag = verdict[:, 0:1].bitcast(mybir.dt.uint32)
            for b in range(BATCH):
                dve.wait_ge(o_ready.handle, o_ready.at((b + 1) * TPB))
                dve.copy_predicated(oT[:, 0, b * SEQ:(b + 1) * SEQ], flag.to_broadcast([P, SEQ]),
                                    verdict[:, 1 + b:2 + b].to_broadcast([P, SEQ])).then_inc(replaced.handle, 1)

        with nc.Block() as block:
            @block.tensor
            def _(pe):
                norm_tensor(core, pe)
                pe.wait_ge(w_sem, 16)
                queries(pe, 0)
                for step in range(STEPS):
                    if step == 2:
                        queries(pe, 1)
                    if step < TILES:
                        scores(pe, step)
                    if 0 <= step - 2 < TILES:
                        probs_T(pe, step - 2)
                    if 0 <= step - 3 < TILES:
                        head_outputs(pe, step - 3)
                    if not cfg.guarded and step >= 4:
                        project(pe, step - 4)
                if cfg.guarded:
                    pe.wait_ge(nan_in.handle, nan_in.at(1))
                    pe.matmul(core.bank[6][:, 0:1], core.ones[:, :], odd_rows[:, :], start=True, stop=True)
                    for b in range(BATCH):
                        for k in range(PK):
                            last = pe.matmul(core.bank[6][:, 1 + b:2 + b], vbd[:, b, k, :], share[:, :],
                                             start=k == 0, stop=k == PK - 1)
                    last.then_inc(nan_ps.handle, 1)
                    for t in range(TILES):
                        pe.wait_ge(replaced.handle, replaced.at(t // TPB + 1))
                        project(pe, t)

            @block.gpsimd
            def _(pool):
                norm_gpsimd(core, pool)
                pool.wait_ge(core.sig("ln_xn").handle, core.sig("ln_xn").at(TILES))
                pool.wait_ge(w_sem, 16)
                pool.tensor_tensor(core.x[:, :, :], core.x[:, :, :], spread(w[:, cols["bo"]], 1, TILES), ALU.add)\
                    .then_inc(x_biased.handle, 1)
                for step in range(TILES + 1):
                    if cfg.guarded and step < TILES:
                        pool.wait_ge(top_done.handle, top_done.at(step + 1))
                        pool.tensor_tensor(probs[:, step, :, :], by_head(clipped[:, step % 2, :]),
                                           spread(top[:, step, :], 2, KEYS), ALU.subtract)\
                            .then_inc(minus_max.handle, 1)
                    if step >= 1:
                        t = step - 1
                        pool.wait_ge(inv_done.handle, inv_done.at(t + 1))
                        pool.tensor_tensor(probs[:, t, :, :], probs[:, t, :, :], spread(inv[:, t, :], 2, KEYS),
                                           ALU.mult).then_inc(prob.handle, 1)

            @block.scalar
            def _(act):
                norm_scalar(core, act)
                for n in range(C):
                    project_queries(act, n)
                for step in range(STEPS):
                    if step == 2:
                        for n in range(C, BATCH * C):
                            project_queries(act, n)
                    if step < TILES:
                        act.wait_ge(minus_max.handle, minus_max.at(step + 1))
                        act.activation(probs[:, step, :, :], probs[:, step, :, :], ACT.Exp)\
                           .then_inc(exp_done.handle, 1)
                    if 0 <= step - 2 < TILES:
                        t = step - 2
                        act.wait_ge(pT_ps.handle, pT_ps.at(t + 1))
                        act.copy(pT[:, :, t * P:(t + 1) * P],
                                 core.bank[t % 2][:, 0:PK * P].rearrange("p (k c) -> p k c", k=PK))\
                           .then_inc(pT_ready.handle, 1)
                    if 0 <= step - 3 < TILES:
                        t = step - 3
                        act.wait_ge(o_ps.handle, o_ps.at(t + 1))
                        act.copy(oT[:, :, t * P:(t + 1) * P],
                                 core.bank[2 + t % 2][:, 0:C * P].rearrange("p (c s) -> p c s", c=C))\
                           .then_inc(o_ready.handle, 1)

            @block.vector
            def _(dve):
                norm_vector(core, dve)
                link = Chain(dve, chain)
                for step in range(STEPS):
                    if step < TILES:
                        maxima(dve, link, step)
                    if 0 <= step - 1 < TILES:
                        inverse_sums(dve, link, step - 1)
                    if not cfg.guarded and step >= 4:
                        add(dve, step - 4)
                if cfg.guarded:
                    dve.wait_ge(inv_done.handle, inv_done.at(TILES))
                    replace(dve, link)
                    for t in range(TILES):
                        add(dve, t)
                count[0] = link.count
    norm_close(core)
    for s, total in ((q_ps, BATCH * C), (q_ready, BATCH * C), (s_ps, TILES), (minus_max, TILES), (inv_done, TILES), (top_done, TILES), (x_biased, 1),
                     (exp_done, TILES), (prob, TILES), (pT_ps, TILES), (pT_ready, TILES),
                     (o_ps, TILES), (o_ready, TILES), (out_ps, TILES), (out_read, TILES), (chain, count[0])):
        s.close(total)
    if cfg.guarded:
        for s, total in ((clip_done, TILES), (nan_in, 1), (nan_ps, 1), (replaced, BATCH)):
            s.close(total)


def first_of_largest(dve, link, onehot, scores, iota, tmp, top):
    n = scores.shape[2]
    indices = spread(iota[:, 0:n], 1, TILES)
    link(dve.tensor_reduce(top, scores, AXIS.X, ALU.max))
    link(dve.tensor_tensor(tmp, scores, spread(top, 2, n), ALU.is_lt))
    link(dve.scalar_tensor_tensor(tmp, tmp, BIG_INDEX, indices, ALU.mult, ALU.add))
    link(dve.tensor_reduce(top, tmp, AXIS.X, ALU.min))
    link(dve.tensor_tensor(onehot, tmp, spread(top, 2, n), ALU.is_equal))


def router_tensor(core, pe, router, n, done, bank=2):
    xnT = core.sig("ln_xnT")
    for t in range(TILES):
        if t % TPB == 0:
            pe.wait_ge(xnT.handle, xnT.at(t // TPB + 1))
        last = pe.matmul(core.bank[bank][:, t * n:(t + 1) * n], core.xnT[:, t * P:(t + 1) * P], router,
                         start=True, stop=True)
    last.then_inc(done.handle, 1)


L0_EXPERTS, L0_INNER = 4, 512
L0F = {"router": slice(0, 4), "w1": slice(4, 2052), "wo": slice(2052, 2564), "bo": slice(2564, 2692),
       "gamma": slice(2692, 2820), "beta": slice(2820, 2948)}


def expert_feed_forward(core, w, w_sem, b1, b1_sem):
    nc, sig = core.nc, core.sig
    E, C = L0_EXPERTS, L0_INNER // P
    logits_ps, picked, masked = sig("f0_logits"), sig("f0_picked"), sig("f0_masked")
    mT_ps, mT_ready, oT_ps, oT_ready = sig("f0_mT_ps"), sig("f0_mT"), sig("f0_oT_ps"), sig("f0_oT")
    h_ps, h_ready, y_ps = sig("f0_h_ps"), sig("f0_h"), sig("f0_y_ps")
    var_eps, rstd, chain = sig("f0_var_eps"), sig("f0_rstd"), sig("dve_chain")
    count = [0]
    with ExitStack() as ctx:
        def sbuf(name, shape, dt=F32):
            return ctx.enter_context(nc.sbuf_tensor(f"l0_ffn_{name}", shape, dt))
        onehot = sbuf("onehot", [P, TILES, E])
        tmp = sbuf("tmp", [P, TILES, E])
        top = sbuf("top", [P, TILES])
        masked_x = sbuf("masked_x", [P, E, TILES, D])
        masked_xT = sbuf("masked_xT", [P, E, TILES * P])
        onehotT = sbuf("onehotT", [E, TILES * P])
        hT = sbuf("hT", [P, C, TILES * P])
        y = sbuf("y", [P, TILES, D])
        y_stats = sbuf("y_stats", [P, TILES, 6])
        y_mv = sbuf("y_mv", [P, TILES, 2])
        y_var = sbuf("y_var", [P, TILES])
        y_rstd = sbuf("y_rstd", [P, TILES])

        with nc.Block() as block:
            @block.tensor
            def _(pe):
                norm_tensor(core, pe)
                pe.wait_ge(w_sem, 16)
                router_tensor(core, pe, w[:, L0F["router"]], E, logits_ps)
                pe.wait_ge(picked.handle, picked.at(1))
                for b in range(BATCH):
                    for t in range(TPB):
                        last = pe.transpose(core.bank[2 + b][0:E, t * P:(t + 1) * P],
                                            onehot[:, b * TPB + t, :], core.ident)
                    last.then_inc(oT_ps.handle, 1)
                for e in range(E):
                    pe.wait_ge(masked.handle, masked.at(e + 1))
                    for b in range(BATCH):
                        n = e * BATCH + b
                        if n >= 2:
                            pe.wait_ge(mT_ready.handle, mT_ready.at(n - 1))
                        for t in range(TPB):
                            last = pe.transpose(core.bank[b][:, t * P:(t + 1) * P],
                                                masked_x[:, e, b * TPB + t, :], core.ident)
                        last.then_inc(mT_ps.handle, 1)
                pe.wait_ge(mT_ready.handle, mT_ready.at(E * BATCH))
                pe.wait_ge(oT_ready.handle, oT_ready.at(BATCH))
                pe.wait_ge(b1_sem, 16)
                for c in range(C):
                    for b in range(BATCH):
                        n = c * BATCH + b
                        if n >= 4:
                            pe.wait_ge(h_ready.handle, h_ready.at(n - 3))
                        out = core.bank[4 + n % 4]
                        cols = slice(b * SEQ, (b + 1) * SEQ)
                        for e in range(E):
                            at = e * L0_INNER + c * P
                            pe.matmul(out, w[:, L0F["w1"]][:, at:at + P], masked_xT[:, e, cols],
                                      start=e == 0, stop=False)
                        pe.matmul(out, b1[:, c * P:(c + 1) * P], onehotT[:, cols], start=False, stop=True)\
                          .then_inc(h_ps.handle, 1)
                pe.wait_ge(h_ready.handle, h_ready.at(C * BATCH))
                for b in range(BATCH):
                    for t in range(TPB):
                        at = (b * TPB + t) * P
                        for c in range(C):
                            last = pe.matmul(core.bank[2 + b][:, t * P:(t + 1) * P], hT[:, c, at:at + P],
                                             w[:, L0F["wo"]][:, c * D:(c + 1) * D], start=c == 0, stop=c == C - 1)
                    last.then_inc(y_ps.handle, 1)

            @block.gpsimd
            def _(pool):
                norm_gpsimd(core, pool)
                pool.wait_ge(var_eps.handle, var_eps.at(1))
                pool.tensor_tensor(y_rstd[:, :], y_var[:, :], core.minus_half[:, 0:1].to_broadcast([P, TILES]),
                                   ALU.pow).then_inc(rstd.handle, 1)

            @block.scalar
            def _(act):
                norm_scalar(core, act)
                for b in range(BATCH):
                    act.wait_ge(oT_ps.handle, oT_ps.at(b + 1))
                    act.copy(onehotT[:, b * SEQ:(b + 1) * SEQ], core.bank[2 + b][0:E, :])\
                       .then_inc(oT_ready.handle, 1)
                for n in range(L0_EXPERTS * BATCH):
                    e, b = divmod(n, BATCH)
                    act.wait_ge(mT_ps.handle, mT_ps.at(n + 1))
                    act.copy(masked_xT[:, e, b * SEQ:(b + 1) * SEQ], core.bank[b]).then_inc(mT_ready.handle, 1)
                for n in range(C * BATCH):
                    c, b = divmod(n, BATCH)
                    act.wait_ge(h_ps.handle, h_ps.at(n + 1))
                    act.activation(hT[:, c, b * SEQ:(b + 1) * SEQ], core.bank[4 + n % 4], ACT.Gelu)\
                       .then_inc(h_ready.handle, 1)

            @block.vector
            def _(dve):
                norm_vector(core, dve)
                link = Chain(dve, chain)
                dve.wait_ge(logits_ps.handle, logits_ps.at(1))
                first_of_largest(dve, link, onehot[:, :, :],
                                 core.bank[2][:, 0:TILES * E].rearrange("p (t e) -> p t e", t=TILES),
                                 core.const["iota"], tmp[:, :, :], top[:, :])
                dve.memset(y_var[:, :], 0.0).then_inc(picked.handle, 1)
                for e in range(E):
                    dve.tensor_tensor(masked_x[:, e, :, :], core.xn[:, :, :], spread(onehot[:, :, e], 2, D),
                                      ALU.mult).then_inc(masked.handle, 1)
                link(dve.tensor_tensor(y[:, :, :], core.xn[:, :, :], spread(w[:, L0F["bo"]], 1, TILES), ALU.add))
                for b in range(BATCH):
                    dve.wait_ge(y_ps.handle, y_ps.at(b + 1))
                    yb = y[:, b * TPB:(b + 1) * TPB, :]
                    link(dve.tensor_tensor(yb, yb, core.bank[2 + b].rearrange("p (t d) -> p t d", t=TPB), ALU.add))
                for t in range(TILES):
                    link.begin(dve.bn_stats(y_stats[:, t, :], y[:, t, :]))
                link.finish()
                for t in range(TILES):
                    link.begin(dve.bn_aggr(y_mv[:, t, :], y_stats[:, t, :]))
                link.finish()
                dve.wait_ge(picked.handle, picked.at(1))
                dve.tensor_scalar(y_var[:, :], y_mv[:, :, 1], 1e-12, None, ALU.add).then_inc(var_eps.handle, 1)
                dve.wait_ge(rstd.handle, rstd.at(1))
                for t in range(TILES):
                    link.begin(dve.tensor_scalar(y[:, t, :], y[:, t, :], y_mv[:, t, 0:1], y_rstd[:, t:t + 1],
                                                 ALU.subtract, ALU.mult))
                link.finish()
                link(dve.tensor_tensor(y[:, :, :], y[:, :, :], spread(w[:, L0F["gamma"]], 1, TILES), ALU.mult))
                link(dve.tensor_tensor(y[:, :, :], y[:, :, :], spread(w[:, L0F["beta"]], 1, TILES), ALU.add))
                link(dve.tensor_tensor(core.x[:, :, :], core.x[:, :, :], y[:, :, :], ALU.add))
                count[0] = link.count
    norm_close(core)
    for s, total in ((logits_ps, 1), (picked, 1), (masked, E), (mT_ps, E * BATCH), (mT_ready, E * BATCH),
                     (oT_ps, BATCH), (oT_ready, BATCH), (h_ps, C * BATCH), (h_ready, C * BATCH), (y_ps, BATCH),
                     (var_eps, 1), (rstd, 1), (chain, count[0])):
        s.close(total)


L1_EXPERTS, L1_INNER = 8, 512
L1F = {"router": slice(0, 9), "bias": slice(9, 18)}


def gated_experts(core, w, w_sem, w1_dram, w2_dram):
    nc, sig = core.nc, core.sig
    E, N, C = L1_EXPERTS, L1_EXPERTS + 1, L1_INNER // P
    logits_ps, exp_in, exp_out, gates_ready = sig("f1_logits"), sig("f1_exp_in"), sig("f1_exp_out"), sig("f1_gates")
    w1_in, w2_in = [sig("f1_w1_even"), sig("f1_w1_odd")], [sig("f1_w2_even"), sig("f1_w2_odd")]
    up_ps, h_ready, y_ps, y_read, chain = sig("f1_up_ps"), sig("f1_h"), sig("f1_y_ps"), sig("f1_y_read"), sig("dve_chain")
    count = [0]
    with ExitStack() as ctx:
        def sbuf(name, shape, dt=F32):
            return ctx.enter_context(nc.sbuf_tensor(f"l1_ffn_{name}", shape, dt))
        w1 = [sbuf(f"w1_{i}", [P, L1_INNER]) for i in range(2)]
        w2 = [sbuf(f"w2_{i}", [P, C * D]) for i in range(2)]
        hT = [sbuf(f"hT{i}", [P, C, TILES * P]) for i in range(2)]
        probs = sbuf("probs", [P, TILES, N])
        rest = sbuf("rest", [P, TILES, N])
        tmp = sbuf("tmp", [P, TILES, N])
        choice = sbuf("choice", [P, 2, TILES, N])
        top = sbuf("top", [P, TILES])
        gates = sbuf("gates", [P, TILES, N])
        acc = sbuf("acc", [P, TILES, D])

        def load(sp, e, p, later=False):
            if later:
                sp.wait_ge(up_ps.handle, up_ps.at((e - 1) * C))
            sp.dma_start(w1[p][:, :], w1_dram[bass.ds(e, 1), :, :].rearrange("o p c -> (o p) c"))\
              .then_inc(w1_in[p].handle, 16)
            if later:
                sp.wait_ge(y_ps.handle, y_ps.at((e - 1) * BATCH))
            sp.dma_start(w2[p][:, :], w2_dram[bass.ds(e, 1), :, :].rearrange("o p c -> (o p) c"))\
              .then_inc(w2_in[p].handle, 16)

        def up(pe, e, p, half_e, first=False):
            pe.wait_ge(w1_in[p].handle, w1_in[p].at(16 * (half_e + 1)))
            for c in range(C):
                if not (first and c < 2):
                    pe.wait_ge(h_ready.handle, h_ready.at(e * C + c - 1))
                for b in range(BATCH):
                    last = pe.matmul(core.bank[2 + 2 * (c % 2) + b], w1[p][:, c * P:(c + 1) * P],
                                     core.xnT[:, b * SEQ:(b + 1) * SEQ], start=True, stop=True)
                last.then_inc(up_ps.handle, 1)

        def down(pe, e, p, half_e, first=False):
            pe.wait_ge(w2_in[p].handle, w2_in[p].at(16 * (half_e + 1)))
            pe.wait_ge(h_ready.handle, h_ready.at((e + 1) * C))
            for b in range(BATCH):
                if not first:
                    pe.wait_ge(y_read.handle, y_read.at((e - 1) * BATCH + b + 1))
                for t in range(TPB):
                    at = (b * TPB + t) * P
                    for c in range(C):
                        last = pe.matmul(core.bank[6 + b][:, t * P:(t + 1) * P], hT[p][:, c, at:at + P],
                                         w2[p][:, c * D:(c + 1) * D], start=c == 0, stop=c == C - 1)
                last.then_inc(y_ps.handle, 1)

        def gelu(act, e, p, no_down=False):
            if not no_down:
                act.wait_ge(y_ps.handle, y_ps.at((e - 1) * BATCH))
            for c in range(C):
                act.wait_ge(up_ps.handle, up_ps.at(e * C + c + 1))
                act.activation(hT[p][:, c, :].rearrange("p (b s) -> p b s", b=BATCH),
                               core.psum[:, 2 + 2 * (c % 2):4 + 2 * (c % 2), :], ACT.Gelu).then_inc(h_ready.handle, 1)

        def accumulate(dve, e):
            for b in range(BATCH):
                dve.wait_ge(y_ps.handle, y_ps.at(e * BATCH + b + 1))
                for t in range(TPB):
                    at = acc[:, b * TPB + t, :]
                    last = dve.scalar_tensor_tensor(at, core.bank[6 + b][:, t * P:(t + 1) * P],
                                                    gates[:, b * TPB + t, bass.ds(e, 1)], at, ALU.mult, ALU.add)
                last.then_inc(y_read.handle, 1)
                dve.wait_ge(y_read.handle, y_read.at(e * BATCH + b + 1))

        with nc.Block() as block:
            @block.sync
            def _(sp):
                load(sp, 0, 0)
                load(sp, 1, 1)
                with sp.Fori(1, E // 2) as i:
                    for p in range(2):
                        load(sp, i * 2 + p, p, later=True)

            @block.tensor
            def _(pe):
                norm_tensor(core, pe)
                pe.wait_ge(w_sem, 16)
                router_tensor(core, pe, w[:, L1F["router"]], N, logits_ps)
                pe.wait_ge(exp_in.handle, exp_in.at(1))
                up(pe, 0, 0, 0, first=True)
                up(pe, 1, 1, 0)
                down(pe, 0, 0, 0, first=True)
                with pe.Fori(1, E // 2) as i:
                    up(pe, i * 2, 0, i)
                    down(pe, i * 2 - 1, 1, i - 1)
                    up(pe, i * 2 + 1, 1, i)
                    down(pe, i * 2, 0, i)
                down(pe, E - 1, 1, E // 2 - 1)

            @block.gpsimd
            def _(pool):
                norm_gpsimd(core, pool)

            @block.scalar
            def _(act):
                norm_scalar(core, act)
                act.wait_ge(exp_in.handle, exp_in.at(1))
                act.activation(probs[:, :, :], probs[:, :, :], ACT.Exp).then_inc(exp_out.handle, 1)
                gelu(act, 0, 0, no_down=True)
                gelu(act, 1, 1, no_down=True)
                with act.Fori(1, E // 2) as i:
                    gelu(act, i * 2, 0)
                    gelu(act, i * 2 + 1, 1)

            @block.vector
            def _(dve):
                norm_vector(core, dve)
                link = Chain(dve, chain)
                dve.wait_ge(logits_ps.handle, logits_ps.at(1))
                scores = core.bank[2][:, 0:TILES * N].rearrange("p (t e) -> p t e", t=TILES)
                link(dve.tensor_tensor(rest[:, :, :], scores, spread(w[:, L1F["bias"]], 1, TILES), ALU.add))
                link(dve.tensor_reduce(top[:, :], rest[:, :, :], AXIS.X, ALU.max))
                dve.tensor_tensor(probs[:, :, :], rest[:, :, :], spread(top[:, :], 2, N), ALU.subtract)\
                   .then_inc(exp_in.handle, 1)
                dve.wait_ge(exp_out.handle, exp_out.at(1))
                link(dve.tensor_reduce(top[:, :], probs[:, :, :], AXIS.X, ALU.add))
                link(dve.reciprocal(top[:, :], top[:, :]))
                link(dve.tensor_tensor(probs[:, :, :], probs[:, :, :], spread(top[:, :], 2, N), ALU.mult))
                first, second = choice[:, 0], choice[:, 1]
                first_of_largest(dve, link, first, probs[:, :, :], core.const["iota"], tmp[:, :, :], top[:, :])
                link(dve.scalar_tensor_tensor(rest[:, :, :], first, -BIG_INDEX, probs[:, :, :], ALU.mult, ALU.add))
                first_of_largest(dve, link, second, rest[:, :, :], core.const["iota"], tmp[:, :, :], top[:, :])
                link(dve.tensor_tensor(tmp[:, :, :], first, second, ALU.add))
                link(dve.tensor_tensor(gates[:, :, :], tmp[:, :, :], probs[:, :, :], ALU.mult))
                link(dve.tensor_tensor(acc[:, :, :], core.xn[:, :, :], spread(gates[:, :, E], 2, D), ALU.mult))
                with dve.Fori(0, E // 2) as i:
                    for p in range(2):
                        accumulate(dve, i * 2 + p)
                link(dve.tensor_tensor(core.x[:, :, :], core.x[:, :, :], acc[:, :, :], ALU.add))
                count[0] = link.count
    norm_close(core)
    for s, total in ((logits_ps, 1), (exp_in, 1), (exp_out, 1), (w1_in[0], 16 * E // 2), (w1_in[1], 16 * E // 2),
                     (w2_in[0], 16 * E // 2), (w2_in[1], 16 * E // 2), (up_ps, E * C), (h_ready, E * C),
                     (y_ps, E * BATCH), (y_read, E * BATCH), (chain, count[0])):
        s.close(total)


L2_INNER = 512
L2F = {"gate": slice(0, 512), "up": slice(512, 1024), "down": slice(1024, 1536)}


def quantised_feed_forward(core, w, w_sem):
    nc, sig = core.nc, core.sig
    C = L2_INNER // P
    sums_in, sums_ps, wq_ready, xq_ready = sig("f2_sums"), sig("f2_sums_ps"), sig("f2_wq"), sig("f2_xq")
    xT_ps, xT_ready, gu_ps, gate_ready, gu_read = (sig("f2_xT_ps"), sig("f2_xT"), sig("f2_gu_ps"),
                                                   sig("f2_gate"), sig("f2_gu_read"))
    hq_ready, hT_ps, hT_ready, y_ps, scaled = sig("f2_hq"), sig("f2_hT_ps"), sig("f2_hT"), sig("f2_y_ps"), sig("f2_scaled")
    chain, x_gate_ready = sig("dve_chain"), sig("f2_x_gate")
    count = [0]
    with ExitStack() as ctx:
        def sbuf(name, shape, dt=F32):
            return ctx.enter_context(nc.sbuf_tensor(f"l2_ffn_{name}", shape, dt))
        sizes = sbuf("sizes", [P, 3])
        means = sbuf("means", [P, 3])
        w_scale = sbuf("w_scale", [P, 3])
        rounded = sbuf("rounded", [P, 3, 512])
        wq = sbuf("wq", [P, 3, 512], BF16)
        x_top = sbuf("x_top", [P, TILES])
        x_scale = sbuf("x_scale", [P, TILES])
        x_unit = sbuf("x_unit", [P, TILES])
        x_gate = sbuf("x_gate", [P, TILES])
        x_up = sbuf("x_up", [P, TILES])
        x_round = sbuf("x_round", [P, TILES, D])
        xq = sbuf("xq", [P, TILES, D], BF16)
        xqT = sbuf("xqT", [P, TILES * P], BF16)
        gate = sbuf("gate", [P, TILES, L2_INNER])
        h = sbuf("h", [P, TILES, L2_INNER])
        h_top = sbuf("h_top", [P, TILES])
        h_scale = sbuf("h_scale", [P, TILES])
        h_unit = sbuf("h_unit", [P, TILES])
        hq = sbuf("hq", [P, TILES, L2_INNER], BF16)
        hqT = sbuf("hqT", [P, TILES, C, P], BF16)

        def scales(dve, link, top, scale, unit, src):
            link(dve.tensor_reduce(top, src, AXIS.X, ALU.max, apply_absolute_value=True))
            link(dve.tensor_scalar(top, top, 1e-5, None, ALU.max))
            link.begin(dve.reciprocal(scale, top))
            link(dve.tensor_scalar(unit, top, 1.0 / 127.0, None, ALU.mult))
            link(dve.tensor_scalar(scale, scale, 127.0, None, ALU.mult))

        def quantise(dve, link, scale, src, rounded_at, dst, ready):
            tiles = src.shape[1]
            for t in range(tiles):
                link.begin(dve.tensor_scalar(rounded_at[:, t], src[:, t], scale[:, t:t + 1], MAGIC, ALU.mult, ALU.add))
            link.finish()
            link(dve.tensor_scalar(rounded_at, rounded_at, -MAGIC, 127.0, ALU.add, ALU.min))
            dve.tensor_scalar(dst, rounded_at, -128.0, None, ALU.max).then_inc(ready.handle, tiles)

        def earlier_pair(t):
            return (t - 3, t - 2) if t % 2 == 1 and t >= 3 else ()

        def down(pe, t):
            pe.wait_ge(hq_ready.handle, hq_ready.at(t + 1))
            if t >= 2:
                pe.wait_ge(scaled.handle, scaled.at(t - 1))
            flat = core.bank[6 + t % 2].bitcast(BF16)
            for c in range(C):
                last = pe.transpose(flat[:, c * P:(c + 1) * P], hq[:, t, c * P:(c + 1) * P], core.ident_bf)
            last.then_inc(hT_ps.handle, 1)
            pe.wait_ge(hT_ready.handle, hT_ready.at(t + 1))
            for c in range(C):
                last = pe.matmul(core.bank[t % 2][:, 0:D], hqT[:, t, c, :], wq[:, 2, c * D:(c + 1) * D],
                                 start=c == 0, stop=c == C - 1)
            last.then_inc(y_ps.handle, 1)

        def hidden_T(act, t):
            act.wait_ge(hT_ps.handle, hT_ps.at(t + 1))
            act.copy(hqT[:, t, :, :], core.bank[6 + t % 2].bitcast(BF16)[:, 0:L2_INNER]
                     .rearrange("p (c t) -> p c t", c=C)).then_inc(hT_ready.handle, 1)

        def output(dve, link, t):
            link(dve.tensor_scalar(h_unit[:, t:t + 1], h_unit[:, t:t + 1], means[:, 2:3], None, ALU.mult))
            dve.wait_ge(y_ps.handle, y_ps.at(t + 1))
            dve.scalar_tensor_tensor(core.x[:, t, :], core.bank[t % 2][:, 0:D], h_unit[:, t:t + 1],
                                     core.x[:, t, :], ALU.mult, ALU.add).then_inc(scaled.handle, 1)

        with nc.Block() as block:
            @block.tensor
            def _(pe):
                norm_tensor(core, pe)
                pe.wait_ge(sums_in.handle, sums_in.at(1))
                pe.matmul(core.bank[2][:, 0:3], core.ones[:, :], sizes[:, :], start=True, stop=True)\
                  .then_inc(sums_ps.handle, 1)
                for t in range(TILES):
                    pe.wait_ge(xq_ready.handle, xq_ready.at(t + 1))
                    if t == 0:
                        pe.wait_ge(core.sig("ln_xnT").handle, core.sig("ln_xnT").at(BATCH))
                    out = core.bank[t // TPB].bitcast(BF16)
                    last = pe.transpose(out[:, (t % TPB) * P:(t % TPB + 1) * P], xq[:, t, :], core.ident_bf)
                    if t % TPB == TPB - 1:
                        last.then_inc(xT_ps.handle, 1)
                pe.wait_ge(wq_ready.handle, wq_ready.at(3))
                for t in range(TILES):
                    pe.wait_ge(xT_ready.handle, xT_ready.at(t // TPB + 1))
                    if t >= 2:
                        pe.wait_ge(gu_read.handle, gu_read.at(t - 1))
                    for k in range(2):
                        last = pe.matmul(core.bank[2 + 2 * (t % 2) + k], xqT[:, t * P:(t + 1) * P], wq[:, k, :],
                                         start=True, stop=True)
                    last.then_inc(gu_ps.handle, 1)
                    for before in earlier_pair(t):
                        down(pe, before)
                for t in (TILES - 2, TILES - 1):
                    down(pe, t)

            @block.gpsimd
            def _(pool):
                norm_gpsimd(core, pool)

            @block.scalar
            def _(act):
                norm_scalar(core, act)
                for b in range(BATCH):
                    act.wait_ge(xT_ps.handle, xT_ps.at(b + 1))
                    act.copy(xqT[:, b * SEQ:(b + 1) * SEQ], core.bank[b].bitcast(BF16)[:, 0:SEQ])\
                       .then_inc(xT_ready.handle, 1)
                act.wait_ge(x_gate_ready.handle, x_gate_ready.at(1))
                for t in range(TILES):
                    act.wait_ge(gu_ps.handle, gu_ps.at(t + 1))
                    act.activation(gate[:, t, :], core.bank[2 + 2 * (t % 2)], ACT.Silu, scale=x_gate[:, t:t + 1])\
                       .then_inc(gate_ready.handle, 1)
                    for before in earlier_pair(t):
                        hidden_T(act, before)
                for t in (TILES - 2, TILES - 1):
                    hidden_T(act, t)

            @block.vector
            def _(dve):
                link = Chain(dve, chain)
                dve.wait_ge(w_sem, 16)
                w3 = w[:, :].rearrange("p (k c) -> p k c", k=3)
                dve.tensor_reduce(sizes[:, :], w3, AXIS.X, ALU.add, apply_absolute_value=True)\
                   .then_inc(sums_in.handle, 1)
                norm_vector(core, dve)
                dve.wait_ge(sums_ps.handle, sums_ps.at(1))
                link(dve.tensor_scalar(means[:, :], core.bank[2][:, 0:3], 1.0 / (P * 512), 1e-5, ALU.mult, ALU.max))
                link(dve.reciprocal(w_scale[:, :], means[:, :]))
                for k in range(3):
                    link(dve.tensor_scalar(rounded[:, k, :], w3[:, k, :], w_scale[:, k:k + 1], MAGIC, ALU.mult, ALU.add))
                    link(dve.tensor_scalar(rounded[:, k, :], rounded[:, k, :], -MAGIC, 1.0, ALU.add, ALU.min))
                    dve.tensor_scalar(wq[:, k, :], rounded[:, k, :], -1.0, None, ALU.max).then_inc(wq_ready.handle, 1)
                xn_done = core.sig("ln_xn")
                dve.wait_ge(xn_done.handle, xn_done.at(TILES))
                scales(dve, link, x_top[:, :], x_scale[:, :], x_unit[:, :], core.xn[:, :, :])
                for b in range(BATCH):
                    tiles = slice(b * TPB, (b + 1) * TPB)
                    quantise(dve, link, x_scale[:, tiles], core.xn[:, tiles, :], x_round[:, tiles, :],
                             xq[:, tiles, :], xq_ready)
                dve.tensor_scalar(x_gate[:, :], x_unit[:, :], means[:, 0:1], None, ALU.mult)\
                   .then_inc(x_gate_ready.handle, 1)
                link(dve.tensor_scalar(x_up[:, :], x_unit[:, :], means[:, 1:2], None, ALU.mult))
                for t in range(TILES):
                    dve.wait_ge(gate_ready.handle, gate_ready.at(t + 1))
                    dve.scalar_tensor_tensor(h[:, t, :], core.bank[3 + 2 * (t % 2)], x_up[:, t:t + 1],
                                             gate[:, t, :], ALU.mult, ALU.mult).then_inc(gu_read.handle, 1)
                    if t % 2 == 1:
                        pair = slice(t - 1, t + 1)
                        dve.wait_ge(gu_read.handle, gu_read.at(t + 1))
                        scales(dve, link, h_top[:, pair], h_scale[:, pair], h_unit[:, pair], h[:, pair, :])
                        quantise(dve, link, h_scale[:, pair], h[:, pair, :], h[:, pair, :], hq[:, pair, :], hq_ready)
                        for before in earlier_pair(t):
                            output(dve, link, before)
                for t in (TILES - 2, TILES - 1):
                    output(dve, link, t)
                count[0] = link.count

    norm_close(core)
    for s, total in ((sums_in, 1), (x_gate_ready, 1), (sums_ps, 1), (wq_ready, 3), (xq_ready, TILES), (xT_ps, BATCH), (xT_ready, BATCH),
                     (gu_ps, TILES), (gate_ready, TILES), (gu_read, TILES), (hq_ready, TILES), (hT_ps, TILES),
                     (hT_ready, TILES), (y_ps, TILES), (scaled, TILES), (chain, count[0])):
        s.close(total)


L3_EXPERTS, L3_INNER = 16, 256
L3F = {"router": slice(0, 16), "bias": slice(16, 32), "phase": slice(32, 64), "norm": slice(64, 192)}
TURN = 6.283185307179586
SIN_SCALE = 6.2831850

SURE = 25.0


def tanh_cos_experts(core, w, w_sem, up_dram, down_dram):
    nc, sig = core.nc, core.sig
    N = L3_EXPERTS
    C = L3_INNER // P
    BUFS = 4
    logits_ps, logits_read, exp_in, exp_out = sig("f3_logits"), sig("f3_logits_read"), sig("f3_exp_in"), sig("f3_exp_out")
    up_in, down_in = [[sig(f"f3_{name}{i}") for i in range(BUFS)] for name in ("up", "down")]
    f_ps, m_ps, bounded, exp_done, ln_done = sig("f3_f_ps"), sig("f3_m_ps"), sig("f3_bounded"), sig("f3_exp"), sig("f3_ln")
    z_done, u_done, k_done, frac_done = sig("f3_z"), sig("f3_u"), sig("f3_k"), sig("f3_frac")
    tanh_done, sin_done, h_done = sig("f3_tanh"), sig("f3_sin"), sig("f3_h")
    y_ps, y_read, chain, filled = sig("f3_y_ps"), sig("f3_y_read"), sig("dve_chain"), sig("f3_filled")
    mean_sq, rstd = sig("f3_mean_sq"), sig("f3_rstd")
    count = [0]
    with ExitStack() as ctx:
        def sbuf(name, shape, dt=F32):
            return ctx.enter_context(nc.sbuf_tensor(f"l3_ffn_{name}", shape, dt))
        w_up = [sbuf(f"w_up{i}", [P, 2 * C * P]) for i in range(BUFS)]
        w_down = [sbuf(f"w_down{i}", [P, C * D]) for i in range(BUFS)]
        angle = [sbuf(f"angle{i}", [P, C, TILES * P]) for i in range(2)]
        whole = sbuf("whole", [P, C, TILES * P])
        sine = sbuf("sine", [P, C, TILES * P])
        hidden = [sbuf(f"hidden{i}", [P, C, TILES * P]) for i in range(BUFS)]
        phase = sbuf("phase", [P, N * C])
        scores = sbuf("scores", [P, TILES, N])
        rest = sbuf("rest", [P, TILES, N])
        tmp = sbuf("tmp", [P, TILES, N])
        choice = sbuf("choice", [P, 2, TILES, N])
        best = sbuf("best", [P, 2, TILES])
        top = sbuf("top", [P, TILES])
        gap = sbuf("gap", [P, TILES])
        gates = sbuf("gates", [P, TILES, N])
        acc = sbuf("acc", [P, TILES, D])
        mean = sbuf("mean", [P, TILES])
        inv_root = sbuf("inv_root", [P, TILES])

        def at_least(e, n):
            return not isinstance(e, int) or e >= n

        def load(sp, e, j):
            sp.dma_start(w_up[j][:, :], up_dram[bass.ds(e, 1), :, :].rearrange("o p c -> (o p) c"))\
              .then_inc(up_in[j].handle, 16)
            if at_least(e, BUFS):
                sp.wait_ge(y_ps.handle, y_ps.at((e - BUFS + 1) * BATCH))
            sp.dma_start(w_down[j][:, :], down_dram[bass.ds(e, 1), :, :].rearrange("o p c -> (o p) c"))\
              .then_inc(down_in[j].handle, 16)

        def product(pe, j, c, which, bank, done):
            for b in range(BATCH):
                at = (which * C + c) * P
                last = pe.matmul(core.bank[bank + b], w_up[j][:, at:at + P],
                                 core.xnT[:, b * SEQ:(b + 1) * SEQ], start=True, stop=True)
            last.then_inc(done.handle, 1)

        def freq(pe, e, j, c):
            if at_least(e, 1):
                pe.wait_ge(z_done.handle, z_done.at((e - 1) * C + c + 1))
            product(pe, j, c, 0, 2 + 2 * c, f_ps)

        def mag(pe, e, j, c):
            if at_least(e, 1) or c > 0:
                pe.wait_ge(tanh_done.handle, tanh_done.at(e * C + c))
            product(pe, j, c, 1, 0, m_ps)

        def down(pe, e, j, turn, b):
            pe.wait_ge(down_in[j].handle, down_in[j].at(16 * (turn + 1)))
            pe.wait_ge(h_done.handle, h_done.at((e + 1) * C))
            if at_least(e, 1):
                pe.wait_ge(y_read.handle, y_read.at(e * BATCH + b - 1))
            elif b == 0:
                pe.wait_ge(logits_read.handle, logits_read.at(1))
            for t in range(TPB):
                at = (b * TPB + t) * P
                for c in range(C):
                    last = pe.matmul(core.bank[6 + b][:, t * P:(t + 1) * P], hidden[j][:, c, at:at + P],
                                     w_down[j][:, c * D:(c + 1) * D], start=c == 0, stop=c == C - 1)
            last.then_inc(y_ps.handle, 1)

        def tensor_step(pe, e, j, turn):
            j_next, turn_next = (j + 1) % BUFS, turn + (j + 1) // BUFS
            more = not isinstance(e, int) or e < N - 1
            if more:
                pe.wait_ge(up_in[j_next].handle, up_in[j_next].at(16 * (turn_next + 1)))
                mag(pe, e + 1, j_next, 0)
                for c in range(C):
                    freq(pe, e + 1, j_next, c)
            if at_least(e, 2):
                before = ((j - 2) % BUFS, turn - (1 if j < 2 else 0))
                down(pe, e - 2, *before, 0)
            if more:
                mag(pe, e + 1, j_next, 1)
            if at_least(e, 2):
                down(pe, e - 2, *before, 1)

        def tanh(act, e, j, c):
            act.wait_ge(m_ps.handle, m_ps.at(e * C + c + 1))
            if at_least(e, BUFS):
                act.wait_ge(y_ps.handle, y_ps.at((e - BUFS + 1) * BATCH))
            act.activation(hidden[j][:, c, :].rearrange("p (b s) -> p b s", b=BATCH),
                           core.psum[:, 0:BATCH, :], ACT.Tanh).then_inc(tanh_done.handle, 1)

        def sines(act, e, j):
            for c in range(C):
                act.wait_ge(frac_done.handle, frac_done.at(e * C + c + 1))
                if at_least(e, 1):
                    act.wait_ge(h_done.handle, h_done.at((e - 1) * C + c + 1))
                act.activation(sine[:, c, :], angle[j % 2][:, c, :], ACT.Sin, scale=SIN_SCALE)\
                   .then_inc(sin_done.handle, 1)

        def scalar_step(act, e, j):
            at = angle[j % 2]
            if isinstance(e, int) and e == 1:
                act.wait_ge(exp_in.handle, exp_in.at(1))
                act.activation(gap[:, :], gap[:, :], ACT.Exp).then_inc(exp_out.handle, 1)
            tanh(act, e, j, 0)
            for c in range(C):
                act.wait_ge(bounded.handle, bounded.at(e * C + c + 1))
                act.activation(at[:, c, :], at[:, c, :], ACT.Exp).then_inc(exp_done.handle, 1)
            tanh(act, e, j, 1)
            for c in range(C):
                act.wait_ge(exp_done.handle, exp_done.at(e * C + c + 1))
                act.activation(at[:, c, :], at[:, c, :], ACT.Ln, bias=1.0).then_inc(ln_done.handle, 1)
            if at_least(e, 1):
                sines(act, e - 1, j - 1)

        def f_of(c):
            return core.psum[:, 2 + 2 * c:4 + 2 * c, :]

        def by_batch(at):
            return at.rearrange("p (b s) -> p b s", b=BATCH)

        def bound(dve, e, j):
            for c in range(C):
                dve.wait_ge(f_ps.handle, f_ps.at(e * C + c + 1))
                if at_least(e, 2):
                    dve.wait_ge(sin_done.handle, sin_done.at((e - 2) * C + c + 1))
                dve.tensor_scalar(by_batch(angle[j % 2][:, c, :]), f_of(c), SURE, None, ALU.min)\
                   .then_inc(bounded.handle, 1)

        def softplus(dve, e, j, c):
            at = by_batch(angle[j % 2][:, c, :])
            dve.wait_ge(ln_done.handle, ln_done.at(e * C + c + 1))
            dve.scalar_tensor_tensor(at, f_of(c), 1.0, at, ALU.mult, ALU.max).then_inc(z_done.handle, 1)

        def turns(dve, e, j, c):
            at = angle[j % 2][:, c, :]
            dve.wait_ge(z_done.handle, z_done.at(e * C + c + 1))
            dve.tensor_scalar(at, at, 1.0 / TURN, phase[:, bass.ds(e * C + c, 1)], ALU.mult, ALU.add)\
               .then_inc(u_done.handle, 1)
            dve.wait_ge(u_done.handle, u_done.at(e * C + c + 1))
            if at_least(e, 1):
                dve.wait_ge(frac_done.handle, frac_done.at((e - 1) * C + c + 1))
            dve.tensor_scalar(whole[:, c, :], at, MAGIC, -MAGIC, ALU.add, ALU.add).then_inc(k_done.handle, 1)

        def accumulate(dve, e):
            for b in range(BATCH):
                n = e * BATCH + b + 1
                dve.wait_ge(y_ps.handle, y_ps.at(n))
                if at_least(e, 1):
                    dve.wait_ge(y_read.handle, y_read.at(n - BATCH))
                for t in range(TPB):
                    at = acc[:, b * TPB + t, :]
                    last = dve.scalar_tensor_tensor(at, core.bank[6 + b][:, t * P:(t + 1) * P],
                                                    gates[:, b * TPB + t, bass.ds(e, 1)], at, ALU.mult, ALU.add)
                last.then_inc(y_read.handle, 1)

        def make_gates(dve, link):
            first, second = choice[:, 0], choice[:, 1]
            dve.wait_ge(exp_out.handle, exp_out.at(1))
            link(dve.tensor_scalar(top[:, :], gap[:, :], 1.0, None, ALU.add))
            link(dve.reciprocal(top[:, :], top[:, :]))
            link(dve.tensor_tensor(tmp[:, :, :], second, spread(gap[:, :], 2, N), ALU.mult))
            link(dve.tensor_tensor(tmp[:, :, :], tmp[:, :, :], first, ALU.add))
            link(dve.tensor_tensor(gates[:, :, :], tmp[:, :, :], spread(top[:, :], 2, N), ALU.mult))
            dve.wait_ge(filled.handle, filled.at(1))

        def vector_step(dve, e, j, link):
            for c in range(C):
                softplus(dve, e, j, c)
            turns(dve, e, j, 0)
            if not isinstance(e, int) or e < N - 1:
                bound(dve, e + 1, j + 1)
            turns(dve, e, j, 1)
            if isinstance(e, int) and e == 1:
                make_gates(dve, link)
            if at_least(e, 2):
                accumulate(dve, e - 2)

        def wait_alone(pool, signal, n):
            pool.wait_ge(signal.handle, signal.at(n))
            pool.sem_inc(core.sig("pool_paced").handle, 1)

        def times_sine(pool, e, j):
            for c in range(C):
                wait_alone(pool, sin_done, e * C + c + 1)
                at = hidden[j % BUFS][:, c, :]
                pool.tensor_tensor(at, at, sine[:, c, :], ALU.mult).then_inc(h_done.handle, 1)

        def gpsimd_step(pool, e, j):
            for c in range(C):
                wait_alone(pool, k_done, e * C + c + 1)
                at = angle[j % 2][:, c, :]
                pool.tensor_tensor(at, at, whole[:, c, :], ALU.subtract).then_inc(frac_done.handle, 1)
            if at_least(e, 1):
                times_sine(pool, e - 1, j - 1)

        def every_step(engine, step):
            for j in range(BUFS):
                step(j, j, 0)
            with engine.Fori(1, N // BUFS - 1) as i:
                for j in range(BUFS):
                    step(i * BUFS + j, j, i)
            for j in range(BUFS):
                step(N - BUFS + j, j, N // BUFS - 1)

        with nc.Block() as block:
            @block.sync
            def _(sp):
                for e in range(BUFS):
                    load(sp, e, e)
                with sp.Fori(1, N // BUFS) as i:
                    for j in range(BUFS):
                        sp.wait_ge(m_ps.handle, m_ps.at((i * BUFS + j - BUFS + 1) * C))
                        load(sp, i * BUFS + j, j)

            @block.tensor
            def _(pe):
                norm_tensor(core, pe)
                pe.wait_ge(up_in[0].handle, up_in[0].at(16))
                pe.wait_ge(core.sig("ln_xnT").handle, core.sig("ln_xnT").at(BATCH))
                for c in range(C):
                    freq(pe, 0, 0, c)
                mag(pe, 0, 0, 0)
                pe.wait_ge(w_sem, 16)
                router_tensor(core, pe, w[:, L3F["router"]], N, logits_ps, bank=6)
                mag(pe, 0, 0, 1)
                every_step(pe, lambda e, j, turn: tensor_step(pe, e, j, turn))
                for e in (N - 2, N - 1):
                    for b in range(BATCH):
                        down(pe, e, e % BUFS, e // BUFS, b)

            @block.gpsimd
            def _(pool):
                norm_gpsimd(core, pool)
                pool.memset(acc[:, :, :], 0.0).then_inc(filled.handle, 1)
                every_step(pool, lambda e, j, turn: gpsimd_step(pool, e, j))
                times_sine(pool, N - 1, BUFS - 1)
                pool.wait_ge(mean_sq.handle, mean_sq.at(1))
                pool.tensor_tensor(inv_root[:, :], mean[:, :], core.minus_half[:, 0:1].to_broadcast([P, TILES]),
                                   ALU.pow).then_inc(rstd.handle, 1)

            @block.scalar
            def _(act):
                norm_scalar(core, act)
                every_step(act, lambda e, j, turn: scalar_step(act, e, j))
                sines(act, N - 1, BUFS - 1)

            @block.vector
            def _(dve):
                norm_vector(core, dve)
                link = Chain(dve, chain)
                dve.wait_ge(w_sem, 16)
                link(dve.tensor_scalar(phase[:, :], w[:, L3F["phase"]], 0.1 + TURN / 4, 1.0 / TURN,
                                       ALU.add, ALU.mult))
                bound(dve, 0, 0)
                dve.wait_ge(logits_ps.handle, logits_ps.at(1))
                dve.tensor_tensor(scores[:, :, :], core.bank[6][:, 0:TILES * N].rearrange("p (t e) -> p t e", t=TILES),
                                  spread(w[:, L3F["bias"]], 1, TILES), ALU.add).then_inc(logits_read.handle, 1)
                dve.wait_ge(logits_read.handle, logits_read.at(1))
                first, second = choice[:, 0], choice[:, 1]
                first_of_largest(dve, link, first, scores[:, :, :], core.const["iota"], tmp[:, :, :], top[:, :])
                link(dve.tensor_reduce(best[:, 0, :], scores[:, :, :], AXIS.X, ALU.max))
                link(dve.scalar_tensor_tensor(rest[:, :, :], first, NEG, scores[:, :, :], ALU.mult, ALU.add))
                link(dve.tensor_reduce(best[:, 1, :], rest[:, :, :], AXIS.X, ALU.max))
                first_of_largest(dve, link, second, rest[:, :, :], core.const["iota"], tmp[:, :, :], top[:, :])
                dve.tensor_tensor(gap[:, :], best[:, 1, :], best[:, 0, :], ALU.subtract).then_inc(exp_in.handle, 1)
                every_step(dve, lambda e, j, turn: vector_step(dve, e, j, link))
                accumulate(dve, N - 2)
                accumulate(dve, N - 1)
                dve.wait_ge(y_read.handle, y_read.at(N * BATCH))
                scratch = whole[:, 0, :].rearrange("p (t d) -> p t d", t=TILES)
                link(dve.tensor_tensor(scratch, acc[:, :, :], acc[:, :, :], ALU.mult))
                link(dve.tensor_reduce(mean[:, :], scratch, AXIS.X, ALU.add))
                dve.tensor_scalar(mean[:, :], mean[:, :], 1.0 / D, 1e-6, ALU.mult, ALU.add).then_inc(mean_sq.handle, 1)
                link(dve.tensor_tensor(acc[:, :, :], acc[:, :, :], spread(w[:, L3F["norm"]], 1, TILES), ALU.mult))
                dve.wait_ge(rstd.handle, rstd.at(1))
                link(dve.tensor_tensor(acc[:, :, :], acc[:, :, :], spread(inv_root[:, :], 2, D), ALU.mult))
                link(dve.tensor_tensor(core.x[:, :, :], core.x[:, :, :], acc[:, :, :], ALU.add))
                count[0] = link.count
    norm_close(core)
    for s, total in ((logits_ps, 1), (logits_read, 1), (exp_in, 1), (exp_out, 1),
                     *[(s, 16 * N // BUFS) for s in up_in + down_in],
                     *[(s, N * C) for s in (f_ps, m_ps, bounded, exp_done, ln_done, z_done, u_done, k_done,
                                            frac_done, tanh_done, sin_done, h_done)],
                     (y_ps, N * BATCH), (y_read, N * BATCH), (chain, count[0]), (filled, 1), (mean_sq, 1), (rstd, 1)):
        s.close(total)


def constants_layout():
    at, layout = 0, {}
    for name, width in (("ident", P), ("mask_q", P), ("mask_k", P), ("keep_k", P), ("iota", 16),
                        ("rope_cos", 256), ("rope_sin", 256), ("rope_half_cos", 256), ("rope_half_sin", 256),
                        ("head_mask8", 16), ("row_mask8", 512), ("head_mask64", 8), ("row_mask64", 512),
                        ("head_mask32", 4), ("row_mask32", 128)):
        layout[name] = slice(at, at + width)
        at += width
    return layout, at


def decoder(nc, x_in, consts, packs, streamed, out):
    with ExitStack() as ctx:
        core = Core(nc, ctx)
        layout, n_consts = constants_layout()
        const = core.sbuf("constants", [P, n_consts], F32)
        core.const = {name: const[:, cols] for name, cols in layout.items()}
        core.ident, core.keep_k = core.const["ident"], core.const["keep_k"]
        core.rope_cos, core.rope_sin = core.const["rope_cos"], core.const["rope_sin"]
        core.rope_half_cos, core.rope_half_sin = core.const["rope_half_cos"], core.const["rope_half_sin"]
        core.ident_bf_t = core.sbuf("ident_bf", [P, P], BF16)
        core.mask_q_t = core.sbuf("mask_q_bf", [P, P], BF16)
        core.mask_k_t = core.sbuf("mask_k_bf", [P, P], BF16)
        core.ident_bf, core.mask_q, core.mask_k = core.ident_bf_t[:, :], core.mask_q_t[:, :], core.mask_k_t[:, :]
        loaded = ctx.enter_context(nc.semaphore("inputs_loaded"))
        made = ctx.enter_context(nc.semaphore("constants_made"))
        w, w_sem = {}, {}
        for name, ap in packs.items():
            w[name] = core.sbuf(f"w_{name}", [ap.shape[0], ap.shape[1]], F32)
            w_sem[name] = ctx.enter_context(nc.semaphore(f"loaded_{name}"))

        with nc.Block() as block:
            @block.sync
            def _(sp):
                sp.dma_start(core.x[:, :, :], x_in.rearrange("b (t p) d -> p (b t) d", p=P)).then_inc(loaded, 16)
                sp.dma_start(const[:, :], consts).then_inc(loaded, 16)
                for name, ap in packs.items():
                    sp.dma_start(w[name][:, :], ap).then_inc(w_sem[name], 16)

            @block.gpsimd
            def _(pool):
                pool.memset(core.minus_half[:, :], -0.5).then_inc(made, 1)
                pool.memset(core.ones[:, :], 1.0).then_inc(made, 1)

            @block.vector
            def _(dve):
                dve.wait_ge(loaded, 32)
                dve.tensor_copy(core.ident_bf, core.ident).then_inc(made, 1)
                dve.tensor_copy(core.mask_q, core.const["mask_q"]).then_inc(made, 1)
                dve.tensor_copy(core.mask_k, core.const["mask_k"]).then_inc(made, 1)
                dve.wait_ge(made, 5)

        core.kbd, core.vbd = {}, {}
        for cfg in CROSS:
            core.kbd[cfg.name] = core.sbuf(f"{cfg.name}_kbd", [P, BATCH, cfg.chunks, cfg.heads_per_chunk * KEYS], F32)
            core.vbd[cfg.name] = core.sbuf(f"{cfg.name}_vbd", [P, BATCH, max(cfg.chunks, cfg.prob_chunks), P], F32)
        run_layers(core, w, w_sem, streamed)

        stored = ctx.enter_context(nc.semaphore("output_stored"))
        with nc.Block() as block:
            @block.sync
            def _(sp):
                sp.dma_start(out.rearrange("b (t p) d -> p (b t) d", p=P), core.x[:, :, :]).then_inc(stored, 16)
                sp.wait_ge(stored, 16)
                for name in packs:
                    sp.wait_ge(w_sem[name], 16)


CROSS = [CrossAttention("l0_xattn", 16, 8, True, True), CrossAttention("l1_xattn", 8, 64, False, False),
         CrossAttention("l2_xattn", 4, 32, False, False), CrossAttention("l3_xattn", 16, 8, True, False)]
SELF = [SelfAttention("l0_attn", "silu", True, 1.0, False),
        SelfAttention("l1_attn", "square", True, 1.0 / DH, True),
        SelfAttention("l2_attn", "plain", False, DH ** -0.5, True),
        SelfAttention("l3_attn", "rope", True, DH ** -0.5, False)]


def run_layers(core, w, w_sem, streamed):
    def attend(layer):
        self_attention(core, SELF[layer], w[SELF[layer].name], w_sem[SELF[layer].name])

    def attend_context(layer):
        cross_attention(core, CROSS[layer], w[CROSS[layer].name], w_sem[CROSS[layer].name])

    attend(0)
    prepare_context(core, CROSS, w, w_sem, w["context"], w_sem["context"])
    attend_context(0)
    expert_feed_forward(core, w["l0_ffn"], w_sem["l0_ffn"], w["l0_ffn_b1"], w_sem["l0_ffn_b1"])
    attend(1)
    attend_context(1)
    gated_experts(core, w["l1_ffn"], w_sem["l1_ffn"], streamed["l1_w1"], streamed["l1_w2"])
    attend(2)
    attend_context(2)
    quantised_feed_forward(core, w["l2_ffn"], w_sem["l2_ffn"])
    attend(3)
    attend_context(3)
    tanh_cos_experts(core, w["l3_ffn"], w_sem["l3_ffn"], streamed["l3_up"], streamed["l3_down"])


def shape_constants():
    import numpy as np
    layout, n = constants_layout()
    c = np.zeros((P, n), np.float32)
    i = np.arange(P)
    c[:, layout["ident"]] = np.eye(P)
    c[:, layout["mask_q"]] = np.where(i[None, :] > i[:, None], NEG, 0.0)
    c[:, layout["mask_k"]] = np.where(i[None, :] < i[:, None], NEG, 0.0)
    c[:, layout["keep_k"]] = i[None, :] >= i[:, None]
    c[:, layout["iota"]] = np.arange(16)
    pos = (np.arange(TPB)[None, :, None] * P + i[:, None, None]).astype(np.float32)
    inv_freq = (1.0 / np.float32(10000.0) ** (np.arange(0, DH, 2, dtype=np.float32) / DH)).astype(np.float32)
    freqs = pos * inv_freq
    sign = np.where(np.arange(DH) % 2 == 0, -1.0, 1.0)
    for name, angles in (("rope_half", np.concatenate([freqs, freqs], -1)), ("rope", np.repeat(freqs, 2, -1))):
        for fn, f in (("cos", np.cos(angles)), ("sin", np.sin(angles) * sign)):
            c[:, layout[f"{name}_{fn}"]] = np.repeat(f[:, :, None, :], SLOTS, 2).reshape(P, -1)
    for dh, heads_per_chunk in ((8, 16), (64, 2), (32, 4)):
        c[:, layout[f"head_mask{dh}"]][:, :heads_per_chunk] = (i[:, None] // dh) == np.arange(heads_per_chunk)[None, :]
        n_cols = layout[f"row_mask{dh}"].stop - layout[f"row_mask{dh}"].start
        cols = np.arange(n_cols)
        if dh == 8:
            head_of_col, row_base = (cols % 128) // 8, 4 * (cols // 128)
        elif dh == 64:
            head_of_col, row_base = cols // 64, 4 * (cols // 256)
        else:
            head_of_col, row_base = cols // 32, 0 * cols
        c[:, layout[f"row_mask{dh}"]] = (i[:, None] // KEYS + row_base[None, :]) == head_of_col[None, :]
    return c


def packed(inputs):
    import numpy as np

    def get(name):
        return np.asarray(inputs[name])

    def rows(vector):
        return np.broadcast_to(vector.reshape(1, -1), (P, vector.size))

    def qkv(q, k, v):
        cols = []
        for g in range(HG):
            cols += [q[:, g * GH * DH:(g + 1) * GH * DH], k[:, g * GH * DH:(g + 1) * GH * DH]]
        return cols + [v]

    packs = {}
    scales = np.concatenate([get("L0_attn_q_scale").reshape(HG, GH), get("L0_attn_k_scale").reshape(HG, GH)], 1)
    packs["l0_attn"] = [*qkv(get("L0_attn_Wq").T, get("L0_attn_Wk").T, get("L0_attn_Wv").T), get("L0_attn_Wo").T,
                        rows(scales)]
    packs["l1_attn"] = [*qkv(get("L1_attn_Wq").T, get("L1_attn_Wk").T, get("L1_attn_Wv").T), get("L1_attn_Wo").T,
                        *[rows(a[0]) for a in qkv(get("L1_attn_bq")[None], get("L1_attn_bk")[None],
                                                  get("L1_attn_bv")[None])],
                        rows(np.tile(get("L1_attn_norm_w"), SLOTS))]
    packs["l2_attn"] = [*qkv(get("L2_attn_Wq"), get("L2_attn_Wk"), get("L2_attn_Wv")), get("L2_attn_Wout")]
    packs["l3_attn"] = [*qkv(get("L3_attn_qw"), get("L3_attn_kw"), get("L3_attn_vw")), get("L3_attn_ow")]
    ctx = get("ctx_768")
    by_layer = {"l0_xattn": ("L0_xattn_", False), "l1_xattn": ("L1_xattn_", False), "l2_xattn": ("L2_xattn_", True),
                "l3_xattn": ("L3_xattn_", False)}
    packs["context"] = [*[ctx[b].T for b in range(BATCH)],
                        *[ctx[b].T for b in range(BATCH) for _ in range(P // KEYS)]]
    for cfg in CROSS:
        prefix, turned = by_layer[cfg.name]
        wq, wk, wv, wo = [get(prefix + n).T if turned else get(prefix + n) for n in ("Wq", "Wk", "Wv", "Wo")]
        packs["context"] += [wk, wv]
        packs[cfg.name] = [wq, wo.reshape(cfg.chunks, P, D).transpose(1, 0, 2).reshape(P, -1), rows(get(prefix + "bo"))]
        if cfg.biased:
            packs[cfg.name] += [get(prefix + "bq").reshape(cfg.chunks, P).T, get(prefix + "bk").reshape(cfg.chunks, P).T,
                                rows(get(prefix + "bv"))]

    def chunked(a):
        return a.reshape(-1, P, a.shape[-1]).transpose(1, 0, 2).reshape(P, -1)

    packs["l0_ffn"] = [get("L0_ffn_W_router"), *list(get("L0_ffn_W1")), chunked(get("L0_ffn_Wo")),
                       *[rows(get("L0_ffn_" + n)) for n in ("bo", "ln_gamma", "ln_beta")]]
    packs["l0_ffn_b1"] = [get("L0_ffn_b1")]
    packs["l1_ffn"] = [get("L1_ffn_router_w"), rows(get("L1_ffn_router_b"))]
    packs["l2_ffn"] = [get("L2_ffn_w_gate").T, get("L2_ffn_w_up").T, chunked(get("L2_ffn_w_down").T)]
    packs["l3_ffn"] = [get("L3_ffn_router_w").T, rows(get("L3_ffn_router_bias")),
                       get("L3_ffn_bank_phase").reshape(-1, P).T, rows(get("L3_ffn_norm_w"))]
    return {name: np.ascontiguousarray(np.concatenate(cols, 1)) for name, cols in packs.items()}


def experts(inputs):
    import numpy as np

    def get(name):
        return np.asarray(inputs[name])

    def chunked(a):
        return a.reshape(a.shape[0], -1, P, a.shape[-1]).transpose(0, 2, 1, 3).reshape(a.shape[0], P, -1)

    arrays = {"l1_w1": get("L1_ffn_w1"), "l1_w2": chunked(get("L1_ffn_w2"))}

    arrays["l3_up"] = np.concatenate([get("L3_ffn_bank_freq"), get("L3_ffn_bank_mag")], 2)
    arrays["l3_down"] = chunked(get("L3_ffn_bank_down"))
    return {name: np.ascontiguousarray(a) for name, a in arrays.items()}


def kernel(**inputs):
    import numpy as np
    import concourse.bacc as bacc
    from concourse.bass_utils import run_bass_kernel_spmd

    nc = bacc.Bacc("TRN2", target_bir_lowering=False, num_devices=1)
    arrays = {"x": np.ascontiguousarray(inputs["x"]), "consts": shape_constants(), **packed(inputs)}
    by_expert = experts(inputs)
    arrays.update(by_expert)
    aps = {name: nc.dram_tensor(f"in_{name}", a.shape, mybir.dt.from_np(a.dtype), kind="ExternalInput").ap()
           for name, a in arrays.items()}
    out = nc.dram_tensor("out", (BATCH, SEQ, D), F32, kind="ExternalOutput").ap()
    x, consts = aps.pop("x"), aps.pop("consts")
    streamed = {name: aps.pop(name) for name in by_expert}
    decoder(nc, x, consts, aps, streamed, out)
    result = run_bass_kernel_spmd(nc, [{f"in_{name}": a for name, a in arrays.items()}], core_ids=[0])
    return result.results[0]["out"]
```
